# Optimizing a Trainium2 kernel written in Bass

```python
import numpy as np
import jax
import jax.numpy as jnp

def _softmax(x, axis=-1):
    return jax.nn.softmax(x, axis=axis)

def _gelu(x):
    return jax.nn.gelu(x, approximate=True)

def _silu(x):
    return jax.nn.silu(x)

def _sigmoid(x):
    return jax.nn.sigmoid(x)

def _layernorm(x, axis=-1, eps=1e-05):
    m = jnp.mean(x, axis=axis, keepdims=True)
    v = jnp.var(x, axis=axis, keepdims=True)
    return (x - m) / jnp.sqrt(v + eps)

def _scatter_add(tgt, idx, src, axis=0):
    return tgt.at[idx].add(src)

def _segment_sum(src, seg, n):
    return jax.ops.segment_sum(src, seg, n)
kernel_name = 'mk_adj_ffn_d2_adj_r2_032213'

def setup_inputs(seed: int=0):
    np.random.seed(seed)
    _w = jnp.asarray

    def _rec_inputs():
        import jax
        import jax.numpy as jnp
        _gk = jax.random.key(seed)
        x = -0.0006008 + 1.001 * jax.random.normal(jax.random.fold_in(_gk, 1), (3327, 128), jnp.float32)
        _a = jax.random.bernoulli(jax.random.fold_in(_gk, 2), 0.00120228, (3327, 3327))
        _a = jnp.logical_or(_a, jnp.eye(3327, dtype=bool))
        _af = _a.astype(jnp.float32)
        _af = _af * jax.random.uniform(jax.random.fold_in(_gk, 3), (3327, 3327), jnp.float32, 0.05, 1)
        adj = _af
        return (x, adj)
    x, adj = _rec_inputs()

    def _L0_gnn_setup():
        import jax, jax.numpy as jnp
        import numpy as np
        N = 5000
        NFEAT = 128
        NHID = 128
        key = jax.random.key(seed)
        k1, k2, k3, k4 = jax.random.split(key, 4)
        x = jax.random.normal(k1, (N, NFEAT), dtype=jnp.float32)
        adj = jax.random.uniform(k2, (N, N), dtype=jnp.float32)
        stdv = 1.0 / np.sqrt(NHID)
        weight = jax.random.uniform(k3, (2 * NFEAT, NHID), dtype=jnp.float32, minval=-stdv, maxval=stdv)
        bias = jax.random.uniform(k4, (NHID,), dtype=jnp.float32, minval=-stdv, maxval=stdv)
        return {'x': x, 'adj': adj, 'weight': weight, 'bias': bias}
    _L0_gnn_all = _L0_gnn_setup()
    _L0_gnn_in = {k: v for k, v in _L0_gnn_all.items() if k in ('weight', 'bias')}
    del _L0_gnn_all

    def _L0_ffn_setup():
        import jax, jax.numpy as jnp
        import numpy as np
        B, S, H, NH, NE = (4, 512, 128, 4, 4)
        D = H // NH
        EPS = 1e-08

        def layernorm(x, g, b):
            m = jnp.mean(x, axis=-1, keepdims=True)
            v = jnp.mean((x - m) ** 2, axis=-1, keepdims=True)
            return (x - m) / jnp.sqrt(v + EPS) * g + b
        key = jax.random.key(seed)
        ks = jax.random.split(key, 18)
        sc = 0.05
        return {'x': jax.random.normal(ks[0], (B, S, H), jnp.float32), 'hl_w': jax.random.normal(ks[1], (NH, D, H), jnp.float32) * sc, 'hl_b': jax.random.normal(ks[2], (NH, D), jnp.float32) * sc, 'wq': jax.random.normal(ks[3], (NH, NE, D, D), jnp.float32) * sc, 'wk': jax.random.normal(ks[4], (NH, D, D), jnp.float32) * sc, 'wv': jax.random.normal(ks[5], (NH, D, D), jnp.float32) * sc, 'gate_w': jax.random.normal(ks[6], (NH, NE, NE * D), jnp.float32) * sc, 'gate_b': jax.random.normal(ks[7], (NH, NE), jnp.float32) * sc, 'ln_g': jnp.ones((D,), jnp.float32), 'ln_b': jnp.zeros((D,), jnp.float32), 'fc1_w': jax.random.normal(ks[8], (D, D), jnp.float32) * sc, 'fc1_b': jax.random.normal(ks[9], (D,), jnp.float32) * sc, 'fc2_w': jax.random.normal(ks[10], (D, D), jnp.float32) * sc, 'fc2_b': jax.random.normal(ks[11], (D,), jnp.float32) * sc, 'fnorm_g': jnp.ones((D,), jnp.float32), 'fnorm_b': jnp.zeros((D,), jnp.float32), 'fgate_w': jax.random.normal(ks[12], (NH, H), jnp.float32) * sc}
    _L0_ffn_all = _L0_ffn_setup()
    _L0_ffn_in = {k: v for k, v in _L0_ffn_all.items() if k in ('hl_w', 'hl_b', 'wq', 'wk', 'wv', 'gate_w', 'gate_b', 'ln_g', 'ln_b', 'fc1_w', 'fc1_b', 'fc2_w', 'fc2_b', 'fnorm_g', 'fnorm_b', 'fgate_w')}
    del _L0_ffn_all

    def _L1_gnn_setup():
        import jax, jax.numpy as jnp
        import numpy as np
        N = 10000
        D = 128
        F = 128
        K = F // 8
        key = jax.random.key(seed)
        k1, k2, k3, k4, k5 = jax.random.split(key, 5)
        h = jax.random.normal(k1, (N, D), dtype=jnp.float32)
        adj = jax.random.uniform(k2, (N, N), dtype=jnp.float32)
        W1 = jax.random.normal(k3, (D, K), dtype=jnp.float32) * 0.05
        W2 = jax.random.normal(k4, (K, D, F), dtype=jnp.float32) * 0.05
        b = jax.random.normal(k5, (K, F), dtype=jnp.float32) * 0.05
        return {'h': h, 'adj': adj, 'W1': W1, 'W2': W2, 'b': b}
    _L1_gnn_all = _L1_gnn_setup()
    _L1_gnn_in = {k: v for k, v in _L1_gnn_all.items() if k in ('W1', 'W2', 'b')}
    del _L1_gnn_all

    def _L1_ffn_setup():
        import jax, jax.numpy as jnp
        import numpy as np
        B, K, D = (256, 16, 128)
        E = 32
        H = int(D * 0.25)
        key = jax.random.key(seed)
        ks = jax.random.split(key, 7)
        d_rs = D ** (-0.5)
        h_rs = H ** (-0.5)
        x = jax.random.normal(ks[0], (B, K, D), dtype=jnp.float32)
        router_w = jax.random.uniform(ks[1], (E, D), jnp.float32, -d_rs, d_rs)
        router_b = jax.random.uniform(ks[2], (E,), jnp.float32, -d_rs, d_rs)
        W1 = jax.random.uniform(ks[3], (E, D, H), jnp.float32, -h_rs, h_rs)
        b1 = jax.random.uniform(ks[4], (E, H), jnp.float32, -h_rs, h_rs)
        W2 = jax.random.uniform(ks[5], (E, H, D), jnp.float32, -d_rs, d_rs)
        b2 = jax.random.uniform(ks[6], (E, D), jnp.float32, -d_rs, d_rs)
        return {'x': x, 'router_w': router_w, 'router_b': router_b, 'W1': W1, 'b1': b1, 'W2': W2, 'b2': b2}
    _L1_ffn_all = _L1_ffn_setup()
    _L1_ffn_in = {k: v for k, v in _L1_ffn_all.items() if k in ('router_w', 'router_b', 'W1', 'b1', 'W2', 'b2')}
    del _L1_ffn_all
    return {'x': x, 'adj': adj, 'L0_gnn_weight': _L0_gnn_in['weight'], 'L0_gnn_bias': _L0_gnn_in['bias'], 'L0_ffn_hl_w': _L0_ffn_in['hl_w'], 'L0_ffn_hl_b': _L0_ffn_in['hl_b'], 'L0_ffn_wq': _L0_ffn_in['wq'], 'L0_ffn_wk': _L0_ffn_in['wk'], 'L0_ffn_wv': _L0_ffn_in['wv'], 'L0_ffn_gate_w': _L0_ffn_in['gate_w'], 'L0_ffn_gate_b': _L0_ffn_in['gate_b'], 'L0_ffn_ln_g': _L0_ffn_in['ln_g'], 'L0_ffn_ln_b': _L0_ffn_in['ln_b'], 'L0_ffn_fc1_w': _L0_ffn_in['fc1_w'], 'L0_ffn_fc1_b': _L0_ffn_in['fc1_b'], 'L0_ffn_fc2_w': _L0_ffn_in['fc2_w'], 'L0_ffn_fc2_b': _L0_ffn_in['fc2_b'], 'L0_ffn_fnorm_g': _L0_ffn_in['fnorm_g'], 'L0_ffn_fnorm_b': _L0_ffn_in['fnorm_b'], 'L0_ffn_fgate_w': _L0_ffn_in['fgate_w'], 'L1_gnn_W1': _L1_gnn_in['W1'], 'L1_gnn_W2': _L1_gnn_in['W2'], 'L1_gnn_b': _L1_gnn_in['b'], 'L1_ffn_router_w': _L1_ffn_in['router_w'], 'L1_ffn_router_b': _L1_ffn_in['router_b'], 'L1_ffn_W1': _L1_ffn_in['W1'], 'L1_ffn_b1': _L1_ffn_in['b1'], 'L1_ffn_W2': _L1_ffn_in['W2'], 'L1_ffn_b2': _L1_ffn_in['b2']}

def reference(x, adj, L0_gnn_weight, L0_gnn_bias, L0_ffn_hl_w, L0_ffn_hl_b, L0_ffn_wq, L0_ffn_wk, L0_ffn_wv, L0_ffn_gate_w, L0_ffn_gate_b, L0_ffn_ln_g, L0_ffn_ln_b, L0_ffn_fc1_w, L0_ffn_fc1_b, L0_ffn_fc2_w, L0_ffn_fc2_b, L0_ffn_fnorm_g, L0_ffn_fnorm_b, L0_ffn_fgate_w, L1_gnn_W1, L1_gnn_W2, L1_gnn_b, L1_ffn_router_w, L1_ffn_router_b, L1_ffn_W1, L1_ffn_b1, L1_ffn_W2, L1_ffn_b2):
    import jax
    import jax.numpy as jnp

    def _L0_gnn_ref(x, adj, weight, bias):
        import jax, jax.numpy as jnp
        import numpy as np
        N = 5000
        NFEAT = 128
        NHID = 128
        support = adj @ x
        support = jnp.concatenate([x, support], axis=1)
        out = support @ weight + bias
        return jax.nn.relu(out)

    def _L0_ffn_ref(x, hl_w, hl_b, wq, wk, wv, gate_w, gate_b, ln_g, ln_b, fc1_w, fc1_b, fc2_w, fc2_b, fnorm_g, fnorm_b, fgate_w):
        import jax, jax.numpy as jnp
        import numpy as np
        B, S, H, NH, NE = (4, 512, 128, 4, 4)
        D = H // NH
        EPS = 1e-08

        def layernorm(x, g, b):
            m = jnp.mean(x, axis=-1, keepdims=True)
            v = jnp.mean((x - m) ** 2, axis=-1, keepdims=True)
            return (x - m) / jnp.sqrt(v + EPS) * g + b
        b, s, h = x.shape
        nh, d, _ = wk.shape
        ne = wq.shape[1]
        sx = jnp.einsum('bsh,ndh->bnsd', x, hl_w) + hl_b[None, :, None, :]
        pad = sx == 0
        q = jnp.einsum('bnsd,neod->bneso', sx, wq)
        k = jnp.einsum('bnsd,nod->bnso', sx, wk)
        v = jnp.einsum('bnsd,nod->bnso', sx, wv)
        causal = jnp.where(jnp.tril(jnp.ones((s, s), bool)), 0.0, -jnp.inf).astype(x.dtype)
        scores = jnp.einsum('bnesd,bntd->bnest', q, k) * d ** 0.5 + causal
        att = jax.nn.softmax(scores, axis=-1)
        qkv = jnp.einsum('bnest,bntd->bnesd', att, v)
        qkv = jnp.where(pad[:, :, None], 0.0, qkv)
        out = jnp.transpose(qkv, (0, 1, 3, 2, 4)).reshape(b, nh, s, ne * d)
        gs = jax.nn.softmax(jnp.einsum('bnsf,nef->bnse', out, gate_w) + gate_b[None, :, None, :], axis=-1)
        mixed = jnp.einsum('bnsed,bnse->bnsd', out.reshape(b, nh, s, ne, d), gs)
        resid = sx[jnp.arange(nh), jnp.arange(nh)]
        hn = layernorm(mixed + resid, ln_g, ln_b)
        f_n = jnp.transpose(hn, (0, 2, 1, 3)).reshape(b, s, h)
        fx = f_n.reshape(b, s, nh, d)
        pm = fx == 0
        hx = jnp.where(pm, 0.0, fx @ fc1_w.T + fc1_b)
        hx = jax.nn.relu(hx)
        hx = jnp.where(pm, 0.0, hx @ fc2_w.T + fc2_b)
        hx = layernorm(hx + fx, fnorm_g, fnorm_b)
        fout = hx.reshape(b, s, h)
        fg = jax.nn.softmax(fout @ fgate_w.T, axis=-1)
        return (fout.reshape(b, s, nh, d) * fg[..., None]).reshape(b, s, h)

    def _L1_gnn_ref(h, adj, W1, W2, b):
        import jax, jax.numpy as jnp
        import numpy as np
        N = 10000
        D = 128
        F = 128
        K = F // 8
        node = h @ W1
        hw = jnp.einsum('nc,kcf->nkf', h, W2)
        x = jnp.einsum('nk,nkf->nf', node, hw)
        x = adj @ x
        x = x + node @ b
        return jax.nn.relu(x)

    def _L1_ffn_ref(x, router_w, router_b, W1, b1, W2, b2):
        import jax, jax.numpy as jnp
        import numpy as np
        B, K, D = (256, 16, 128)
        E = 32
        H = int(D * 0.25)
        xf = x.reshape(-1, D)
        logits = xf @ router_w.T + router_b
        idx = jnp.argmax(logits, axis=-1)
        w1t = jnp.take(W1, idx, axis=0)
        h = jnp.einsum('nd,ndh->nh', xf, w1t) + jnp.take(b1, idx, axis=0)
        h = jax.nn.relu(h)
        w2t = jnp.take(W2, idx, axis=0)
        out = jnp.einsum('nh,nhd->nd', h, w2t) + jnp.take(b2, idx, axis=0)
        out = jax.nn.relu(out)
        return out.reshape(x.shape)
    x = x + _L0_gnn_ref(_layernorm(x, axis=-1), adj, L0_gnn_weight, L0_gnn_bias)
    x = x + _L0_ffn_ref(_layernorm(x, axis=-1)[None], L0_ffn_hl_w, L0_ffn_hl_b, L0_ffn_wq, L0_ffn_wk, L0_ffn_wv, L0_ffn_gate_w, L0_ffn_gate_b, L0_ffn_ln_g, L0_ffn_ln_b, L0_ffn_fc1_w, L0_ffn_fc1_b, L0_ffn_fc2_w, L0_ffn_fc2_b, L0_ffn_fnorm_g, L0_ffn_fnorm_b, L0_ffn_fgate_w)[0]
    x = x + _L1_gnn_ref(_layernorm(x, axis=-1), adj, L1_gnn_W1, L1_gnn_W2, L1_gnn_b)
    x = x + _L1_ffn_ref(_layernorm(x, axis=-1)[None], L1_ffn_router_w, L1_ffn_router_b, L1_ffn_W1, L1_ffn_b1, L1_ffn_W2, L1_ffn_b2)[0]
    return x

_drawn_inputs = setup_inputs


def setup_inputs(seed=0):
    import zlib

    import numpy as np

    out = dict(_drawn_inputs(seed))
    spreads = {'L0_ffn_ln_g': (1.0, 0.2),
     'L0_ffn_ln_b': (0.0, 0.1),
     'L0_ffn_fnorm_g': (1.0, 0.2),
     'L0_ffn_fnorm_b': (0.0, 0.285)}
    factors = {'L0_ffn_wq': 4.146,
     'L0_ffn_wk': 4.139,
     'L0_ffn_wv': 3.125,
     'L0_ffn_gate_w': 8.0,
     'L0_ffn_gate_b': 8.0,
     'L0_ffn_fc1_w': 3.182,
     'L0_ffn_fc1_b': 8.0,
     'L0_ffn_fc2_w': 2.815,
     'L0_ffn_fc2_b': 3.189,
     'L1_ffn_b1': 7.912,
     'L1_ffn_b2': 3.228}
    for name, (base, spread) in spreads.items():
        noise = np.random.default_rng([zlib.crc32(name.encode()), seed]).standard_normal(out[name].shape)
        drawn = base * np.exp(spread * noise) if base else spread * noise
        out[name] = jnp.asarray(drawn.astype(out[name].dtype))
    for name, factor in factors.items():
        out[name] = (out[name] * factor).astype(out[name].dtype)
    return out
```

```python
from contextlib import ExitStack

import concourse.bass as bass
from concourse import mybir

ALU = mybir.AluOpType
ACT = mybir.ActivationFunctionType
X = mybir.AxisListType.X
F32 = mybir.dt.float32
F32R = mybir.dt.float32r
BF16 = mybir.dt.bfloat16
U32 = mybir.dt.uint32

P = 128
N = 3327
NT = -(-N // P)
NP = NT * P
D = 128
QT = 4
BLK = QT * P
NB = NT // QT
LT = NT - NB * QT
NH, NE, HD = 4, 4, 32
NODE_K = 16
ME, MH = 32, 32
EC = ME * MH // P
PIECES = ((0, 7), (7, 13), (13, 20), (20, 26))
SCORE_SCALE = float(HD) ** 0.5
MASKED = -1e30
LN_EPS, HEAD_LN_EPS = 1e-5, 1e-8

PACK_GNN0 = (
    ("ident", P, P), ("w_self", P, D), ("w_near", P, D), ("bias", 1, D), ("ones_row", 1, P),
    ("ones_rows", P, 1), ("hl_wT", P, D), ("hl_b", P, 1), ("wk", P, NH * P), ("wv", P, D),
)
PACK_ATT = (
    ("ident", P, P), ("mask_rows", P, P), ("mask_cols", P, P), ("sel", 32, 16), ("ones32", P, 32),
    ("wq", P, NH * NE * P), ("first_rows", P, NE),
)
PACK_POST = (
    ("ident", P, P), ("ones_row", 1, P), ("rep", P, NH * P), ("gate_w", P, NH * NE * NE),
    ("gate_b", P, NH * NE), ("ln_g", P, HD), ("ln_b", P, HD), ("fnorm_g", P, HD), ("fnorm_b", P, HD),
    ("fc1", P, D), ("fc2", P, D), ("fc1_b", 1, D), ("fc2_b", 1, D), ("fgateT", P, NH),
    ("node_w", P, NODE_K), ("node_b", NODE_K, D), ("node_w2", P, NODE_K * D),
)
PACK_MOE = (
    ("ident", P, P), ("ones_row", 1, P), ("routerT", P, ME), ("router_b", 1, ME), ("iota", P, ME),
    ("w1", P, ME * MH), ("b1", P, EC), ("w2", P, EC * D), ("b2", ME, D), ("rep", ME, ME * MH),
)


def pack_width(pack):
    return sum(cols for _, _, cols in pack)


def pack_views(tile, pack):
    views, at = {}, 0
    for name, rows, cols in pack:
        views[name] = tile[0:rows, at:at + cols]
        at += cols
    return views


def wait(eng, sem, value):
    if not isinstance(value, int) or value > 0:
        eng.wait_ge(sem, value)


class Links:

    def __init__(self, eng, sem, start=0, spare=None):
        self.eng, self.sem, self.start, self.n, self.spare = eng, sem, start, 0, spare

    def __call__(self, ins, apart=False):
        self.n += 1
        ins.then_inc(self.sem, 1)
        self.eng.wait_ge(self.sem, self.start + self.n)
        if apart:
            self.apart()

    def apart(self):
        self.eng.memset(self.spare, 0.0)


def layernorm_head(dve, link, src, cen, sq, stat, width, eps, std_asked):
    shape = list(src.shape)
    s0, s1 = stat
    link(dve.tensor_reduce(s0, src, X, ALU.add))
    link(dve.scalar_tensor_tensor(cen, s0.unsqueeze(len(shape) - 1).to_broadcast(shape), -1.0 / width, src, ALU.mult, ALU.add))
    link(dve.tensor_tensor(sq, cen, cen, ALU.mult))
    link(dve.tensor_reduce(s1, sq, X, ALU.add))
    dve.tensor_scalar(s1, s1, 1.0 / width, eps, ALU.mult, ALU.add).then_inc(std_asked, 1)


def layernorm_tail(dve, link, cen, stat, shape):
    s0, s1 = stat
    link(dve.reciprocal(s1, s0))
    return s1.unsqueeze(len(shape) - 1).to_broadcast(shape)


def gnn0_program(nc, x_in, adj_main, adj_last, pack_in, xres, xn, sxT, kst, vals):
    with ExitStack() as ctx:
        sb = lambda name, shape, dt=F32: ctx.enter_context(nc.sbuf_tensor(f"g_{name}", shape, dt))
        ps = lambda name: ctx.enter_context(nc.psum_tensor(f"gp_{name}", [P, 512], F32))
        sem = lambda name: ctx.enter_context(nc.semaphore(f"g_{name}"))
        wp = sb("wp", [P, pack_width(PACK_GNN0)])
        w = pack_views(wp, PACK_GNN0)
        adj = sb("adj", [P, NT, BLK])
        FIRST = ((0, 7), (7, 13), (13, 20), (20, 26))
        cen, sq = sb("cen", [P, 7, D]), sb("sq", [P, 7, D])
        st, spare = sb("st", [P, 2, 7]), sb("spare", [1, 1])
        near, xnT, hT, sxb = sb("near", [P, BLK]), sb("xnT", [P, BLK]), sb("hT", [P, BLK]), sb("sxb", [P, BLK])
        xnb, h = sb("xnb", [P, QT, D]), sb("h", [P, QT, D])
        ps_near, ps_turn, ps_h, ps_v = ps("near"), ps("turn"), ps("h"), ps("v")
        ps_k = [ps(f"k{n}") for n in range(NH)]
        x_landed, pack_landed = sem("x_landed"), sem("pack_landed")
        adj_landed = [sem(f"adj_landed{i}") for i in range(len(PIECES))]
        (adj_used, links, var_ready, std_ready, xn_ready, xn_staged, near_copied, xn_turned, xnT_copied, h_ready,
         x_updated, row_ready, row_turned, hT_ready, sx_summed, sx_ready, k_summed, k_high_ready, k_ready,
         v_summed, v_ready) = (sem(x) for x in (
            "adj_used", "links", "var_ready", "std_ready", "xn_ready", "xn_staged", "near_copied", "xn_turned",
            "xnT_copied", "h_ready", "x_updated", "row_ready", "row_turned", "hT_ready", "sx_summed", "sx_ready",
            "k_summed", "k_high_ready", "k_ready", "v_summed", "v_ready"))
        LINKS = 5
        STARTS = 5 * len(FIRST)
        block = ctx.enter_context(nc.Block())

        def for_blocks(eng, body):
            body(0, QT)
            with eng.Fori(1, NB) as b:
                body(b, QT)
            body(NB, LT)

        @block.sync
        def _(sp):
            sp.dma_start(xres[:], x_in.rearrange("(t p) d -> p t d", p=P)).then_inc(x_landed, 16)
            sp.dma_start(wp[:], pack_in).then_inc(pack_landed, 16)

            def load(b, width, src):
                for i, (k0, k1) in enumerate(PIECES):
                    wait(sp, adj_used, len(PIECES) * (b - 1) + i + 1)
                    sp.dma_start(adj[:, k0:k1, 0:width], src[:, k0:k1, :]).then_inc(adj_landed[i], 16)

            load(0, BLK, adj_main[0])
            with sp.Fori(1, NB) as b:
                load(b, BLK, adj_main[bass.ds(b, 1)].rearrange("o p k m -> (o p) k m"))
            load(NB, LT * P, adj_last)

        @block.vector
        def _(dve):
            link = Links(dve, links)
            dve.wait_ge(x_landed, 16)
            for g, (t0, t1) in enumerate(FIRST):
                n = t1 - t0
                stat = (st[:, 0, 0:n], st[:, 1, 0:n])
                layernorm_head(dve, link, xres[:, t0:t1, :], cen[:, 0:n, :], sq[:, 0:n, :], stat, D, LN_EPS, var_ready)
                dve.wait_ge(std_ready, g + 1)
                rstd = layernorm_tail(dve, link, cen[:], stat, [P, n, D])
                dve.tensor_tensor(xn[:, t0:t1, :], cen[:, 0:n, :], rstd, ALU.mult).then_inc(xn_ready, 1)
                dve.wait_ge(xn_ready, g + 1)

            def body(b, nt):
                link = Links(dve, links, STARTS + b * LINKS)
                xb = xres[:, bass.ds(b * QT, nt), :]
                width = nt * P
                dve.wait_ge(h_ready, b + 1)
                dve.scalar_tensor_tensor(xb, ps_h[:, 0:width].rearrange("p (t d) -> p t d", d=D), 0.0, xb,
                                         ALU.max, ALU.add).then_inc(x_updated, 1)
                dve.wait_ge(x_updated, b + 1)
                dve.memset(spare[:], 0.0)
                stat = (st[:, 0, 0:nt], st[:, 1, 0:nt])
                layernorm_head(dve, link, xb, cen[:, 0:nt, :], sq[:, 0:nt, :], stat, D, LN_EPS, var_ready)
                dve.wait_ge(std_ready, len(FIRST) + b + 1)
                rstd = layernorm_tail(dve, link, cen[:], stat, [P, nt, D])
                dve.tensor_tensor(h[:, 0:nt, :], cen[:, 0:nt, :], rstd, ALU.mult).then_inc(row_ready, 1)
                for n in range(NH):
                    dve.wait_ge(k_high_ready, NH * b + n + 1)
                    low = kst[64:96, n, bass.ds(b * BLK, width)]
                    dve.tensor_tensor(low, ps_k[n][64:96, 0:width], low.bitcast(F32), ALU.subtract).then_inc(k_ready, 1)
                assert link.n == LINKS, link.n

            for_blocks(dve, body)

        @block.scalar
        def _(act):
            for g, (t0, t1) in enumerate(FIRST):
                act.wait_ge(var_ready, g + 1)
                act.activation(st[:, 0, 0:t1 - t0], st[:, 1, 0:t1 - t0], ACT.Sqrt).then_inc(std_ready, 1)

            def sums(b, nt):
                width = nt * P
                act.wait_ge(adj_used, len(PIECES) * (b + 1))
                wait(act, h_ready, b)
                act.copy(near[:, 0:width], ps_near[:, 0:width]).then_inc(near_copied, 1)
                act.wait_ge(xn_turned, b + 1)
                act.copy(xnT[:, 0:width], ps_v[:, 0:width]).then_inc(xnT_copied, 1)

            def keys(b, nt):
                width = nt * P
                act.wait_ge(var_ready, len(FIRST) + b + 1)
                act.activation(st[:, 0, 0:nt], st[:, 1, 0:nt], ACT.Sqrt).then_inc(std_ready, 1)
                act.wait_ge(row_turned, b + 1)
                act.copy(hT[:, 0:width], ps_turn[:, 0:width]).then_inc(hT_ready, 1)
                act.wait_ge(sx_summed, b + 1)
                act.activation(sxb[:, 0:width], ps_h[:, 0:width], ACT.Identity, bias=w["hl_b"]).then_inc(sx_ready, 1)
                act.wait_ge(sx_ready, 2 * b + 1)
                act.copy(sxT[:, bass.ds(b * BLK, width)], sxb[:, 0:width]).then_inc(sx_ready, 1)
                for n in range(NH):
                    act.wait_ge(k_summed, NH * b + n + 1)
                    act.activation(kst[:, n, bass.ds(b * BLK, width)], ps_k[n][:, 0:width], ACT.Identity,
                                   bias=w["ones_rows"]).then_inc(k_high_ready, 1)
                act.wait_ge(v_summed, b + 1)
                act.copy(vals[:, bass.ds(b * QT, nt), :], ps_v[:, 0:width].rearrange("p (t d) -> p t d", d=D))\
                    .then_inc(v_ready, 1)

            sums(0, QT)
            with act.Fori(1, NB) as b:
                keys(b - 1, QT)
                sums(b, QT)
            keys(NB - 1, QT)
            sums(NB, LT)
            keys(NB, LT)

        @block.gpsimd
        def _(pool):
            def stage(b, nt):
                pool.wait_ge(xn_ready, len(FIRST))
                wait(pool, xn_turned, b)
                pool.tensor_copy(xnb[:, 0:nt, :], xn[:, bass.ds(b * QT, nt), :]).then_inc(xn_staged, 1)

            for_blocks(pool, stage)

        @block.tensor
        def _(pe):
            pe.wait_ge(pack_landed, 16)

            def piece(b, nt, i):
                k0, k1 = PIECES[i]
                pe.wait_ge(adj_landed[i], 16 * (b + 1))
                pe.wait_ge(xn_ready, i + 1)
                if i == 0:
                    wait(pe, near_copied, b)
                for k in range(k0, k1):
                    last = pe.matmul(ps_near[:, 0:nt * P], xn[:, k, :], adj[:, k, 0:nt * P],
                                     start=(k == 0), stop=(k == NT - 1))
                last.then_inc(adj_used, 1)

            def turn_xn(b, nt):
                pe.wait_ge(xn_staged, b + 1)
                wait(pe, v_ready, b)
                for j in range(nt):
                    last = pe.matmul(ps_v[:, j * P:(j + 1) * P], xnb[:, j, :], w["ident"], start=True, stop=True)
                last.then_inc(xn_turned, 1)

            def layer(b, nt):
                pe.wait_ge(near_copied, b + 1)
                pe.wait_ge(xnT_copied, b + 1)
                wait(pe, sx_ready, 2 * b)
                for j in range(nt):
                    cols = slice(j * P, (j + 1) * P)
                    pe.matmul(ps_h[:, cols], xnT[:, cols], w["w_self"], start=True, stop=False)
                    pe.matmul(ps_h[:, cols], near[:, cols], w["w_near"], start=False, stop=False)
                    last = pe.matmul(ps_h[:, cols], w["ones_row"], w["bias"], start=False, stop=True)
                last.then_inc(h_ready, 1)

            def turn_row(b, nt):
                pe.wait_ge(row_ready, b + 1)
                for j in range(nt):
                    last = pe.matmul(ps_turn[:, j * P:(j + 1) * P], h[:, j, :], w["ident"], start=True, stop=True)
                last.then_inc(row_turned, 1)

            def project(b, nt):
                pe.wait_ge(hT_ready, b + 1)
                pe.wait_ge(x_updated, b + 1)
                pe.matmul(ps_h[:, 0:nt * P], w["hl_wT"], hT[:, 0:nt * P], start=True, stop=True).then_inc(sx_summed, 1)

            def keys(b, nt):
                pe.wait_ge(sx_ready, 2 * b + 1)
                wait(pe, k_ready, NH * b)
                for n in range(NH):
                    pe.matmul(ps_k[n][:, 0:nt * P], w["wk"][:, n * P:(n + 1) * P], sxb[:, 0:nt * P],
                              start=True, stop=True).then_inc(k_summed, 1)
                for j in range(nt):
                    cols = slice(j * P, (j + 1) * P)
                    last = pe.matmul(ps_v[:, cols], sxb[:, cols], w["wv"], start=True, stop=True)
                last.then_inc(v_summed, 1)

            def sums_beside(b, nt, b0, nt0):
                piece(b, nt, 0)
                turn_row(b0, nt0)
                piece(b, nt, 1)
                project(b0, nt0)
                piece(b, nt, 2)
                keys(b0, nt0)
                piece(b, nt, 3)
                turn_xn(b, nt)
                layer(b, nt)

            for i in range(len(PIECES)):
                piece(0, QT, i)
            turn_xn(0, QT)
            layer(0, QT)
            with pe.Fori(1, NB) as b:
                sums_beside(b, QT, b - 1, QT)
            sums_beside(NB, LT, NB - 1, QT)
            turn_row(NB, LT)
            project(NB, LT)
            keys(NB, LT)


def attention_program(nc, pack_in, sxT, kst, vals, rsum, o_scratch):
    with ExitStack() as ctx:
        sb = lambda name, shape, dt=F32: ctx.enter_context(nc.sbuf_tensor(f"a_{name}", shape, dt))
        sem = lambda name: ctx.enter_context(nc.semaphore(f"a_{name}"))
        wp = sb("wp", [P, pack_width(PACK_ATT)])
        w = pack_views(wp, PACK_ATT)
        ident16, mask_rows, mask_cols = (sb(n, [P, P], BF16) for n in ("ident16", "mask_rows16", "mask_cols16"))
        kstat, vstat = sb("kstat", [P, BLK], F32R), sb("vstat", [P, QT, HD])
        qst = [sb(f"qst{i}", [P, NE, BLK], F32R) for i in range(2)]
        probs = [sb(f"probs{i}", [P, NE, BLK]) for i in range(QT)]
        m, m_chunk, m2 = sb("m", [P, 16]), sb("m_chunk", [P, 16]), sb("m2", [P, 16, 2])
        spare, zeros = sb("spare", [1, 1]), sb("zeros", [P, 32])
        o_tile, l_tile = [sb(f"o_tile{i}", [P, BLK]) for i in range(2)], sb("l_tile", [P, BLK])

        ps_slot = [ctx.enter_context(nc.psum_tensor(f"ap_slot{i}", [P, 512], F32)) for i in range(2)]
        ps_score = [ctx.enter_context(nc.psum_tensor(f"ap_score{i}", [P, 2, 512], F32)) for i in range(2)]
        ps_o = ctx.enter_context(nc.psum_tensor("ap_o", [P, 512], F32))
        ps_l = ctx.enter_context(nc.psum_tensor("ap_l", [P, 512], F32))

        pack_landed, masks_ready, m_cleared = sem("pack_landed"), sem("masks_ready"), sem("m_cleared")
        slot_ready, slot_free, q_high_ready, chunk_merged, max_half, max_split = (
            sem(x) for x in ("slot_ready", "slot_free", "q_high_ready", "chunk_merged", "max_half", "max_split"))
        keys_staged, vals_staged, scores_ready, probs_ready, o_summed, pair_added, l_summed = (
            sem(x) for x in ("keys_staged", "vals_staged", "scores_ready", "probs_ready", "o_summed",
                             "pair_added", "l_summed"))
        probs_cleared = sem("probs_cleared")
        o_copied, l_copied, o_stored = sem("o_copied"), sem("l_copied"), [sem(f"o_stored{i}") for i in range(2)]
        block = ctx.enter_context(nc.Block())

        def keys_before(b, nt, n):
            return 8 * b * (b + 1) + n * (QT * b + nt)

        def chunks_before(b, n):
            return 2 * b * (b + 1) + n * (b + 1)

        def pairs_before(b, nt, n):
            return 4 * b * (b + 1) + n * (2 * b + nt // 2)

        def first_slot(b):
            if first(b):
                return Slot(NE + QT * NE + 1, 1)
            last = (QT - LT) * NE * (NB + 1) if isinstance(b, int) and b == NB else 0
            return Slot(20 + 32 * b * b + 72 * b - last, 0)

        class Slot:

            def __init__(self, at, odd):
                self.at, self.odd = at, odd

            def take(self):
                at, odd = self.at, self.odd
                self.at, self.odd = at + 1, 1 - odd
                return at, ps_slot[odd]

            def jump(self, at):
                self.at = at

        def first(b):
            return isinstance(b, int) and b == 0

        def following(b, nt, next_nt, n):
            if n + 1 < NH:
                return b, nt, n + 1
            return (b + 1, next_nt, 0) if next_nt else None

        def preceding(b, nt, n):
            if n > 0:
                return b, nt, n - 1
            return None if first(b) else (b - 1, QT, NH - 1)

        def buffer(i, tiles):
            return probs[i + QT - tiles]

        def for_blocks(eng, body):
            body(0, QT, QT)
            with eng.Fori(1, NB - 1) as b:
                body(b, QT, QT)
            body(NB - 1, QT, LT)
            body(NB, LT, 0)

        @block.sync
        def _(sp):
            sp.dma_start(wp[:], pack_in).then_inc(pack_landed, 16)

            def body(b, nt, next_nt):
                for n in range(NH):
                    sp.wait_ge(o_copied, NH * b + n + 1)
                    sp.dma_start(o_scratch[bass.ds(b, 1), :, n, 0:nt * P].rearrange("o p s -> (o p) s"),
                                 o_tile[n % 2][:, 0:nt * P]).then_inc(o_stored[n % 2], 16)

            for_blocks(sp, body)
            for stored in o_stored:
                sp.wait_ge(stored, 16 * (NH // 2) * (NB + 1))

        @block.gpsimd
        def _(pool):
            def chunk(b, n, keys, pairs, tiles, diagonal, width):
                for i in range(1, tiles, 2):
                    pool.wait_ge(probs_ready, 2 * (keys + i) + 2)
                    pool.wait_ge(o_summed, keys + i)
                    cols = slice(i * P if diagonal else 0, width)
                    even, odd = buffer(i - 1, tiles)[:, :, cols], buffer(i, tiles)[:, :, cols]
                    pool.tensor_tensor(even, even, odd, ALU.add).then_inc(pair_added, 1)

            def body(b, nt, next_nt):
                for n in range(NH):
                    keys, pairs = keys_before(b, nt, n), pairs_before(b, nt, n)
                    chunk(b, n, keys, pairs, nt, True, nt * P)
                    if not first(b):
                        with pool.Fori(0, b) as c:
                            chunk(b, n, keys + nt + QT * c, pairs + nt // 2 + 2 * c, QT, False, nt * P)

            for_blocks(pool, body)

        @block.scalar
        def _(act):
            def stage_keys(n, first_tile, tiles, keys):
                wait(act, scores_ready, 2 * keys)
                act.copy(kstat[:, 0:tiles * P], kst[:, n, bass.ds(first_tile * P, tiles * P)]).then_inc(keys_staged, 1)

            def stage_values(n, first_tile, tiles, keys):
                wait(act, o_summed, keys)
                act.copy(vstat[:, 0:tiles, :], vals[:, bass.ds(first_tile, tiles), n * HD:(n + 1) * HD])\
                    .then_inc(vals_staged, 1)

            def queries(nt, slot, n):
                for e in range(NE):
                    s, to = slot.take()
                    act.wait_ge(slot_ready, s + 1)
                    act.activation(qst[n % 2][:, e, 0:nt * P], to[:, 0:nt * P], ACT.Copy, scale=SCORE_SCALE)\
                        .then_inc(q_high_ready, 1)

            def copy_sums(unit):
                b, nt, n = unit
                act.wait_ge(l_summed, pairs_before(b, nt, n + 1))
                act.copy(l_tile[:, 0:nt * P], ps_l[:, 0:nt * P]).then_inc(l_copied, 1)

            def chunk(n, first_tile, tiles, keys, pairs, diagonal, width, before):
                for i in range(tiles):
                    wait(act, l_summed, pairs - 1 if i + QT - tiles < 2 else pairs)
                    for p in range(2):
                        act.wait_ge(scores_ready, 2 * (keys + i) + p + 1)
                        cols = slice(i * P if diagonal else 0, width)
                        act.activation(buffer(i, tiles)[:, 2 * p:2 * p + 2, cols], ps_score[p][:, :, cols], ACT.Exp)\
                            .then_inc(probs_ready, 1)
                    if i == 0:
                        stage_values(n, first_tile, tiles, keys)
                    if i == 1 and before:
                        copy_sums(before)

            def body(b, nt, next_nt):
                slot = first_slot(b)
                width = nt * P
                for n in range(NH):
                    keys, pairs = keys_before(b, nt, n), pairs_before(b, nt, n)
                    ahead, before = following(b, nt, next_nt, n), preceding(b, nt, n)
                    if ahead:
                        queries(ahead[1], slot, ahead[2])
                    if ahead:
                        slot.jump(slot.at + NE * ahead[1] * (ahead[0] + 1))
                        slot.take()
                    if before:
                        slot.take()
                    chunk(n, b * QT, nt, keys, pairs, True, width, before)
                    if not first(b):
                        with act.Fori(0, b) as c:
                            at = keys + nt + QT * c
                            stage_keys(n, c * QT, QT, at)
                            chunk(n, c * QT, QT, at, pairs + nt // 2 + 2 * c, False, width, None)
                    if ahead:
                        stage_keys(ahead[2], ahead[0] * QT, ahead[1], keys_before(b, nt, n + 1))
                    act.wait_ge(o_summed, keys_before(b, nt, n + 1))
                    wait(act, o_stored[n % 2], 16 * (NH // 2 * b + n // 2))
                    act.copy(o_tile[n % 2][:, 0:width], ps_o[:, 0:width]).then_inc(o_copied, 1)

            act.wait_ge(pack_landed, 16)
            queries(QT, Slot(0, 0), 0)
            stage_keys(0, 0, QT, 0)
            for_blocks(act, body)
            copy_sums((NB, LT, NH - 1))

        @block.vector
        def _(dve):
            dve.memset(m[:], 0.0).then_inc(m_cleared, 1)
            dve.memset(zeros[:], 0.0).then_inc(masks_ready, 1)
            dve.memset(m_chunk[:], 0.0).then_inc(chunk_merged, 1)
            dve.wait_ge(m_cleared, 1)
            dve.wait_ge(pack_landed, 16)
            for to, src in ((ident16, "ident"), (mask_rows, "mask_rows"), (mask_cols, "mask_cols")):
                dve.tensor_copy(to[:], w[src]).then_inc(masks_ready, 1)

            def queries(unit, slot):
                b, nt, n = unit
                for e in range(NE):
                    s, at = slot.take()
                    dve.wait_ge(q_high_ready, NE * (NH * b + n) + e + 1)
                    low = qst[n % 2][96:128, e, 0:nt * P]
                    dve.scalar_tensor_tensor(low, at[96:128, 0:nt * P], SCORE_SCALE, low.bitcast(F32),
                                             ALU.mult, ALU.subtract).then_inc(slot_free, 1)

            def maxima(nt, slot, to, widths):
                for j in range(nt):
                    for e in range(NE):
                        s, at = slot.take()
                        dve.wait_ge(slot_ready, s + 1)
                        dve.tensor_reduce(to[:, e * QT + j:e * QT + j + 1], at[:, 0:widths[j]], X, ALU.max)\
                            .then_inc(slot_free, 1)

            def diagonal_maxima(unit, slot):
                b, nt, n = unit
                wait(dve, max_split, NH * b + n)
                maxima(nt, slot, m, [(j + 1) * P for j in range(nt)])

            def chunk_maxima(unit, slot, c):
                b, nt, n = unit
                dve.wait_ge(chunk_merged, 2 * b * (b - 1) + n * b + 1 + c)
                maxima(nt, slot, m_chunk, [BLK] * nt)
                dve.wait_ge(slot_free, slot.at)
                dve.tensor_tensor(m[:], m[:], m_chunk[:], ALU.max).then_inc(chunk_merged, 1)

            def shift(unit, slot):
                b, nt, n = unit
                dve.wait_ge(slot_free, slot.at)
                wait(dve, chunk_merged, 2 * b * (b - 1) + (n + 1) * b + 1)
                dve.tensor_scalar(m2[:, :, 0].bitcast(F32R), m[:], -1.0, None, ALU.mult).then_inc(max_half, 1)
                dve.wait_ge(max_half, NH * b + n + 1)
                dve.scalar_tensor_tensor(m2[:, :, 1], m[:], -1.0, m2[:, :, 0], ALU.mult, ALU.subtract)\
                    .then_inc(max_split, 1)
                s, at = slot.take()
                dve.wait_ge(slot_ready, s + 1)
                shape = [32, NE, nt, P]
                rows = qst[n % 2][0:32, :, 0:nt * P].rearrange("r e (j s) -> r e j s", s=P)
                mine = w["sel"].rearrange("r (e j) -> r e j", j=QT)[:, :, 0:nt].unsqueeze(3).to_broadcast(shape)
                dve.tensor_tensor(rows, at[0:32, 0:P].unsqueeze(1).unsqueeze(1).to_broadcast(shape), mine,
                                  ALU.mult).then_inc(slot_free, 1)

            def invert_sums(unit, slot):
                b, nt, n = unit
                s, at = slot.take()
                dve.wait_ge(slot_ready, s + 1)
                if not isinstance(b, int):
                    dve.memset(spare[:], 0.0)
                dve.reciprocal(rsum[:, bass.ds(b * QT, nt), n * NE:(n + 1) * NE],
                               at[:, 0:nt * NE].rearrange("p (t e) -> p t e", e=NE)).then_inc(slot_free, 1)

            def clear(b, nt, n):
                wait(dve, l_summed, pairs_before(b, nt, n))
                dve.memset(buffer(2, QT)[:, :, 0:2 * P], 0.0).then_inc(probs_cleared, 1)

            def body(b, nt, next_nt):
                slot = first_slot(b)
                for n in range(NH):
                    ahead, before = following(b, nt, next_nt, n), preceding(b, nt, n)
                    if ahead:
                        queries(ahead, slot)
                        diagonal_maxima(ahead, slot)
                        if ahead[2] == 0:
                            chunk_maxima(ahead, slot, 0)
                    if nt == QT:
                        clear(b, nt, n)
                    if before:
                        invert_sums(before, slot)
                    if ahead and not first(b):
                        start = slot.at
                        with dve.Fori(0, b) as c:
                            slot.jump(start + NE * ahead[1] * c)
                            at_chunk = c if ahead[2] else c + 1
                            chunk_maxima(ahead, slot, at_chunk)
                        slot.jump(start + NE * ahead[1] * b)
                    if ahead:
                        shift(ahead, slot)
                return slot

            slot = Slot(0, 0)
            queries((0, QT, 0), slot)
            diagonal_maxima((0, QT, 0), slot)
            shift((0, QT, 0), slot)
            ends = []
            for_blocks(dve, lambda *block: ends.append(body(*block)))
            invert_sums((NB, LT, NH - 1), ends[-1])

        @block.tensor
        def _(pe):
            pe.wait_ge(pack_landed, 16)
            pe.wait_ge(masks_ready, 4)

            def queries(unit, slot):
                b, nt, n = unit
                for e in range(NE):
                    s, to = slot.take()
                    wait(pe, slot_free, s - 1)
                    at = (n * NE + e) * P
                    pe.matmul(to[:, 0:nt * P], w["wq"][:, at:at + P], sxT[:, bass.ds(b * BLK, nt * P)],
                              start=True, stop=True).then_inc(slot_ready, 1)
                return slot.at

            def for_max(unit, slot, j, e, c):
                b, nt, n = unit
                s, to = slot.take()
                wait(pe, slot_free, s - 1)
                diagonal = c is None
                width = (j + 1) * P if diagonal else BLK
                last = pe.matmul(to[:, 0:width], qst[n % 2][:, e, j * P:(j + 1) * P],
                                 kst[:, n, bass.ds((b if diagonal else c) * BLK, width)], start=True, stop=True)
                if diagonal:
                    last = pe.matmul(to[:, width - P:width], ident16[:], mask_rows[:], start=False, stop=True,
                                     skip_group_check=True)
                last.then_inc(slot_ready, 1)

            def scores(n, keys, i, p, cols, diagonal):
                wait(pe, probs_ready, 2 * (keys + i - 1) + p + 1)
                for e in range(2):
                    last = pe.matmul(ps_score[p][:, e, cols], kstat[:, i * P:(i + 1) * P],
                                     qst[n % 2][:, 2 * p + e, cols], start=True, stop=True)
                    if diagonal:
                        last = pe.matmul(ps_score[p][:, e, cols.start:cols.start + P], ident16[:], mask_cols[:],
                                         start=False, stop=True, skip_group_check=True)
                last.then_inc(scores_ready, 1)

            def outputs(keys, i, tiles, cols, start):
                pe.wait_ge(probs_ready, 2 * (keys + i) + 2)
                for e in range(NE):
                    last = pe.matmul(ps_o[e * HD:(e + 1) * HD, cols], vstat[:, i, :], buffer(i, tiles)[:, e, cols],
                                     start=start, stop=True, skip_group_check=True)
                last.then_inc(o_summed, 1)

            def sums(pairs, held, width, start):
                pe.wait_ge(pair_added, pairs + 1)
                for e in range(NE):
                    last = pe.matmul(ps_l[e * HD:(e + 1) * HD, 0:width], w["ones32"], held[:, e, 0:width],
                                     start=start, stop=True, skip_group_check=True)
                last.then_inc(l_summed, 1)

            def turn_sums(unit, slot):
                b, nt, n = unit
                s, to = slot.take()
                wait(pe, slot_free, s - 1)
                pe.wait_ge(l_copied, NH * b + n + 1)
                for j in range(nt):
                    last = pe.matmul(to[:, j * NE:(j + 1) * NE], l_tile[:, j * P:(j + 1) * P], w["first_rows"],
                                     start=True, stop=True)
                last.then_inc(slot_ready, 1)

            def chunk(unit, slot, ahead, maxima, queries_at, before, keys, pairs, chunk_at, tiles, diagonal):
                b, nt, n = unit
                width = nt * P
                cols = [slice(i * P if diagonal else 0, width) for i in range(tiles)]
                per = -(-len(maxima) // tiles)
                pe.wait_ge(keys_staged, chunk_at + 1)
                for i in range(tiles):
                    beside = maxima[i * per:(i + 1) * per]
                    half = (len(beside) + 3) // 4
                    scores(n, keys, i, 0, cols[i], diagonal)
                    if i == 0 and beside and queries_at is not None:
                        pe.wait_ge(slot_free, queries_at)
                    for at in beside[0:half]:
                        for_max(ahead, slot, *at)
                    scores(n, keys, i, 1, cols[i], diagonal)
                    for at in beside[half:2 * half]:
                        for_max(ahead, slot, *at)
                    if i == (1 if tiles == QT else 0) and (before or not diagonal):
                        cleared = before or (unit if nt == QT else None)
                        if cleared and cleared[1] == QT:
                            pe.wait_ge(probs_cleared, NH * cleared[0] + cleared[2] + 1)
                        sums(pairs - 1, probs[2], before[1] * P if before else width, False)
                    if i == 0:
                        pe.wait_ge(vals_staged, chunk_at + 1)
                        if diagonal:
                            wait(pe, o_copied, NH * b + n)
                    else:
                        outputs(keys, i - 1, tiles, cols[i - 1], diagonal and i == 1)
                    for at in beside[2 * half:]:
                        for_max(ahead, slot, *at)
                outputs(keys, tiles - 1, tiles, cols[tiles - 1], diagonal and tiles == 1)
                if diagonal and before:
                    turn_sums(before, slot)
                if tiles == QT:
                    sums(pairs, probs[0], width, diagonal)
                else:
                    for e in range(NE):
                        pe.matmul(ps_l[e * HD:(e + 1) * HD, 0:width], zeros[:], w["wq"][:, 0:width],
                                  start=True, stop=True, skip_group_check=True)

            def turn_max(unit, slot):
                b, nt, n = unit
                s, to = slot.take()
                pe.wait_ge(max_split, NH * b + n + 1)
                wait(pe, slot_free, s - 1)
                pe.matmul(to[0:32, 0:P], m2[:].rearrange("p g h -> p (g h)"), w["ident"], start=True, stop=True)\
                    .then_inc(slot_ready, 1)

            def body(b, nt, next_nt):
                slot = first_slot(b)
                for n in range(NH):
                    unit = (b, nt, n)
                    keys, pairs, chunks = keys_before(b, nt, n), pairs_before(b, nt, n), chunks_before(b, n)
                    ahead, before = following(b, nt, next_nt, n), preceding(b, nt, n)
                    pe.wait_ge(slot_free, slot.at)
                    each, diagonal, queries_at = [], [], None
                    if ahead:
                        queries_at = queries(ahead, slot)
                        each = [(j, e) for j in range(ahead[1]) for e in range(NE)]
                        diagonal = [(j, e, None) for j, e in each]
                        if ahead[2] == 0:
                            diagonal += [(j, e, b) for j, e in each]
                    chunk(unit, slot, ahead, diagonal, queries_at, before, keys, pairs, chunks, nt, True)
                    if not first(b):
                        start = slot.at
                        with pe.Fori(0, b) as c:
                            slot.jump(start + len(each) * c)
                            chunk(unit, slot, ahead, [(j, e, c) for j, e in each], None, None,
                                  keys + nt + QT * c, pairs + nt // 2 + 2 * c, chunks + 1 + c, QT, False)
                        slot.jump(start + len(each) * b)
                    if ahead:
                        turn_max(ahead, slot)
                return slot

            slot, unit = Slot(0, 0), (0, QT, 0)
            pe.wait_ge(slot_free, queries(unit, slot))
            for j in range(QT):
                for e in range(NE):
                    for_max(unit, slot, j, e, None)
            turn_max(unit, slot)
            ends = []
            for_blocks(pe, lambda *block: ends.append(body(*block)))
            last = (NB, LT, NH - 1)
            sums(pairs_before(NB, LT, NH) - 1, probs[2], LT * P, False)
            turn_sums(last, ends[-1])


def post_program(nc, pack_in, o_scratch, xres, sxT, rsum, z, nb):
    with ExitStack() as ctx:
        sb = lambda name, shape, dt=F32: ctx.enter_context(nc.sbuf_tensor(f"p_{name}", shape, dt))
        ps = lambda name: ctx.enter_context(nc.psum_tensor(f"pp_{name}", [P, 512], F32))
        sem = lambda name: ctx.enter_context(nc.semaphore(f"p_{name}"))
        wp = sb("wp", [P, pack_width(PACK_POST)])
        w = pack_views(wp, PACK_POST)
        o_in, onT = sb("o_in", [P, NH, BLK]), sb("onT", [P, NH, BLK])
        sxb, turnT, hT, nodeT = sb("sxb", [P, BLK]), sb("turnT", [P, BLK]), sb("hT", [P, BLK]), sb("nodeT", [NODE_K, BLK])
        h, cen, sq, nz = (sb(n, [P, QT, D]) for n in ("h", "cen", "sq", "nz"))
        st = sb("st", [P, 2, QT * NH])
        gate_terms = sb("gate_terms", [P, QT * NH, NE, NE])
        gate, gtop, gsum = sb("gate", [P, QT * NH, NE]), sb("gtop", [P, QT * NH]), sb("gsum", [P, QT * NH])
        prod, zprod = sb("prod", [P, QT, 512]), [sb(f"zprod{i}", [P, NODE_K * D]) for i in range(2)]
        node, spare = sb("node", [P, QT, NODE_K]), sb("spare", [1, 1])
        bank, ps_turn, ps_out, ps_z = [ps(f"bank{i}") for i in range(4)], ps("turn"), ps("out"), [ps(f"z{i}") for i in range(2)]

        pack_landed, links, z_links = sem("pack_landed"), sem("links"), sem("z_links")
        (o_landed, sx_staged, sx_spread, masked, gates_ready, outs_ready, sx_turned, exp_asked, exp_ready,
         var_ready, std_ready, row_ready, turned, turn_copied, fc_ready, fgate_ready, node_ready, nodeT_ready,
         node_copied, nb_ready, nb_copied, z_ready, z_scaled, z_summed) = (sem(x) for x in (
            "o_landed", "sx_staged", "sx_spread", "masked", "gates_ready", "outs_ready", "sx_turned", "exp_asked",
            "exp_ready", "var_ready", "std_ready", "row_ready", "turned", "turn_copied", "fc_ready", "fgate_ready",
            "node_ready", "nodeT_ready", "node_copied", "nb_ready", "nb_copied", "z_ready", "z_scaled", "z_summed"))
        block = ctx.enter_context(nc.Block())

        LINKS = 40

        def row_view(tile, nt):
            return tile[:, 0:nt * P].rearrange("p (t d) -> p t d", d=D)

        def heads_view(tile, nt):
            return tile[:, 0:nt, :].rearrange("p t (n d) -> p (t n) d", d=HD)

        def for_blocks(eng, body):
            body(0, QT, None)
            body(1, QT, 0)
            with eng.Fori(2, NB) as b:
                body(b, QT, b - 1)
            body(NB, LT, NB - 1)

        @block.sync
        def _(sp):
            sp.dma_start(wp[:], pack_in).then_inc(pack_landed, 16)

            def body(b, nt, b0):
                wait(sp, masked, NH * b)
                sp.dma_start(o_in[:, :, 0:nt * P], o_scratch[bass.ds(b, 1), :, :, 0:nt * P].rearrange("o p n s -> (o p) n s"))\
                    .then_inc(o_landed, 16)

            for_blocks(sp, body)

        @block.gpsimd
        def _(pool):
            def sum_z(b, nt):
                for j in range(nt):
                    link = Links(pool, z_links, 3 * (QT * b + j))
                    terms = zprod[j % 2]
                    pool.wait_ge(z_scaled, 4 * (QT * b + j) + 4)
                    width = NODE_K * D // 2
                    while width > D:
                        link(pool.tensor_tensor(terms[:, 0:width], terms[:, 0:width], terms[:, width:2 * width], ALU.add))
                        width //= 2
                    pool.tensor_tensor(z[:, bass.ds(b * QT + j, 1), :].rearrange("p o f -> p (o f)"),
                                       terms[:, 0:D], terms[:, D:2 * D], ALU.add).then_inc(z_summed, 1)

            with pool.Fori(0, NB) as b:
                sum_z(b, QT)
            sum_z(NB, LT)

        @block.scalar
        def _(act):
            def scale_z(b, first, last):
                for s in range(first, last):
                    j, q = s // 4, s % 4
                    act.wait_ge(z_ready, 16 * b + s + 1)
                    if q == 0:
                        wait(act, z_summed, QT * b + j - 1)
                    for i in range(4):
                        k = 4 * q + i
                        last_one = act.activation(zprod[j % 2][:, k * D:(k + 1) * D], ps_z[q % 2][:, i * D:(i + 1) * D],
                                                  ACT.Identity, scale=node[:, j, k:k + 1])
                    last_one.then_inc(z_scaled, 1)

            def root(b, i, count):
                act.wait_ge(var_ready, 3 * b + i)
                act.activation(st[:, 0, 0:count], st[:, 1, 0:count], ACT.Sqrt).then_inc(std_ready, 1)

            def turn(b, nt, i, to):
                act.wait_ge(turned, 4 * b + i)
                act.copy(to[:, 0:nt * P], ps_turn[:, 0:nt * P]).then_inc(turn_copied, 1)

            def exponent(b, i, count):
                act.wait_ge(exp_asked, 2 * b + i)
                g = gate[:, 0:count, :]
                act.activation(g, g, ACT.Exp).then_inc(exp_ready, 1)

            def body(b, nt, b0):
                width = nt * P
                beside = (lambda first, last: scale_z(b0, first, last)) if b0 is not None else (lambda *_: None)
                wait(act, sx_turned, b)
                act.copy(sxb[:, 0:width], sxT[:, bass.ds(b * BLK, width)]).then_inc(sx_staged, 1)
                beside(0, 3)
                exponent(b, 1, nt * NH)
                beside(3, 7)
                root(b, 1, nt * NH)
                turn(b, nt, 1, turnT)
                beside(7, 9)
                turn(b, nt, 2, turnT)
                beside(9, 12)
                root(b, 2, nt * NH)
                turn(b, nt, 3, turnT)
                beside(12, 13)
                exponent(b, 2, nt)
                beside(13, 16)
                root(b, 3, nt)
                turn(b, nt, 4, hT)
                act.wait_ge(node_ready, b + 1)
                act.copy(nodeT[:, 0:width], ps_out[0:NODE_K, 0:width]).then_inc(nodeT_ready, 1)
                act.wait_ge(nb_ready, b + 1)
                act.copy(nb[:, bass.ds(b * QT, nt), :], row_view(ps_out, nt)).then_inc(nb_copied, 1)

            act.wait_ge(pack_landed, 16)
            for_blocks(act, body)
            act.wait_ge(node_copied, NB + 1)
            scale_z(NB, 0, 4 * LT)

        @block.vector
        def _(dve):
            dve.wait_ge(pack_landed, 16)

            def softmax(b, i, link, count, read):
                shape = [P, count, NE]
                g, top, total = gate[:, 0:count, :], gtop[:, 0:count], gsum[:, 0:count]
                link(read(g))
                link(dve.tensor_reduce(top, g, X, ALU.max))
                dve.tensor_tensor(g, g, top.unsqueeze(2).to_broadcast(shape), ALU.subtract).then_inc(exp_asked, 1)
                dve.wait_ge(exp_ready, 2 * b + i)
                link(dve.tensor_reduce(total, g, X, ALU.add))
                link(dve.reciprocal(total, total))
                link(dve.tensor_tensor(g, g, total.unsqueeze(2).to_broadcast(shape), ALU.mult))

            def layernorm(b, i, link, src, to, shape, eps, affine=None):
                count, width = shape[1], shape[2]
                view = (lambda t: t[:, 0:shape[1], :]) if width == D else (lambda t: heads_view(t, shape[1] // NH))
                stat = (st[:, 0, 0:count], st[:, 1, 0:count])
                link.apart()
                layernorm_head(dve, link, src, view(cen), view(sq), stat, width, eps, var_ready)
                dve.wait_ge(std_ready, 3 * b + i)
                rstd = layernorm_tail(dve, link, view(cen), stat, shape)
                last = dve.tensor_tensor(to, view(cen), rstd, ALU.mult)
                if affine:
                    link(last)
                    link(dve.tensor_tensor(to, to, w[affine[0]].unsqueeze(1).to_broadcast(shape), ALU.mult))
                    last = dve.tensor_tensor(to, to, w[affine[1]].unsqueeze(1).to_broadcast(shape), ALU.add)
                return last

            def body(b, nt, b0):
                width, groups = nt * P, nt * NH
                link = Links(dve, links, b * LINKS, spare[:])
                xb = xres[:, bass.ds(b * QT, nt), :]
                dve.wait_ge(o_landed, 16 * (b + 1))
                for n in range(NH):
                    dve.wait_ge(sx_spread, NH * b + n + 1)
                    dve.scalar_tensor_tensor(onT[:, n, 0:width], bank[n][:, 0:width], 0.0, o_in[:, n, 0:width],
                                             ALU.not_equal, ALU.mult).then_inc(masked, 1)

                rs = rsum[:, bass.ds(b * QT, nt), :].rearrange("p t (n e) -> p (t n) e", e=NE)
                terms = gate_terms[:, 0:groups, :, :]
                dve.wait_ge(gates_ready, b + 1)
                link(dve.tensor_tensor(terms, ps_out[:, 0:groups * NE * NE].rearrange("p (g o e) -> p g o e", o=NE, e=NE),
                                       rs.unsqueeze(2).to_broadcast([P, groups, NE, NE]), ALU.mult), apart=True)
                link(dve.tensor_reduce(gate[:, 0:groups, :], terms, X, ALU.add))
                gb = w["gate_b"].rearrange("p (n e) -> p n e", e=NE).unsqueeze(1).to_broadcast([P, nt, NH, NE])
                with_heads = lambda g: g.rearrange("p (t n) e -> p t n e", n=NH)
                softmax(b, 1, link, groups, lambda g: dve.tensor_tensor(with_heads(g), with_heads(g), gb, ALU.add))
                link(dve.tensor_tensor(gate[:, 0:groups, :], gate[:, 0:groups, :], rs, ALU.mult))
                dve.wait_ge(outs_ready, b + 1)
                for j in range(nt):
                    shape = [P, NH * NE, HD]
                    gs = gate[:, j * NH:(j + 1) * NH, :].rearrange("p n e -> p (n e)").unsqueeze(2).to_broadcast(shape)
                    last = dve.tensor_tensor(prod[:, j, :].rearrange("p (g d) -> p g d", d=HD),
                                             bank[j][:].rearrange("p (g d) -> p g d", d=HD), gs, ALU.mult)
                link(last)
                hv = heads_view(h, nt)
                link(dve.tensor_reduce(hv, prod[:, 0:nt, :].rearrange("p t (n e d) -> p (t n) d e", e=NE, d=HD), X, ALU.add))
                dve.wait_ge(sx_turned, b + 1)
                link(dve.tensor_tensor(h[:, 0:nt, :], row_view(ps_turn, nt), h[:, 0:nt, :], ALU.add))
                layernorm(b, 1, link, hv, hv, [P, groups, HD], HEAD_LN_EPS, ("ln_g", "ln_b")).then_inc(row_ready, 1)
                dve.wait_ge(row_ready, 4 * b + 1)
                link(dve.tensor_single_scalar(nz[:, 0:nt, :], h[:, 0:nt, :], 0.0, ALU.not_equal))
                dve.wait_ge(fc_ready, 2 * b + 1)
                dve.scalar_tensor_tensor(sq[:, 0:nt, :], row_view(ps_out, nt), 0.0, nz[:, 0:nt, :], ALU.max, ALU.mult)\
                    .then_inc(row_ready, 1)
                dve.wait_ge(fc_ready, 2 * b + 2)
                link(dve.tensor_tensor(nz[:, 0:nt, :], row_view(ps_out, nt), nz[:, 0:nt, :], ALU.mult))
                link(dve.tensor_tensor(h[:, 0:nt, :], h[:, 0:nt, :], nz[:, 0:nt, :], ALU.add))
                layernorm(b, 2, link, hv, hv, [P, groups, HD], HEAD_LN_EPS, ("fnorm_g", "fnorm_b")).then_inc(row_ready, 1)
                dve.wait_ge(fgate_ready, b + 1)
                softmax(b, 2, link, nt, lambda g: dve.tensor_copy(
                    g, ps_out[:, 0:groups].rearrange("p (t n) -> p t n", n=NH)))
                fg = gate[:, 0:nt, :].rearrange("p t n -> p (t n)").unsqueeze(2).to_broadcast([P, groups, HD])
                link(dve.tensor_tensor(heads_view(cen, nt), hv, fg, ALU.mult))
                link(dve.tensor_tensor(xb, xb, cen[:, 0:nt, :], ALU.add))
                layernorm(b, 3, link, xb, h[:, 0:nt, :], [P, nt, D], LN_EPS).then_inc(row_ready, 1)
                dve.wait_ge(node_ready, b + 1)
                dve.tensor_copy(node[:, 0:nt, :], ps_turn[:, 0:nt * NODE_K].rearrange("p (t k) -> p t k", k=NODE_K))\
                    .then_inc(node_copied, 1)
                assert link.n == LINKS, link.n

            for_blocks(dve, body)

        @block.tensor
        def _(pe):
            pe.wait_ge(pack_landed, 16)

            def turn(b, nt, i, src):
                pe.wait_ge(row_ready, 4 * b + i)
                for j in range(nt):
                    last = pe.matmul(ps_turn[:, j * P:(j + 1) * P], src[:, j, :], w["ident"], start=True, stop=True)
                last.then_inc(turned, 1)

            def z_products(b, first, last):
                for s in range(first, last):
                    j, q = s // 4, s % 4
                    wait(pe, z_scaled, 16 * b + s - 1)
                    pe.matmul(ps_z[q % 2][:], hT[:, j * P:(j + 1) * P], w["node_w2"][:, q * 512:(q + 1) * 512],
                              start=True, stop=True).then_inc(z_ready, 1)

            def body(b, nt, b0):
                width = nt * P
                cols = [slice(j * P, (j + 1) * P) for j in range(nt)]
                beside = (lambda first, last: z_products(b0, first, last)) if b0 is not None else (lambda *_: None)
                pe.wait_ge(sx_staged, b + 1)
                for n in range(NH):
                    pe.matmul(bank[n][:, 0:width], w["rep"][:, n * P:(n + 1) * P], sxb[:, 0:width],
                              start=True, stop=True).then_inc(sx_spread, 1)
                wait(pe, node_copied, b)
                for j in range(nt):
                    last = pe.matmul(ps_turn[:, cols[j]], sxb[:, cols[j]], w["ident"], start=True, stop=True)
                last.then_inc(sx_turned, 1)
                beside(0, 3)
                pe.wait_ge(masked, NH * (b + 1))
                wait(pe, nb_copied, b)
                for j in range(nt):
                    for n in range(NH):
                        at = (j * NH + n) * NE * NE
                        last = pe.matmul(ps_out[:, at:at + NE * NE], onT[:, n, cols[j]],
                                         w["gate_w"][:, n * NE * NE:(n + 1) * NE * NE], start=True, stop=True)
                last.then_inc(gates_ready, 1)
                for j in range(nt):
                    for n in range(NH):
                        last = pe.matmul(bank[j][:, n * P:(n + 1) * P], onT[:, n, cols[j]], w["ident"], start=True, stop=True)
                last.then_inc(outs_ready, 1)
                beside(3, 7)
                for layer, src in enumerate((h, sq)):
                    turn(b, nt, 1 + layer, src)
                    beside(*((7, 8), (9, 10))[layer])
                    pe.wait_ge(turn_copied, 4 * b + 1 + layer)
                    for j in range(nt):
                        pe.matmul(ps_out[:, cols[j]], turnT[:, cols[j]], w[f"fc{layer + 1}"], start=True, stop=False)
                        last = pe.matmul(ps_out[:, cols[j]], w["ones_row"], w[f"fc{layer + 1}_b"], start=False, stop=True)
                    last.then_inc(fc_ready, 1)
                    beside(*((8, 9), (10, 12))[layer])
                turn(b, nt, 3, h)
                beside(12, 13)
                pe.wait_ge(turn_copied, 4 * b + 3)
                for j in range(nt):
                    last = pe.matmul(ps_out[:, j * NH:(j + 1) * NH], turnT[:, cols[j]], w["fgateT"], start=True, stop=True)
                last.then_inc(fgate_ready, 1)
                beside(13, 16)
                turn(b, nt, 4, h)
                pe.wait_ge(turn_copied, 4 * b + 4)
                pe.matmul(ps_out[0:NODE_K, 0:width], w["node_w"], hT[:, 0:width], start=True, stop=True)
                for j in range(nt):
                    last = pe.matmul(ps_turn[:, j * NODE_K:(j + 1) * NODE_K], hT[:, cols[j]], w["node_w"],
                                     start=True, stop=True)
                last.then_inc(node_ready, 1)
                pe.wait_ge(nodeT_ready, b + 1)
                for j in range(nt):
                    last = pe.matmul(ps_out[:, cols[j]], nodeT[:, cols[j]], w["node_b"], start=True, stop=True)
                last.then_inc(nb_ready, 1)

            for_blocks(pe, body)
            z_products(NB, 0, 4 * LT)


def moe_program(nc, adj_main, adj_last, pack_in, out, xres, z, nb):
    with ExitStack() as ctx:
        sb = lambda name, shape, dt=F32: ctx.enter_context(nc.sbuf_tensor(name, shape, dt))
        ps = lambda name: ctx.enter_context(nc.psum_tensor(name, [P, 512], F32))
        sem = lambda name: ctx.enter_context(nc.semaphore(name))
        wp = sb("m_wp", [P, pack_width(PACK_MOE)])
        w = pack_views(wp, PACK_MOE)
        adj = sb("m_adj", [P, NT, BLK])
        near, hT, ohT = sb("m_near", [P, BLK]), sb("m_hT", [P, BLK]), sb("m_ohT", [ME, BLK])
        x3, h, cen, sq = (sb(f"m_{n}", [P, QT, D]) for n in ("x3", "h", "cen", "sq"))
        out_tile = sb("m_out", [P, 2, QT, D])
        st, spare = sb("m_st", [P, 2, QT]), sb("m_spare", [1, 1])
        logits, onehot = sb("m_logits", [P, QT, ME]), sb("m_onehot", [P, QT, ME])
        top, where, expert = sb("m_top", [P, QT, 8]), sb("m_where", [P, QT, 8], U32), sb("m_expert", [P, QT])
        hid = sb("m_hid", [P, 2, BLK])
        hsel = sb("m_hsel", [P, EC, BLK])
        ps_near, ps_turn, ps_out = ps("mp_near"), ps("mp_turn"), ps("mp_out")
        ps_hid, ps_sel = [ps(f"mp_hid{i}") for i in range(2)], [ps(f"mp_sel{i}") for i in range(2)]
        pack_landed = sem("m_pack_landed")
        adj_landed = [sem(f"m_adj_landed{i}") for i in range(len(PIECES))]
        (adj_used, near_copied, near_turned, links, var_ready, std_ready, h_ready, h_turned, hT_ready,
         logits_ready, logits_read, onehot_ready, onehot_turned, ohT_ready, hid_ready, hid_relu, hid_chosen,
         out_ready, out_added, out_stored) = (sem(f"m_{n}") for n in (
            "adj_used", "near_copied", "near_turned", "links", "var_ready", "std_ready", "h_ready", "h_turned",
            "hT_ready", "logits_ready", "logits_read", "onehot_ready", "onehot_turned", "ohT_ready", "hid_ready",
            "hid_relu", "hid_chosen", "out_ready", "out_added", "out_stored"))
        LINKS = 11
        block = ctx.enter_context(nc.Block())

        @block.sync
        def _(sp):
            sp.dma_start(wp[:], pack_in).then_inc(pack_landed, 16)

            def load(b, width, src):
                for i, (k0, k1) in enumerate(PIECES):
                    wait(sp, adj_used, len(PIECES) * (b - 1) + i + 1)
                    sp.dma_start(adj[:, k0:k1, 0:width], src[:, k0:k1, :]).then_inc(adj_landed[i], 16)

            def store(b, nt):
                sp.wait_ge(out_added, b + 1)
                sp.dma_start(out.rearrange("(t p) d -> p t d", p=P)[:, bass.ds(b * QT, nt), :],
                             out_tile[:, 0, 0:nt, :]).then_inc(out_stored, 16)

            load(0, BLK, adj_main[0])
            with sp.Fori(1, NB) as b:
                load(b, BLK, adj_main[bass.ds(b, 1)].rearrange("o p k m -> (o p) k m"))
                store(b - 1, QT)
            load(NB, LT * P, adj_last)
            store(NB - 1, QT)
            store(NB, LT)
            sp.wait_ge(out_stored, 16 * (NB + 1))

        @block.vector
        def _(dve):
            def choose(b, nt):
                link = Links(dve, links, b * LINKS, spare[:])
                tiles = slice(0, nt)
                rows = bass.ds(b * QT, nt)
                stat = (st[:, 0, tiles], st[:, 1, tiles])
                shape = [P, nt, D]
                dve.wait_ge(near_turned, b + 1)
                link(dve.tensor_tensor(x3[:, tiles, :], ps_turn[:, 0:nt * D].rearrange("p (t d) -> p t d", d=D),
                                       nb[:, rows, :], ALU.add))
                link(dve.scalar_tensor_tensor(x3[:, tiles, :], x3[:, tiles, :], 0.0, xres[:, rows, :],
                                              ALU.max, ALU.add))
                layernorm_head(dve, link, x3[:, tiles, :], cen[:, tiles, :], sq[:, tiles, :], stat, D, LN_EPS, var_ready)
                dve.wait_ge(std_ready, b + 1)
                rstd = layernorm_tail(dve, link, cen, stat, shape)
                dve.tensor_tensor(h[:, tiles, :], cen[:, tiles, :], rstd, ALU.mult).then_inc(h_ready, 1)
                dve.wait_ge(logits_ready, b + 1)
                dve.tensor_copy(logits[:, tiles, :], ps_out[:, 0:nt * ME].rearrange("p (t e) -> p t e", e=ME))\
                    .then_inc(logits_read, 1)
                dve.wait_ge(logits_read, b + 1)
                link.apart()
                for j in range(nt):
                    last = dve.max(top[:, j, :], logits[:, j, :])
                link(last, apart=True)
                for j in range(nt):
                    last = dve.max_index(where[:, j, :], top[:, j, :], logits[:, j, :])
                link(last)
                link(dve.tensor_copy(expert[:, tiles], where[:, tiles, 0]))
                for j in range(nt):
                    ins = dve.tensor_scalar(onehot[:, j, :], w["iota"], expert[:, j:j + 1], None, ALU.is_equal)
                link(ins)
                dve.nop().then_inc(onehot_ready, 1)
                for c in range(EC):
                    dve.wait_ge(hid_relu, b * EC + c + 1)
                    dve.tensor_tensor(hsel[:, c, 0:nt * P], ps_sel[c % 2][:, 0:nt * P], hid[:, c % 2, 0:nt * P],
                                      ALU.mult).then_inc(hid_chosen, 1)
                dve.wait_ge(out_ready, b + 1)
                wait(dve, out_stored, 16 * b)
                dve.scalar_tensor_tensor(out_tile[:, 0, tiles, :], ps_out[:, 0:nt * D].rearrange("p (t d) -> p t d", d=D),
                                         0.0, x3[:, tiles, :], ALU.max, ALU.add).then_inc(out_added, 1)
                dve.wait_ge(out_added, b + 1)
                assert nt < QT or link.n == LINKS, link.n

            choose(0, QT)
            with dve.Fori(1, NB) as b:
                choose(b, QT)
            choose(NB, LT)

        @block.scalar
        def _(act):
            def rows(b, nt):
                width = nt * P
                act.wait_ge(adj_used, len(PIECES) * (b + 1))
                act.copy(near[:, 0:width], ps_near[:, 0:width]).then_inc(near_copied, 1)
                act.wait_ge(var_ready, b + 1)
                act.activation(st[:, 0, 0:nt], st[:, 1, 0:nt], ACT.Sqrt).then_inc(std_ready, 1)
                act.wait_ge(h_turned, b + 1)
                act.copy(hT[:, 0:width], ps_near[:, 0:width]).then_inc(hT_ready, 1)
                act.wait_ge(onehot_turned, b + 1)
                act.copy(ohT[:, 0:width], ps_near[0:ME, 0:width]).then_inc(ohT_ready, 1)
                for c in range(EC):
                    act.wait_ge(hid_ready, b * EC + c + 1)
                    wait(act, hid_chosen, b * EC + c - 1)
                    act.activation(hid[:, c % 2, 0:width], ps_hid[c % 2][:, 0:width], ACT.Relu,
                                   bias=w["b1"][:, c:c + 1]).then_inc(hid_relu, 1)

            rows(0, QT)
            with act.Fori(1, NB) as b:
                rows(b, QT)
            rows(NB, LT)

        @block.tensor
        def _(pe):
            pe.wait_ge(pack_landed, 16)

            def rows(b, nt):
                width = nt * P
                cols = [slice(j * P, (j + 1) * P) for j in range(nt)]
                wait(pe, ohT_ready, b)
                for i, (k0, k1) in enumerate(PIECES):
                    pe.wait_ge(adj_landed[i], 16 * (b + 1))
                    for k in range(k0, k1):
                        last = pe.matmul(ps_near[:, 0:width], z[:, k, :], adj[:, k, 0:width],
                                         start=(k == 0), stop=(k == NT - 1))
                    last.then_inc(adj_used, 1)
                pe.wait_ge(near_copied, b + 1)
                for j in range(nt):
                    last = pe.matmul(ps_turn[:, cols[j]], near[:, cols[j]], w["ident"], start=True, stop=True)
                last.then_inc(near_turned, 1)
                pe.wait_ge(h_ready, b + 1)
                for j in range(nt):
                    last = pe.matmul(ps_near[:, cols[j]], h[:, j, :], w["ident"], start=True, stop=True)
                last.then_inc(h_turned, 1)
                pe.wait_ge(hT_ready, b + 1)
                wait(pe, out_added, b)
                for j in range(nt):
                    to = ps_out[:, j * ME:(j + 1) * ME]
                    pe.matmul(to, hT[:, cols[j]], w["routerT"], start=True, stop=False)
                    last = pe.matmul(to, w["ones_row"], w["router_b"], start=False, stop=True)
                last.then_inc(logits_ready, 1)
                pe.wait_ge(onehot_ready, b + 1)
                for j in range(nt):
                    last = pe.matmul(ps_near[0:ME, cols[j]], onehot[:, j, :], w["ident"], start=True, stop=True)
                last.then_inc(onehot_turned, 1)
                pe.wait_ge(ohT_ready, b + 1)
                for c in range(EC):
                    wait(pe, hid_chosen, b * EC + c - 1)
                    pe.matmul(ps_hid[c % 2][:, 0:width], w["w1"][:, c * P:(c + 1) * P], hT[:, 0:width], start=True, stop=True)
                    pe.matmul(ps_sel[c % 2][:, 0:width], w["rep"][:, c * P:(c + 1) * P], ohT[:, 0:width],
                              start=True, stop=True).then_inc(hid_ready, 1)
                pe.wait_ge(hid_chosen, (b + 1) * EC)
                pe.wait_ge(logits_read, b + 1)
                for j in range(nt):
                    to = ps_out[:, cols[j]]
                    for c in range(EC):
                        pe.matmul(to, hsel[:, c, cols[j]], w["w2"][:, c * D:(c + 1) * D], start=(c == 0), stop=False)
                    last = pe.matmul(to, ohT[:, cols[j]], w["b2"], start=False, stop=True)
                last.then_inc(out_ready, 1)

            rows(0, QT)
            with pe.Fori(1, NB) as b:
                rows(b, QT)
            rows(NB, LT)


def model_program(nc, x_in, adj_main, adj_last, pack_gnn0, pack_att, pack_post, pack_moe, o_scratch, out):
    with ExitStack() as ctx:
        rows = lambda ctx, name, width=D: ctx.enter_context(nc.sbuf_tensor(name, [P, NT, width], F32))
        xres = rows(ctx, "xres")
        z = rows(ctx, "z")
        nb = rows(ctx, "nb")
        with ExitStack() as middle:
            sxT = middle.enter_context(nc.sbuf_tensor("sxT", [P, NP], F32))
            rsum = rows(middle, "rsum", NH * NE)
            with ExitStack() as inner:
                kst = inner.enter_context(nc.sbuf_tensor("kst", [P, NH, NP], F32R))
                gnn0_program(nc, x_in, adj_main, adj_last, pack_gnn0, xres, z, sxT, kst, nb)
                attention_program(nc, pack_att, sxT, kst, nb, rsum, o_scratch)
            post_program(nc, pack_post, o_scratch, xres, sxT, rsum, z, nb)
        moe_program(nc, adj_main, adj_last, pack_moe, out, xres, z, nb)


def pack_weights(np, pack, arrays):
    packed, at = np.zeros((P, pack_width(pack)), np.float32), 0
    for name, rows, cols in pack:
        packed[0:rows, at:at + cols] = arrays[name]
        at += cols
    return packed


def kernel(**inputs):
    import numpy as np
    import concourse.bacc as bacc
    from concourse.bass_utils import run_bass_kernel_spmd

    a = {name: np.asarray(value) for name, value in inputs.items()}
    f = lambda name: a["L0_ffn_" + name]

    x = np.zeros((NP, D), np.float32)
    x[:N] = a["x"]
    adjT = np.zeros((NP, NP), np.float32)
    adjT[:N, :N] = a["adj"].T
    adjT = adjT.reshape(NT, P, NP).transpose(1, 0, 2)
    adj_main = np.ascontiguousarray(
        adjT[:, :, :NB * BLK].reshape(P, NT, NB, BLK).transpose(2, 0, 1, 3))
    adj_last = np.ascontiguousarray(adjT[:, :, NB * BLK:])

    wk = np.zeros((P, NH, P), np.float32)
    wq = np.zeros((P, NH, NE, P), np.float32)
    wv = np.zeros((P, NH * HD), np.float32)
    rep = np.zeros((P, NH, NE, HD), np.float32)
    gate_w = np.zeros((P, NH, NE, NE), np.float32)
    fc1, fc2 = np.zeros((P, D), np.float32), np.zeros((P, D), np.float32)
    for n in range(NH):
        rows = slice(n * HD, (n + 1) * HD)
        for part in range(1, 4):
            cols = slice(part * HD, (part + 1) * HD)
            wk[rows, n, cols] = f("wk")[n].T
            for e in range(NE):
                wq[rows, n, e, cols] = f("wq")[n, e].T
        wv[rows, rows] = f("wv")[n].T
        fc1[rows, rows] = f("fc1_w").T
        fc2[rows, rows] = f("fc2_w").T
        for e in range(NE):
            gate_w[e * HD:(e + 1) * HD, n, :, e] = f("gate_w")[n][:, e * HD:(e + 1) * HD].T
            rep[rows, n, e, :] = np.eye(HD, dtype=np.float32)
    ident = np.eye(P, dtype=np.float32)
    after = np.triu(np.ones((P, P), np.float32), 1) * np.float32(MASKED)
    sel = np.repeat(np.eye(16, dtype=np.float32), 2, axis=0)
    ones_row = np.ones((1, P), np.float32)
    ones_rows = np.zeros((P, 1), np.float32)
    ones_rows[:32] = 1.0
    first_row = np.zeros((P, 1), np.float32)
    first_row[::HD] = 1.0
    spread = lambda v: np.broadcast_to(v.reshape(1, -1), (P, v.size))
    weight = a["L0_gnn_weight"]
    pack_gnn0 = pack_weights(np, PACK_GNN0, dict(
        ident=ident, w_self=weight[:D], w_near=weight[D:], bias=a["L0_gnn_bias"].reshape(1, D), ones_row=ones_row,
        ones_rows=ones_rows, hl_wT=f("hl_w").reshape(NH * HD, D).T, hl_b=f("hl_b").reshape(P, 1),
        wk=wk.reshape(P, -1), wv=wv))
    pack_att = pack_weights(np, PACK_ATT, dict(
        ident=ident, mask_rows=after, mask_cols=after.T, sel=sel, ones32=np.ones((P, 32), np.float32),
        wq=wq.reshape(P, -1), first_rows=np.repeat(np.eye(NE, dtype=np.float32), HD, axis=0) * first_row))
    pack_post = pack_weights(np, PACK_POST, dict(
        ident=ident, ones_row=ones_row, rep=rep.reshape(P, -1), gate_w=gate_w.reshape(P, -1), gate_b=spread(f("gate_b")),
        ln_g=spread(f("ln_g")), ln_b=spread(f("ln_b")), fnorm_g=spread(f("fnorm_g")), fnorm_b=spread(f("fnorm_b")),
        fc1=fc1, fc2=fc2, fc1_b=np.tile(f("fc1_b"), NH).reshape(1, D), fc2_b=np.tile(f("fc2_b"), NH).reshape(1, D),
        fgateT=f("fgate_w").T, node_w=a["L1_gnn_W1"], node_b=a["L1_gnn_b"],
        node_w2=a["L1_gnn_W2"].transpose(1, 0, 2).reshape(P, -1)))
    pack_moe = pack_weights(np, PACK_MOE, dict(
        ident=ident, ones_row=ones_row, routerT=a["L1_ffn_router_w"].T, router_b=a["L1_ffn_router_b"].reshape(1, ME),
        iota=spread(np.arange(ME, dtype=np.float32)), w1=a["L1_ffn_W1"].transpose(1, 0, 2).reshape(P, -1),
        b1=a["L1_ffn_b1"].reshape(EC, P).T, w2=a["L1_ffn_W2"].reshape(EC, P, D).transpose(1, 0, 2).reshape(P, -1),
        b2=a["L1_ffn_b2"], rep=np.repeat(np.eye(ME, dtype=np.float32), MH, axis=1)))

    arrays = dict(x_in=x, adj_main=adj_main, adj_last=adj_last, pack_gnn0=pack_gnn0, pack_att=pack_att,
                  pack_post=pack_post, pack_moe=pack_moe)
    nc = bacc.Bacc("TRN2", target_bir_lowering=False, num_devices=1)
    args = {name: nc.dram_tensor(name, v.shape, F32, kind="ExternalInput").ap() for name, v in arrays.items()}
    args["out"] = nc.dram_tensor("out", (NP, D), F32, kind="ExternalOutput").ap()
    o_scratch = nc.dram_tensor("o_scratch", (NB + 1, P, NH, BLK), F32, kind="Internal").ap()
    model_program(nc, o_scratch=o_scratch, **args)
    result = run_bass_kernel_spmd(nc, [arrays], core_ids=[0]).results[0]["out"]
    return result[:N]
```

```python
from contextlib import ExitStack

import concourse.bass as bass
from concourse import mybir

ALU = mybir.AluOpType
ACT = mybir.ActivationFunctionType
X = mybir.AxisListType.X
F32 = mybir.dt.float32
F32R = mybir.dt.float32r
BF16 = mybir.dt.bfloat16
U32 = mybir.dt.uint32

P = 128
N = 3327
NT = -(-N // P)
NP = NT * P
D = 128
QT = 4
BLK = QT * P
NB = NT // QT
LT = NT - NB * QT
NH, NE, HD = 4, 4, 32
NODE_K = 16
ME, MH = 32, 32
EC = ME * MH // P
PIECES = ((0, 7), (7, 13), (13, 20), (20, 26))
SCORE_SCALE = float(HD) ** 0.5
MASKED = -1e30
LN_EPS, HEAD_LN_EPS = 1e-5, 1e-8

PACK_GNN0 = (
    ("ident", P, P), ("w_self", P, D), ("w_near", P, D), ("bias", 1, D), ("ones_row", 1, P),
    ("ones_rows", P, 1), ("hl_wT", P, D), ("hl_b", P, 1), ("wk", P, NH * P), ("wv", P, D),
)
PACK_ATT = (
    ("ident", P, P), ("mask_rows", P, P), ("mask_cols", P, P), ("sel", 32, 16), ("ones32", P, 32),
    ("wq", P, NH * NE * P), ("first_rows", P, NE),
)
PACK_POST = (
    ("ident", P, P), ("ones_row", 1, P), ("rep", P, NH * P), ("gate_w", P, NH * NE * NE),
    ("gate_b", P, NH * NE), ("ln_g", P, HD), ("ln_b", P, HD), ("fnorm_g", P, HD), ("fnorm_b", P, HD),
    ("fc1", P, D), ("fc2", P, D), ("fc1_b", 1, D), ("fc2_b", 1, D), ("fgateT", P, NH),
    ("node_w", P, NODE_K), ("node_b", NODE_K, D), ("node_w2", P, NODE_K * D),
)
PACK_MOE = (
    ("ident", P, P), ("ones_row", 1, P), ("routerT", P, ME), ("router_b", 1, ME), ("iota", P, ME),
    ("w1", P, ME * MH), ("b1", P, EC), ("w2", P, EC * D), ("b2", ME, D), ("rep", ME, ME * MH),
)


def pack_width(pack):
    return sum(cols for _, _, cols in pack)


def pack_views(tile, pack):
    views, at = {}, 0
    for name, rows, cols in pack:
        views[name] = tile[0:rows, at:at + cols]
        at += cols
    return views


def wait(eng, sem, value):
    if not isinstance(value, int) or value > 0:
        eng.wait_ge(sem, value)


class Links:

    def __init__(self, eng, sem, start=0, spare=None):
        self.eng, self.sem, self.start, self.n, self.spare = eng, sem, start, 0, spare

    def __call__(self, ins, apart=False):
        self.n += 1
        ins.then_inc(self.sem, 1)
        self.eng.wait_ge(self.sem, self.start + self.n)
        if apart:
            self.apart()

    def apart(self):
        self.eng.memset(self.spare, 0.0)


def layernorm_head(dve, link, src, cen, sq, stat, width, eps, std_asked):
    shape = list(src.shape)
    s0, s1 = stat
    link(dve.tensor_reduce(s0, src, X, ALU.add))
    link(dve.scalar_tensor_tensor(cen, s0.unsqueeze(len(shape) - 1).to_broadcast(shape), -1.0 / width, src, ALU.mult, ALU.add))
    link(dve.tensor_tensor(sq, cen, cen, ALU.mult))
    link(dve.tensor_reduce(s1, sq, X, ALU.add))
    dve.tensor_scalar(s1, s1, 1.0 / width, eps, ALU.mult, ALU.add).then_inc(std_asked, 1)


def layernorm_tail(dve, link, cen, stat, shape):
    s0, s1 = stat
    link(dve.reciprocal(s1, s0))
    return s1.unsqueeze(len(shape) - 1).to_broadcast(shape)


def gnn0_program(nc, x_in, adj_main, adj_last, pack_in, xres, xn, sxT, kst, vals):
    with ExitStack() as ctx:
        sb = lambda name, shape, dt=F32: ctx.enter_context(nc.sbuf_tensor(f"g_{name}", shape, dt))
        ps = lambda name: ctx.enter_context(nc.psum_tensor(f"gp_{name}", [P, 512], F32))
        sem = lambda name: ctx.enter_context(nc.semaphore(f"g_{name}"))
        wp = sb("wp", [P, pack_width(PACK_GNN0)])
        w = pack_views(wp, PACK_GNN0)
        adj = sb("adj", [P, NT, BLK])
        FIRST = ((0, 7), (7, 13), (13, 20), (20, 26))
        cen, sq = sb("cen", [P, 7, D]), sb("sq", [P, 7, D])
        st, spare = sb("st", [P, 2, 7]), sb("spare", [1, 1])
        near, xnT, hT, sxb = sb("near", [P, BLK]), sb("xnT", [P, BLK]), sb("hT", [P, BLK]), sb("sxb", [P, BLK])
        xnb, h = sb("xnb", [P, QT, D]), sb("h", [P, QT, D])
        ps_near, ps_turn, ps_h, ps_v = ps("near"), ps("turn"), ps("h"), ps("v")
        ps_k = [ps(f"k{n}") for n in range(NH)]
        x_landed, pack_landed = sem("x_landed"), sem("pack_landed")
        adj_landed = [sem(f"adj_landed{i}") for i in range(len(PIECES))]
        (adj_used, links, var_ready, std_ready, xn_ready, xn_staged, near_copied, xn_turned, xnT_copied, h_ready,
         x_updated, row_ready, row_turned, hT_ready, sx_summed, sx_ready, k_summed, k_high_ready, k_ready,
         v_summed, v_ready) = (sem(x) for x in (
            "adj_used", "links", "var_ready", "std_ready", "xn_ready", "xn_staged", "near_copied", "xn_turned",
            "xnT_copied", "h_ready", "x_updated", "row_ready", "row_turned", "hT_ready", "sx_summed", "sx_ready",
            "k_summed", "k_high_ready", "k_ready", "v_summed", "v_ready"))
        LINKS = 5
        STARTS = 5 * len(FIRST)
        block = ctx.enter_context(nc.Block())

        def for_blocks(eng, body):
            body(0, QT)
            with eng.Fori(1, NB) as b:
                body(b, QT)
            body(NB, LT)

        @block.sync
        def _(sp):
            sp.dma_start(xres[:], x_in.rearrange("(t p) d -> p t d", p=P)).then_inc(x_landed, 16)
            sp.dma_start(wp[:], pack_in).then_inc(pack_landed, 16)

            def load(b, width, src):
                for i, (k0, k1) in enumerate(PIECES):
                    wait(sp, adj_used, len(PIECES) * (b - 1) + i + 1)
                    sp.dma_start(adj[:, k0:k1, 0:width], src[:, k0:k1, :]).then_inc(adj_landed[i], 16)

            load(0, BLK, adj_main[0])
            with sp.Fori(1, NB) as b:
                load(b, BLK, adj_main[bass.ds(b, 1)].rearrange("o p k m -> (o p) k m"))
            load(NB, LT * P, adj_last)

        @block.vector
        def _(dve):
            link = Links(dve, links)
            dve.wait_ge(x_landed, 16)
            for g, (t0, t1) in enumerate(FIRST):
                n = t1 - t0
                stat = (st[:, 0, 0:n], st[:, 1, 0:n])
                layernorm_head(dve, link, xres[:, t0:t1, :], cen[:, 0:n, :], sq[:, 0:n, :], stat, D, LN_EPS, var_ready)
                dve.wait_ge(std_ready, g + 1)
                rstd = layernorm_tail(dve, link, cen[:], stat, [P, n, D])
                dve.tensor_tensor(xn[:, t0:t1, :], cen[:, 0:n, :], rstd, ALU.mult).then_inc(xn_ready, 1)
                dve.wait_ge(xn_ready, g + 1)

            def body(b, nt):
                link = Links(dve, links, STARTS + b * LINKS)
                xb = xres[:, bass.ds(b * QT, nt), :]
                width = nt * P
                dve.wait_ge(h_ready, b + 1)
                dve.scalar_tensor_tensor(xb, ps_h[:, 0:width].rearrange("p (t d) -> p t d", d=D), 0.0, xb,
                                         ALU.max, ALU.add).then_inc(x_updated, 1)
                dve.wait_ge(x_updated, b + 1)
                dve.memset(spare[:], 0.0)
                stat = (st[:, 0, 0:nt], st[:, 1, 0:nt])
                layernorm_head(dve, link, xb, cen[:, 0:nt, :], sq[:, 0:nt, :], stat, D, LN_EPS, var_ready)
                dve.wait_ge(std_ready, len(FIRST) + b + 1)
                rstd = layernorm_tail(dve, link, cen[:], stat, [P, nt, D])
                dve.tensor_tensor(h[:, 0:nt, :], cen[:, 0:nt, :], rstd, ALU.mult).then_inc(row_ready, 1)
                for n in range(NH):
                    dve.wait_ge(k_high_ready, NH * b + n + 1)
                    low = kst[64:96, n, bass.ds(b * BLK, width)]
                    dve.tensor_tensor(low, ps_k[n][64:96, 0:width], low.bitcast(F32), ALU.subtract).then_inc(k_ready, 1)
                assert link.n == LINKS, link.n

            for_blocks(dve, body)

        @block.scalar
        def _(act):
            for g, (t0, t1) in enumerate(FIRST):
                act.wait_ge(var_ready, g + 1)
                act.activation(st[:, 0, 0:t1 - t0], st[:, 1, 0:t1 - t0], ACT.Sqrt).then_inc(std_ready, 1)

            def sums(b, nt):
                width = nt * P
                act.wait_ge(adj_used, len(PIECES) * (b + 1))
                wait(act, h_ready, b)
                act.copy(near[:, 0:width], ps_near[:, 0:width]).then_inc(near_copied, 1)
                act.wait_ge(xn_turned, b + 1)
                act.copy(xnT[:, 0:width], ps_v[:, 0:width]).then_inc(xnT_copied, 1)

            def keys(b, nt):
                width = nt * P
                act.wait_ge(var_ready, len(FIRST) + b + 1)
                act.activation(st[:, 0, 0:nt], st[:, 1, 0:nt], ACT.Sqrt).then_inc(std_ready, 1)
                act.wait_ge(row_turned, b + 1)
                act.copy(hT[:, 0:width], ps_turn[:, 0:width]).then_inc(hT_ready, 1)
                act.wait_ge(sx_summed, b + 1)
                act.activation(sxb[:, 0:width], ps_h[:, 0:width], ACT.Identity, bias=w["hl_b"]).then_inc(sx_ready, 1)
                act.wait_ge(sx_ready, 2 * b + 1)
                act.copy(sxT[:, bass.ds(b * BLK, width)], sxb[:, 0:width]).then_inc(sx_ready, 1)
                for n in range(NH):
                    act.wait_ge(k_summed, NH * b + n + 1)
                    act.activation(kst[:, n, bass.ds(b * BLK, width)], ps_k[n][:, 0:width], ACT.Identity,
                                   bias=w["ones_rows"]).then_inc(k_high_ready, 1)
                act.wait_ge(v_summed, b + 1)
                act.copy(vals[:, bass.ds(b * QT, nt), :], ps_v[:, 0:width].rearrange("p (t d) -> p t d", d=D))\
                    .then_inc(v_ready, 1)

            sums(0, QT)
            with act.Fori(1, NB) as b:
                keys(b - 1, QT)
                sums(b, QT)
            keys(NB - 1, QT)
            sums(NB, LT)
            keys(NB, LT)

        @block.gpsimd
        def _(pool):
            def stage(b, nt):
                pool.wait_ge(xn_ready, len(FIRST))
                wait(pool, xn_turned, b)
                pool.tensor_copy(xnb[:, 0:nt, :], xn[:, bass.ds(b * QT, nt), :]).then_inc(xn_staged, 1)

            for_blocks(pool, stage)

        @block.tensor
        def _(pe):
            pe.wait_ge(pack_landed, 16)

            def piece(b, nt, i):
                k0, k1 = PIECES[i]
                pe.wait_ge(adj_landed[i], 16 * (b + 1))
                pe.wait_ge(xn_ready, i + 1)
                if i == 0:
                    wait(pe, near_copied, b)
                for k in range(k0, k1):
                    last = pe.matmul(ps_near[:, 0:nt * P], xn[:, k, :], adj[:, k, 0:nt * P],
                                     start=(k == 0), stop=(k == NT - 1))
                last.then_inc(adj_used, 1)

            def turn_xn(b, nt):
                pe.wait_ge(xn_staged, b + 1)
                wait(pe, v_ready, b)
                for j in range(nt):
                    last = pe.matmul(ps_v[:, j * P:(j + 1) * P], xnb[:, j, :], w["ident"], start=True, stop=True)
                last.then_inc(xn_turned, 1)

            def layer(b, nt):
                pe.wait_ge(near_copied, b + 1)
                pe.wait_ge(xnT_copied, b + 1)
                wait(pe, sx_ready, 2 * b)
                for j in range(nt):
                    cols = slice(j * P, (j + 1) * P)
                    pe.matmul(ps_h[:, cols], xnT[:, cols], w["w_self"], start=True, stop=False)
                    pe.matmul(ps_h[:, cols], near[:, cols], w["w_near"], start=False, stop=False)
                    last = pe.matmul(ps_h[:, cols], w["ones_row"], w["bias"], start=False, stop=True)
                last.then_inc(h_ready, 1)

            def turn_row(b, nt):
                pe.wait_ge(row_ready, b + 1)
                for j in range(nt):
                    last = pe.matmul(ps_turn[:, j * P:(j + 1) * P], h[:, j, :], w["ident"], start=True, stop=True)
                last.then_inc(row_turned, 1)

            def project(b, nt):
                pe.wait_ge(hT_ready, b + 1)
                pe.wait_ge(x_updated, b + 1)
                pe.matmul(ps_h[:, 0:nt * P], w["hl_wT"], hT[:, 0:nt * P], start=True, stop=True).then_inc(sx_summed, 1)

            def keys(b, nt):
                pe.wait_ge(sx_ready, 2 * b + 1)
                wait(pe, k_ready, NH * b)
                for n in range(NH):
                    pe.matmul(ps_k[n][:, 0:nt * P], w["wk"][:, n * P:(n + 1) * P], sxb[:, 0:nt * P],
                              start=True, stop=True).then_inc(k_summed, 1)
                for j in range(nt):
                    cols = slice(j * P, (j + 1) * P)
                    last = pe.matmul(ps_v[:, cols], sxb[:, cols], w["wv"], start=True, stop=True)
                last.then_inc(v_summed, 1)

            def sums_beside(b, nt, b0, nt0):
                piece(b, nt, 0)
                turn_row(b0, nt0)
                piece(b, nt, 1)
                project(b0, nt0)
                piece(b, nt, 2)
                keys(b0, nt0)
                piece(b, nt, 3)
                turn_xn(b, nt)
                layer(b, nt)

            for i in range(len(PIECES)):
                piece(0, QT, i)
            turn_xn(0, QT)
            layer(0, QT)
            with pe.Fori(1, NB) as b:
                sums_beside(b, QT, b - 1, QT)
            sums_beside(NB, LT, NB - 1, QT)
            turn_row(NB, LT)
            project(NB, LT)
            keys(NB, LT)


def attention_program(nc, pack_in, sxT, kst, vals, rsum, o_scratch):
    with ExitStack() as ctx:
        sb = lambda name, shape, dt=F32: ctx.enter_context(nc.sbuf_tensor(f"a_{name}", shape, dt))
        sem = lambda name: ctx.enter_context(nc.semaphore(f"a_{name}"))
        wp = sb("wp", [P, pack_width(PACK_ATT)])
        w = pack_views(wp, PACK_ATT)
        ident16, mask_rows, mask_cols = (sb(n, [P, P], BF16) for n in ("ident16", "mask_rows16", "mask_cols16"))
        kstat, vstat = sb("kstat", [P, BLK], F32R), sb("vstat", [P, QT, HD])
        qst = [sb(f"qst{i}", [P, NE, BLK], F32R) for i in range(2)]
        probs = [sb(f"probs{i}", [P, NE, BLK]) for i in range(QT)]
        pair_sum = [sb(f"pair_sum{i}", [P, NE, BLK]) for i in range(2)]
        m, m_chunk, m2 = sb("m", [P, 16]), sb("m_chunk", [P, 16]), sb("m2", [P, 16, 2])
        spare, zeros = sb("spare", [1, 1]), sb("zeros", [P, BLK], BF16)
        nothing = sb("nothing", [P, 1])
        o_tile, l_tile = [sb(f"o_tile{i}", [P, BLK]) for i in range(2)], sb("l_tile", [P, BLK])

        ps_slot = [ctx.enter_context(nc.psum_tensor(f"ap_slot{i}", [P, 512], F32)) for i in range(2)]
        ps_score = [ctx.enter_context(nc.psum_tensor(f"ap_score{i}", [P, 2, 512], F32)) for i in range(2)]
        ps_o = ctx.enter_context(nc.psum_tensor("ap_o", [P, 512], F32))
        ps_l = ctx.enter_context(nc.psum_tensor("ap_l", [P, 512], F32))

        pack_landed, masks_ready, m_cleared = sem("pack_landed"), sem("masks_ready"), sem("m_cleared")
        slot_ready, slot_free, q_high_ready, chunk_merged, max_half, max_split = (
            sem(x) for x in ("slot_ready", "slot_free", "q_high_ready", "chunk_merged", "max_half", "max_split"))
        keys_staged, vals_staged, scores_ready, probs_ready, o_summed = (
            sem(x) for x in ("keys_staged", "vals_staged", "scores_ready", "probs_ready", "o_summed"))
        pair_added, l_summed = ([sem(f"{x}{i}") for i in range(2)] for x in ("pair_added", "l_summed"))
        half_shifted = sem("half_shifted")
        pair_cleared = sem("pair_cleared")
        o_copied, l_copied, o_stored = sem("o_copied"), sem("l_copied"), [sem(f"o_stored{i}") for i in range(2)]
        block = ctx.enter_context(nc.Block())

        def keys_before(b, nt, n):
            return 8 * b * (b + 1) + n * (QT * b + nt)

        def chunks_before(b, n):
            return 2 * b * (b + 1) + n * (b + 1)

        def first_slot(b):
            if first(b):
                return Slot(NE + QT * NE + 1, 1)
            last = (QT - LT) * NE * (NB + 1) if isinstance(b, int) and b == NB else 0
            return Slot(20 + 32 * b * b + 72 * b - last, 0)

        class Slot:

            def __init__(self, at, odd):
                self.at, self.odd = at, odd

            def take(self):
                at, odd = self.at, self.odd
                self.at, self.odd = at + 1, 1 - odd
                return at, ps_slot[odd]

            def jump(self, at):
                self.at = at

        def first(b):
            return isinstance(b, int) and b == 0

        def following(b, nt, next_nt, n):
            if n + 1 < NH:
                return b, nt, n + 1
            return (b + 1, next_nt, 0) if next_nt else None

        def preceding(b, nt, n):
            if n > 0:
                return b, nt, n - 1
            return None if first(b) else (b - 1, QT, NH - 1)

        def for_blocks(eng, body):
            body(0, QT, QT)
            with eng.Fori(1, NB - 1) as b:
                body(b, QT, QT)
            body(NB - 1, QT, LT)
            body(NB, LT, 0)

        @block.sync
        def _(sp):
            sp.dma_start(wp[:], pack_in).then_inc(pack_landed, 16)

            def body(b, nt, next_nt):
                for n in range(NH):
                    sp.wait_ge(o_copied, NH * b + n + 1)
                    sp.dma_start(o_scratch[bass.ds(b, 1), :, n, 0:nt * P].rearrange("o p s -> (o p) s"),
                                 o_tile[n % 2][:, 0:nt * P]).then_inc(o_stored[n % 2], 16)

            for_blocks(sp, body)
            for stored in o_stored:
                sp.wait_ge(stored, 16 * (NH // 2) * (NB + 1))

        @block.gpsimd
        def _(pool):
            def chunk(keys, chunk_at, tiles, diagonal, width):
                for g in range(2):
                    even, odd = 2 * g, 2 * g + 1
                    wait(pool, l_summed[g], chunk_at)
                    if even >= tiles:
                        pool.nop().then_inc(pair_added[g], 1)
                        continue
                    pool.wait_ge(probs_ready, 2 * (keys + odd) + 2)
                    first = odd * P if diagonal else 0
                    if diagonal:
                        alone = probs[even][:, :, even * P:odd * P]
                        pool.tensor_tensor(pair_sum[g][:, :, even * P:odd * P], alone, nothing[:].unsqueeze(2).to_broadcast([P, NE, P]), ALU.add)
                    pool.tensor_tensor(pair_sum[g][:, :, first:width], probs[even][:, :, first:width],
                                       probs[odd][:, :, first:width], ALU.add).then_inc(pair_added[g], 1)

            def body(b, nt, next_nt):
                for n in range(NH):
                    keys, chunks = keys_before(b, nt, n), chunks_before(b, n)
                    chunk(keys, chunks, nt, True, nt * P)
                    if not first(b):
                        with pool.Fori(0, b) as c:
                            chunk(keys + nt + QT * c, chunks + 1 + c, QT, False, nt * P)

            pool.wait_ge(masks_ready, 1)
            for_blocks(pool, body)

        @block.scalar
        def _(act):
            def stage_keys(n, first_tile, tiles, keys):
                wait(act, scores_ready, 2 * keys)
                act.copy(kstat[:, 0:tiles * P], kst[:, n, bass.ds(first_tile * P, tiles * P)]).then_inc(keys_staged, 1)

            def stage_values(n, first_tile, tiles, keys):
                wait(act, o_summed, keys)
                act.copy(vstat[:, 0:tiles, :], vals[:, bass.ds(first_tile, tiles), n * HD:(n + 1) * HD])\
                    .then_inc(vals_staged, 1)

            def queries(nt, slot, n, first, last):
                for e in range(first, last):
                    s, to = slot.take()
                    act.wait_ge(slot_ready, s + 1)
                    act.activation(qst[n % 2][:, e, 0:nt * P], to[:, 0:nt * P], ACT.Copy, scale=SCORE_SCALE)\
                        .then_inc(q_high_ready, 1)

            def copy_sums(unit):
                b, nt, n = unit
                act.wait_ge(l_summed[1], chunks_before(b, n + 1))
                act.copy(l_tile[:, 0:nt * P], ps_l[:, 0:nt * P]).then_inc(l_copied, 1)

            def chunk(n, first_tile, tiles, keys, chunk_at, diagonal, width, before, ask=None):
                stage_values(n, first_tile, tiles, keys)
                for i in range(tiles):
                    wait(act, pair_added[i // 2], chunk_at)
                    for p in range(2):
                        act.wait_ge(scores_ready, 2 * (keys + i) + p + 1)
                        cols = slice(i * P if diagonal else 0, width)
                        act.activation(probs[i][:, 2 * p:2 * p + 2, cols], ps_score[p][:, :, cols], ACT.Exp)\
                            .then_inc(probs_ready, 1)
                    if i == 0 and ask:
                        ask()
                    if i == min(2, tiles - 1) and before:
                        copy_sums(before)

            def body(b, nt, next_nt):
                slot = first_slot(b)
                width = nt * P
                for n in range(NH):
                    keys, chunks = keys_before(b, nt, n), chunks_before(b, n)
                    ahead, before = following(b, nt, next_nt, n), preceding(b, nt, n)
                    if ahead:
                        queries(ahead[1], slot, ahead[2], 0, 2)
                        middle = Slot(slot.at, slot.odd)
                        slot.jump(slot.at + NE - 2)
                    if ahead:
                        slot.jump(slot.at + NE * ahead[1] * (ahead[0] + 1))
                        slot.take()
                    if before:
                        slot.take()
                    chunk(n, b * QT, nt, keys, chunks, True, width, before,
                          (lambda: queries(ahead[1], middle, ahead[2], 2, NE)) if ahead else None)
                    if not first(b):
                        with act.Fori(0, b) as c:
                            at = keys + nt + QT * c
                            stage_keys(n, c * QT, QT, at)
                            chunk(n, c * QT, QT, at, chunks + 1 + c, False, width, None)
                    if ahead:
                        stage_keys(ahead[2], ahead[0] * QT, ahead[1], keys_before(b, nt, n + 1))
                    act.wait_ge(o_summed, keys_before(b, nt, n + 1))
                    wait(act, o_stored[n % 2], 16 * (NH // 2 * b + n // 2))
                    act.copy(o_tile[n % 2][:, 0:width], ps_o[:, 0:width]).then_inc(o_copied, 1)

            act.wait_ge(pack_landed, 16)
            queries(QT, Slot(0, 0), 0, 0, NE)
            stage_keys(0, 0, QT, 0)
            for_blocks(act, body)
            copy_sums((NB, LT, NH - 1))

        @block.vector
        def _(dve):
            dve.memset(m[:], 0.0).then_inc(m_cleared, 1)
            dve.memset(nothing[:], 0.0).then_inc(masks_ready, 1)
            dve.memset(zeros[:], 0.0).then_inc(masks_ready, 1)
            dve.memset(m_chunk[:], 0.0).then_inc(chunk_merged, 1)
            dve.wait_ge(m_cleared, 1)
            dve.wait_ge(pack_landed, 16)
            for to, src in ((ident16, "ident"), (mask_rows, "mask_rows"), (mask_cols, "mask_cols")):
                dve.tensor_copy(to[:], w[src]).then_inc(masks_ready, 1)

            def queries(unit, slot):
                b, nt, n = unit
                for e in range(NE):
                    s, at = slot.take()
                    dve.wait_ge(q_high_ready, NE * (NH * b + n) + e + 1)
                    low = qst[n % 2][96:128, e, 0:nt * P]
                    dve.scalar_tensor_tensor(low, at[96:128, 0:nt * P], SCORE_SCALE, low.bitcast(F32),
                                             ALU.mult, ALU.subtract).then_inc(slot_free, 1)

            def maxima(nt, slot, to, widths):
                for j in range(nt):
                    for e in range(NE):
                        s, at = slot.take()
                        dve.wait_ge(slot_ready, s + 1)
                        dve.tensor_reduce(to[:, e * QT + j:e * QT + j + 1], at[:, 0:widths[j]], X, ALU.max)\
                            .then_inc(slot_free, 1)

            def diagonal_maxima(unit, slot):
                b, nt, n = unit
                wait(dve, max_split, NH * b + n)
                maxima(nt, slot, m, [(j + 1) * P for j in range(nt)])

            def chunk_maxima(unit, slot, c):
                b, nt, n = unit
                dve.wait_ge(chunk_merged, 2 * b * (b - 1) + n * b + 1 + c)
                maxima(nt, slot, m_chunk, [BLK] * nt)
                dve.wait_ge(slot_free, slot.at)
                dve.tensor_tensor(m[:], m[:], m_chunk[:], ALU.max).then_inc(chunk_merged, 1)

            def shift(unit, slot):
                b, nt, n = unit
                dve.wait_ge(slot_free, slot.at)
                wait(dve, chunk_merged, 2 * b * (b - 1) + (n + 1) * b + 1)
                dve.tensor_scalar(m2[:, :, 0].bitcast(F32R), m[:], -1.0, None, ALU.mult).then_inc(max_half, 1)
                dve.wait_ge(max_half, NH * b + n + 1)
                dve.scalar_tensor_tensor(m2[:, :, 1], m[:], -1.0, m2[:, :, 0], ALU.mult, ALU.subtract)\
                    .then_inc(max_split, 1)
                s, at = slot.take()
                dve.wait_ge(slot_ready, s + 1)
                shape = [32, 2, nt, P]
                for pair, done in ((slice(0, 2), half_shifted), (slice(2, 4), slot_free)):
                    rows = qst[n % 2][0:32, pair, 0:nt * P].rearrange("r e (j s) -> r e j s", s=P)
                    mine = w["sel"].rearrange("r (e j) -> r e j", j=QT)[:, pair, 0:nt].unsqueeze(3).to_broadcast(shape)
                    dve.tensor_tensor(rows, at[0:32, 0:P].unsqueeze(1).unsqueeze(1).to_broadcast(shape), mine,
                                      ALU.mult).then_inc(done, 1)

            def invert_sums(unit, slot):
                b, nt, n = unit
                s, at = slot.take()
                dve.wait_ge(slot_ready, s + 1)
                if not isinstance(b, int):
                    dve.memset(spare[:], 0.0)
                dve.reciprocal(rsum[:, bass.ds(b * QT, nt), n * NE:(n + 1) * NE],
                               at[:, 0:nt * NE].rearrange("p (t e) -> p t e", e=NE)).then_inc(slot_free, 1)

            def clear(b, nt, n):
                wait(dve, l_summed[1], chunks_before(b, n))
                dve.memset(pair_sum[1][:, :, 0:2 * P], 0.0).then_inc(pair_cleared, 1)

            def body(b, nt, next_nt):
                slot = first_slot(b)
                for n in range(NH):
                    ahead, before = following(b, nt, next_nt, n), preceding(b, nt, n)
                    if ahead:
                        queries(ahead, slot)
                        diagonal_maxima(ahead, slot)
                        if ahead[2] == 0:
                            chunk_maxima(ahead, slot, 0)
                    clear(b, nt, n)
                    if before:
                        invert_sums(before, slot)
                    if ahead and not first(b):
                        start = slot.at
                        with dve.Fori(0, b) as c:
                            slot.jump(start + NE * ahead[1] * c)
                            at_chunk = c if ahead[2] else c + 1
                            chunk_maxima(ahead, slot, at_chunk)
                        slot.jump(start + NE * ahead[1] * b)
                    if ahead:
                        shift(ahead, slot)
                return slot

            slot = Slot(0, 0)
            queries((0, QT, 0), slot)
            diagonal_maxima((0, QT, 0), slot)
            shift((0, QT, 0), slot)
            ends = []
            for_blocks(dve, lambda *block: ends.append(body(*block)))
            invert_sums((NB, LT, NH - 1), ends[-1])

        @block.tensor
        def _(pe):
            pe.wait_ge(pack_landed, 16)
            pe.wait_ge(masks_ready, 5)

            def query(unit, slot, e):
                b, nt, n = unit
                s, to = slot.take()
                wait(pe, slot_free, s - 1)
                at = (n * NE + e) * P
                pe.matmul(to[:, 0:nt * P], w["wq"][:, at:at + P], sxT[:, bass.ds(b * BLK, nt * P)],
                          start=True, stop=True).then_inc(slot_ready, 1)

            def for_max(unit, slot, j, e, c):
                b, nt, n = unit
                s, to = slot.take()
                wait(pe, slot_free, s - 1)
                diagonal = c is None
                width = (j + 1) * P if diagonal else BLK
                last = pe.matmul(to[:, 0:width], qst[n % 2][:, e, j * P:(j + 1) * P],
                                 kst[:, n, bass.ds((b if diagonal else c) * BLK, width)], start=True, stop=True)
                if diagonal:
                    last = pe.matmul(to[:, width - P:width], ident16[:], mask_rows[:], start=False, stop=True,
                                     skip_group_check=True)
                last.then_inc(slot_ready, 1)

            def scores(n, keys, i, p, cols, diagonal):
                wait(pe, probs_ready, 2 * (keys + i - 1) + p + 1)
                for e in range(2):
                    last = pe.matmul(ps_score[p][:, e, cols], kstat[:, i * P:(i + 1) * P],
                                     qst[n % 2][:, 2 * p + e, cols], start=True, stop=True)
                    if diagonal:
                        last = pe.matmul(ps_score[p][:, e, cols.start:cols.start + P], ident16[:], mask_cols[:],
                                         start=False, stop=True, skip_group_check=True)
                last.then_inc(scores_ready, 1)

            def outputs(keys, i, cols, start):
                pe.wait_ge(probs_ready, 2 * (keys + i) + 2)
                for e in range(NE):
                    last = pe.matmul(ps_o[e * HD:(e + 1) * HD, cols], vstat[:, i, :], probs[i][:, e, cols],
                                     start=start, stop=True, skip_group_check=True)
                last.then_inc(o_summed, 1)

            def sums(g, chunks, unit):
                b, nt, n = unit
                pe.wait_ge(pair_added[g], chunks)
                if g == 1:
                    pe.wait_ge(pair_cleared, NH * b + n + 1)
                for e in range(NE):
                    last = pe.matmul(ps_l[e * HD:(e + 1) * HD, 0:nt * P], w["ones32"], pair_sum[g][:, e, 0:nt * P],
                                     start=False, stop=True, skip_group_check=True)
                last.then_inc(l_summed[g], 1)

            def zero_sums():
                pe.matmul(ps_l[:], zeros[:, 0:P], zeros[:], start=True, stop=True, skip_group_check=True)

            def turn_sums(unit, slot):
                b, nt, n = unit
                s, to = slot.take()
                wait(pe, slot_free, s - 1)
                pe.wait_ge(l_copied, NH * b + n + 1)
                for j in range(nt):
                    last = pe.matmul(to[:, j * NE:(j + 1) * NE], l_tile[:, j * P:(j + 1) * P], w["first_rows"],
                                     start=True, stop=True)
                last.then_inc(slot_ready, 1)

            def chunk(unit, slot, ahead, maxima, before, keys, chunk_at, tiles, diagonal, shift_at=None):
                b, nt, n = unit
                width = nt * P
                cols = [slice(i * P if diagonal else 0, width) for i in range(tiles)]
                asks = diagonal and ahead is not None
                per = -(-len(maxima) // (tiles - asks))
                pe.wait_ge(keys_staged, chunk_at + 1)
                for i in range(tiles):
                    at = i - asks
                    beside = maxima[at * per:(at + 1) * per] if at >= 0 else []
                    half = len(beside) // 2
                    for pair in range(2):
                        if diagonal and i == 0:
                            pe.wait_ge(*((half_shifted, NH * b + n + 1), (slot_free, shift_at))[pair])
                        scores(n, keys, i, pair, cols[i], diagonal)
                    if i == 0 and asks:
                        for e in range(1, NE):
                            query(ahead, slot, e)
                        queries_at = slot.at
                    if i == 1 and asks:
                        pe.wait_ge(slot_free, queries_at)
                    for at in beside[0:half]:
                        for_max(ahead, slot, *at)
                    if i == 0 and (before or not diagonal):
                        sums(0, chunk_at, before or unit)
                    if i == min(2, tiles - 1) and (before or not diagonal):
                        sums(1, chunk_at, before or unit)
                    if i == 1:
                        pe.wait_ge(vals_staged, chunk_at + 1)
                        if diagonal:
                            wait(pe, o_copied, NH * b + n)
                    if i > 0:
                        outputs(keys, i - 1, cols[i - 1], diagonal and i == 1)
                    for at in beside[half:]:
                        for_max(ahead, slot, *at)
                outputs(keys, tiles - 1, cols[tiles - 1], diagonal and tiles == 1)
                if diagonal:
                    if before:
                        turn_sums(before, slot)
                    zero_sums()

            def turn_max(unit, slot):
                b, nt, n = unit
                s, to = slot.take()
                pe.wait_ge(max_split, NH * b + n + 1)
                wait(pe, slot_free, s - 1)
                pe.matmul(to[0:32, 0:P], m2[:].rearrange("p g h -> p (g h)"), w["ident"], start=True, stop=True)\
                    .then_inc(slot_ready, 1)

            def body(b, nt, next_nt):
                slot = first_slot(b)
                for n in range(NH):
                    unit = (b, nt, n)
                    keys, chunks = keys_before(b, nt, n), chunks_before(b, n)
                    ahead, before = following(b, nt, next_nt, n), preceding(b, nt, n)
                    shift_at = slot.at
                    each, diagonal = [], []
                    if ahead:
                        query(ahead, slot, 0)
                        each = [(j, e) for j in range(ahead[1]) for e in range(NE)]
                        diagonal = [(j, e, None) for j, e in each]
                        if ahead[2] == 0:
                            diagonal += [(j, e, b) for j, e in each]
                    chunk(unit, slot, ahead, diagonal, before, keys, chunks, nt, True, shift_at)
                    if not first(b):
                        start = slot.at
                        with pe.Fori(0, b) as c:
                            slot.jump(start + len(each) * c)
                            chunk(unit, slot, ahead, [(j, e, c) for j, e in each], None,
                                  keys + nt + QT * c, chunks + 1 + c, QT, False)
                        slot.jump(start + len(each) * b)
                    if ahead:
                        turn_max(ahead, slot)
                return slot

            slot, unit = Slot(0, 0), (0, QT, 0)
            for e in range(NE):
                query(unit, slot, e)
            pe.wait_ge(slot_free, slot.at)
            for j in range(QT):
                for e in range(NE):
                    for_max(unit, slot, j, e, None)
            turn_max(unit, slot)
            ends = []
            for_blocks(pe, lambda *block: ends.append(body(*block)))
            last = (NB, LT, NH - 1)
            for g in range(2):
                sums(g, chunks_before(NB, NH), last)
            turn_sums(last, ends[-1])


def post_program(nc, pack_in, o_scratch, xres, sxT, rsum, z, nb):
    with ExitStack() as ctx:
        sb = lambda name, shape, dt=F32: ctx.enter_context(nc.sbuf_tensor(f"p_{name}", shape, dt))
        ps = lambda name: ctx.enter_context(nc.psum_tensor(f"pp_{name}", [P, 512], F32))
        sem = lambda name: ctx.enter_context(nc.semaphore(f"p_{name}"))
        wp = sb("wp", [P, pack_width(PACK_POST)])
        w = pack_views(wp, PACK_POST)
        o_in, onT = sb("o_in", [P, NH, BLK]), sb("onT", [P, NH, BLK])
        sxb, turnT, hT, nodeT = sb("sxb", [P, BLK]), sb("turnT", [P, BLK]), sb("hT", [P, BLK]), sb("nodeT", [NODE_K, BLK])
        h, cen, sq, nz = (sb(n, [P, QT, D]) for n in ("h", "cen", "sq", "nz"))
        st = sb("st", [P, 2, QT * NH])
        gate_terms = sb("gate_terms", [P, QT * NH, NE, NE])
        gate, gtop, gsum = sb("gate", [P, QT * NH, NE]), sb("gtop", [P, QT * NH]), sb("gsum", [P, QT * NH])
        prod, zprod = sb("prod", [P, QT, 512]), [sb(f"zprod{i}", [P, NODE_K * D]) for i in range(2)]
        node, spare = sb("node", [P, QT, NODE_K]), sb("spare", [1, 1])
        bank, ps_turn, ps_out, ps_z = [ps(f"bank{i}") for i in range(4)], ps("turn"), ps("out"), [ps(f"z{i}") for i in range(2)]

        pack_landed, links, z_links = sem("pack_landed"), sem("links"), sem("z_links")
        (o_landed, sx_staged, sx_spread, masked, gates_ready, outs_ready, sx_turned, exp_asked, exp_ready,
         var_ready, std_ready, row_ready, turned, turn_copied, fc_ready, fgate_ready, node_ready, nodeT_ready,
         node_copied, nb_ready, nb_copied, z_ready, z_scaled, z_summed) = (sem(x) for x in (
            "o_landed", "sx_staged", "sx_spread", "masked", "gates_ready", "outs_ready", "sx_turned", "exp_asked",
            "exp_ready", "var_ready", "std_ready", "row_ready", "turned", "turn_copied", "fc_ready", "fgate_ready",
            "node_ready", "nodeT_ready", "node_copied", "nb_ready", "nb_copied", "z_ready", "z_scaled", "z_summed"))
        block = ctx.enter_context(nc.Block())

        LINKS = 40

        def row_view(tile, nt):
            return tile[:, 0:nt * P].rearrange("p (t d) -> p t d", d=D)

        def heads_view(tile, nt):
            return tile[:, 0:nt, :].rearrange("p t (n d) -> p (t n) d", d=HD)

        def for_blocks(eng, body):
            body(0, QT, None)
            body(1, QT, 0)
            with eng.Fori(2, NB) as b:
                body(b, QT, b - 1)
            body(NB, LT, NB - 1)

        @block.sync
        def _(sp):
            sp.dma_start(wp[:], pack_in).then_inc(pack_landed, 16)

            def body(b, nt, b0):
                wait(sp, masked, NH * b)
                sp.dma_start(o_in[:, :, 0:nt * P], o_scratch[bass.ds(b, 1), :, :, 0:nt * P].rearrange("o p n s -> (o p) n s"))\
                    .then_inc(o_landed, 16)

            for_blocks(sp, body)

        @block.gpsimd
        def _(pool):
            def sum_z(b, nt):
                for j in range(nt):
                    link = Links(pool, z_links, 3 * (QT * b + j))
                    terms = zprod[j % 2]
                    pool.wait_ge(z_scaled, 4 * (QT * b + j) + 4)
                    width = NODE_K * D // 2
                    while width > D:
                        link(pool.tensor_tensor(terms[:, 0:width], terms[:, 0:width], terms[:, width:2 * width], ALU.add))
                        width //= 2
                    pool.tensor_tensor(z[:, bass.ds(b * QT + j, 1), :].rearrange("p o f -> p (o f)"),
                                       terms[:, 0:D], terms[:, D:2 * D], ALU.add).then_inc(z_summed, 1)

            with pool.Fori(0, NB) as b:
                sum_z(b, QT)
            sum_z(NB, LT)

        @block.scalar
        def _(act):
            def scale_z(b, first, last):
                for s in range(first, last):
                    j, q = s // 4, s % 4
                    act.wait_ge(z_ready, 16 * b + s + 1)
                    if q == 0:
                        wait(act, z_summed, QT * b + j - 1)
                    for i in range(4):
                        k = 4 * q + i
                        last_one = act.activation(zprod[j % 2][:, k * D:(k + 1) * D], ps_z[q % 2][:, i * D:(i + 1) * D],
                                                  ACT.Identity, scale=node[:, j, k:k + 1])
                    last_one.then_inc(z_scaled, 1)

            def root(b, i, count):
                act.wait_ge(var_ready, 3 * b + i)
                act.activation(st[:, 0, 0:count], st[:, 1, 0:count], ACT.Sqrt).then_inc(std_ready, 1)

            def turn(b, nt, i, to):
                act.wait_ge(turned, 4 * b + i)
                act.copy(to[:, 0:nt * P], ps_turn[:, 0:nt * P]).then_inc(turn_copied, 1)

            def exponent(b, i, count):
                act.wait_ge(exp_asked, 2 * b + i)
                g = gate[:, 0:count, :]
                act.activation(g, g, ACT.Exp).then_inc(exp_ready, 1)

            def body(b, nt, b0):
                width = nt * P
                beside = (lambda first, last: scale_z(b0, first, last)) if b0 is not None else (lambda *_: None)
                wait(act, sx_turned, b)
                act.copy(sxb[:, 0:width], sxT[:, bass.ds(b * BLK, width)]).then_inc(sx_staged, 1)
                beside(0, 3)
                exponent(b, 1, nt * NH)
                beside(3, 7)
                root(b, 1, nt * NH)
                turn(b, nt, 1, turnT)
                beside(7, 9)
                turn(b, nt, 2, turnT)
                beside(9, 12)
                root(b, 2, nt * NH)
                turn(b, nt, 3, turnT)
                beside(12, 13)
                exponent(b, 2, nt)
                beside(13, 16)
                root(b, 3, nt)
                turn(b, nt, 4, hT)
                act.wait_ge(node_ready, b + 1)
                act.copy(nodeT[:, 0:width], ps_out[0:NODE_K, 0:width]).then_inc(nodeT_ready, 1)
                act.wait_ge(nb_ready, b + 1)
                act.copy(nb[:, bass.ds(b * QT, nt), :], row_view(ps_out, nt)).then_inc(nb_copied, 1)

            act.wait_ge(pack_landed, 16)
            for_blocks(act, body)
            act.wait_ge(node_copied, NB + 1)
            scale_z(NB, 0, 4 * LT)

        @block.vector
        def _(dve):
            dve.wait_ge(pack_landed, 16)

            def softmax(b, i, link, count, read):
                shape = [P, count, NE]
                g, top, total = gate[:, 0:count, :], gtop[:, 0:count], gsum[:, 0:count]
                link(read(g))
                link(dve.tensor_reduce(top, g, X, ALU.max))
                dve.tensor_tensor(g, g, top.unsqueeze(2).to_broadcast(shape), ALU.subtract).then_inc(exp_asked, 1)
                dve.wait_ge(exp_ready, 2 * b + i)
                link(dve.tensor_reduce(total, g, X, ALU.add))
                link(dve.reciprocal(total, total))
                link(dve.tensor_tensor(g, g, total.unsqueeze(2).to_broadcast(shape), ALU.mult))

            def layernorm(b, i, link, src, to, shape, eps, affine=None):
                count, width = shape[1], shape[2]
                view = (lambda t: t[:, 0:shape[1], :]) if width == D else (lambda t: heads_view(t, shape[1] // NH))
                stat = (st[:, 0, 0:count], st[:, 1, 0:count])
                link.apart()
                layernorm_head(dve, link, src, view(cen), view(sq), stat, width, eps, var_ready)
                dve.wait_ge(std_ready, 3 * b + i)
                rstd = layernorm_tail(dve, link, view(cen), stat, shape)
                last = dve.tensor_tensor(to, view(cen), rstd, ALU.mult)
                if affine:
                    link(last)
                    link(dve.tensor_tensor(to, to, w[affine[0]].unsqueeze(1).to_broadcast(shape), ALU.mult))
                    last = dve.tensor_tensor(to, to, w[affine[1]].unsqueeze(1).to_broadcast(shape), ALU.add)
                return last

            def body(b, nt, b0):
                width, groups = nt * P, nt * NH
                link = Links(dve, links, b * LINKS, spare[:])
                xb = xres[:, bass.ds(b * QT, nt), :]
                dve.wait_ge(o_landed, 16 * (b + 1))
                for n in range(NH):
                    dve.wait_ge(sx_spread, NH * b + n + 1)
                    dve.scalar_tensor_tensor(onT[:, n, 0:width], bank[n][:, 0:width], 0.0, o_in[:, n, 0:width],
                                             ALU.not_equal, ALU.mult).then_inc(masked, 1)

                rs = rsum[:, bass.ds(b * QT, nt), :].rearrange("p t (n e) -> p (t n) e", e=NE)
                terms = gate_terms[:, 0:groups, :, :]
                dve.wait_ge(gates_ready, b + 1)
                link(dve.tensor_tensor(terms, ps_out[:, 0:groups * NE * NE].rearrange("p (g o e) -> p g o e", o=NE, e=NE),
                                       rs.unsqueeze(2).to_broadcast([P, groups, NE, NE]), ALU.mult), apart=True)
                link(dve.tensor_reduce(gate[:, 0:groups, :], terms, X, ALU.add))
                gb = w["gate_b"].rearrange("p (n e) -> p n e", e=NE).unsqueeze(1).to_broadcast([P, nt, NH, NE])
                with_heads = lambda g: g.rearrange("p (t n) e -> p t n e", n=NH)
                softmax(b, 1, link, groups, lambda g: dve.tensor_tensor(with_heads(g), with_heads(g), gb, ALU.add))
                link(dve.tensor_tensor(gate[:, 0:groups, :], gate[:, 0:groups, :], rs, ALU.mult))
                dve.wait_ge(outs_ready, b + 1)
                for j in range(nt):
                    shape = [P, NH * NE, HD]
                    gs = gate[:, j * NH:(j + 1) * NH, :].rearrange("p n e -> p (n e)").unsqueeze(2).to_broadcast(shape)
                    last = dve.tensor_tensor(prod[:, j, :].rearrange("p (g d) -> p g d", d=HD),
                                             bank[j][:].rearrange("p (g d) -> p g d", d=HD), gs, ALU.mult)
                link(last)
                hv = heads_view(h, nt)
                link(dve.tensor_reduce(hv, prod[:, 0:nt, :].rearrange("p t (n e d) -> p (t n) d e", e=NE, d=HD), X, ALU.add))
                dve.wait_ge(sx_turned, b + 1)
                link(dve.tensor_tensor(h[:, 0:nt, :], row_view(ps_turn, nt), h[:, 0:nt, :], ALU.add))
                layernorm(b, 1, link, hv, hv, [P, groups, HD], HEAD_LN_EPS, ("ln_g", "ln_b")).then_inc(row_ready, 1)
                dve.wait_ge(row_ready, 4 * b + 1)
                link(dve.tensor_single_scalar(nz[:, 0:nt, :], h[:, 0:nt, :], 0.0, ALU.not_equal))
                dve.wait_ge(fc_ready, 2 * b + 1)
                dve.scalar_tensor_tensor(sq[:, 0:nt, :], row_view(ps_out, nt), 0.0, nz[:, 0:nt, :], ALU.max, ALU.mult)\
                    .then_inc(row_ready, 1)
                dve.wait_ge(fc_ready, 2 * b + 2)
                link(dve.tensor_tensor(nz[:, 0:nt, :], row_view(ps_out, nt), nz[:, 0:nt, :], ALU.mult))
                link(dve.tensor_tensor(h[:, 0:nt, :], h[:, 0:nt, :], nz[:, 0:nt, :], ALU.add))
                layernorm(b, 2, link, hv, hv, [P, groups, HD], HEAD_LN_EPS, ("fnorm_g", "fnorm_b")).then_inc(row_ready, 1)
                dve.wait_ge(fgate_ready, b + 1)
                softmax(b, 2, link, nt, lambda g: dve.tensor_copy(
                    g, ps_out[:, 0:groups].rearrange("p (t n) -> p t n", n=NH)))
                fg = gate[:, 0:nt, :].rearrange("p t n -> p (t n)").unsqueeze(2).to_broadcast([P, groups, HD])
                link(dve.tensor_tensor(heads_view(cen, nt), hv, fg, ALU.mult))
                link(dve.tensor_tensor(xb, xb, cen[:, 0:nt, :], ALU.add))
                layernorm(b, 3, link, xb, h[:, 0:nt, :], [P, nt, D], LN_EPS).then_inc(row_ready, 1)
                dve.wait_ge(node_ready, b + 1)
                dve.tensor_copy(node[:, 0:nt, :], ps_turn[:, 0:nt * NODE_K].rearrange("p (t k) -> p t k", k=NODE_K))\
                    .then_inc(node_copied, 1)
                assert link.n == LINKS, link.n

            for_blocks(dve, body)

        @block.tensor
        def _(pe):
            pe.wait_ge(pack_landed, 16)

            def turn(b, nt, i, src):
                pe.wait_ge(row_ready, 4 * b + i)
                for j in range(nt):
                    last = pe.matmul(ps_turn[:, j * P:(j + 1) * P], src[:, j, :], w["ident"], start=True, stop=True)
                last.then_inc(turned, 1)

            def z_products(b, first, last):
                for s in range(first, last):
                    j, q = s // 4, s % 4
                    wait(pe, z_scaled, 16 * b + s - 1)
                    pe.matmul(ps_z[q % 2][:], hT[:, j * P:(j + 1) * P], w["node_w2"][:, q * 512:(q + 1) * 512],
                              start=True, stop=True).then_inc(z_ready, 1)

            def body(b, nt, b0):
                width = nt * P
                cols = [slice(j * P, (j + 1) * P) for j in range(nt)]
                beside = (lambda first, last: z_products(b0, first, last)) if b0 is not None else (lambda *_: None)
                pe.wait_ge(sx_staged, b + 1)
                for n in range(NH):
                    pe.matmul(bank[n][:, 0:width], w["rep"][:, n * P:(n + 1) * P], sxb[:, 0:width],
                              start=True, stop=True).then_inc(sx_spread, 1)
                wait(pe, node_copied, b)
                for j in range(nt):
                    last = pe.matmul(ps_turn[:, cols[j]], sxb[:, cols[j]], w["ident"], start=True, stop=True)
                last.then_inc(sx_turned, 1)
                beside(0, 3)
                pe.wait_ge(masked, NH * (b + 1))
                wait(pe, nb_copied, b)
                for j in range(nt):
                    for n in range(NH):
                        at = (j * NH + n) * NE * NE
                        last = pe.matmul(ps_out[:, at:at + NE * NE], onT[:, n, cols[j]],
                                         w["gate_w"][:, n * NE * NE:(n + 1) * NE * NE], start=True, stop=True)
                last.then_inc(gates_ready, 1)
                for j in range(nt):
                    for n in range(NH):
                        last = pe.matmul(bank[j][:, n * P:(n + 1) * P], onT[:, n, cols[j]], w["ident"], start=True, stop=True)
                last.then_inc(outs_ready, 1)
                beside(3, 7)
                for layer, src in enumerate((h, sq)):
                    turn(b, nt, 1 + layer, src)
                    beside(*((7, 8), (9, 10))[layer])
                    pe.wait_ge(turn_copied, 4 * b + 1 + layer)
                    for j in range(nt):
                        pe.matmul(ps_out[:, cols[j]], turnT[:, cols[j]], w[f"fc{layer + 1}"], start=True, stop=False)
                        last = pe.matmul(ps_out[:, cols[j]], w["ones_row"], w[f"fc{layer + 1}_b"], start=False, stop=True)
                    last.then_inc(fc_ready, 1)
                    beside(*((8, 9), (10, 12))[layer])
                turn(b, nt, 3, h)
                beside(12, 13)
                pe.wait_ge(turn_copied, 4 * b + 3)
                for j in range(nt):
                    last = pe.matmul(ps_out[:, j * NH:(j + 1) * NH], turnT[:, cols[j]], w["fgateT"], start=True, stop=True)
                last.then_inc(fgate_ready, 1)
                beside(13, 16)
                turn(b, nt, 4, h)
                pe.wait_ge(turn_copied, 4 * b + 4)
                pe.matmul(ps_out[0:NODE_K, 0:width], w["node_w"], hT[:, 0:width], start=True, stop=True)
                for j in range(nt):
                    last = pe.matmul(ps_turn[:, j * NODE_K:(j + 1) * NODE_K], hT[:, cols[j]], w["node_w"],
                                     start=True, stop=True)
                last.then_inc(node_ready, 1)
                pe.wait_ge(nodeT_ready, b + 1)
                for j in range(nt):
                    last = pe.matmul(ps_out[:, cols[j]], nodeT[:, cols[j]], w["node_b"], start=True, stop=True)
                last.then_inc(nb_ready, 1)

            for_blocks(pe, body)
            z_products(NB, 0, 4 * LT)


def moe_program(nc, adj_main, adj_last, pack_in, out, xres, z, nb):
    with ExitStack() as ctx:
        sb = lambda name, shape, dt=F32: ctx.enter_context(nc.sbuf_tensor(f"m_{name}", shape, dt))
        ps = lambda name: ctx.enter_context(nc.psum_tensor(f"mp_{name}", [P, 512], F32))
        sem = lambda name: ctx.enter_context(nc.semaphore(f"m_{name}"))
        wp = sb("wp", [P, pack_width(PACK_MOE)])
        w = pack_views(wp, PACK_MOE)
        adj = sb("adj", [P, NT, BLK])
        near, hT, ohT = sb("near", [P, BLK]), sb("hT", [P, BLK]), sb("ohT", [ME, BLK])
        ohT16, rep16 = sb("ohT16", [ME, BLK], BF16), sb("rep16", [ME, ME * MH], BF16)
        x3, h, cen, sq, out_tile = (sb(n, [P, QT, D]) for n in ("x3", "h", "cen", "sq", "out"))
        st, spare = sb("st", [P, 2, QT]), sb("spare", [1, 1])
        logits, onehot = sb("logits", [P, QT, ME]), sb("onehot", [P, QT, ME])
        top, where, expert = sb("top", [P, QT, 8]), sb("where", [P, QT, 8], U32), sb("expert", [P, QT])
        hid, hsel = sb("hid", [P, EC, BLK]), sb("hsel", [P, EC, BLK])
        ps_near, ps_turn, ps_logits, ps_out = ps("near"), ps("turn"), ps("logits"), ps("out")
        ps_hid, ps_sel = [ps(f"hid{i}") for i in range(2)], [ps(f"sel{i}") for i in range(2)]
        pack_landed = sem("pack_landed")
        adj_landed = [sem(f"adj_landed{i}") for i in range(len(PIECES))]
        (adj_used, near_copied, near_turned, links, var_ready, std_ready, h_ready, h_turned, hT_ready,
         logits_ready, logits_read, onehot_ready, onehot_turned, ohT_ready, rep_ready, hid_ready, hid_relu,
         sel_ready, hid_chosen, out_ready, out_added, out_stored) = (sem(n) for n in (
            "adj_used", "near_copied", "near_turned", "links", "var_ready", "std_ready", "h_ready", "h_turned",
            "hT_ready", "logits_ready", "logits_read", "onehot_ready", "onehot_turned", "ohT_ready", "rep_ready",
            "hid_ready", "hid_relu", "sel_ready", "hid_chosen", "out_ready", "out_added", "out_stored"))
        LINKS = 11
        block = ctx.enter_context(nc.Block())

        def run(eng, step):
            step((0, QT), None, None)
            step((1, QT), (0, QT), None)
            step((2, QT), (1, QT), (0, QT))
            with eng.Fori(3, NB) as b:
                step((b, QT), (b - 1, QT), (b - 2, QT))
            step((NB, LT), (NB - 1, QT), (NB - 2, QT))
            step(None, (NB, LT), (NB - 1, QT))
            step(None, None, (NB, LT))

        @block.sync
        def _(sp):
            sp.dma_start(wp[:], pack_in).then_inc(pack_landed, 16)

            def step(products, choice, final):
                if products:
                    b, nt = products
                    src = adj_last if isinstance(b, int) and b == NB else (
                        adj_main[bass.ds(b, 1)].rearrange("o p k m -> (o p) k m"))
                    for i, (k0, k1) in enumerate(PIECES):
                        wait(sp, adj_used, len(PIECES) * (b - 1) + i + 1)
                        sp.dma_start(adj[:, k0:k1, 0:nt * P], src[:, k0:k1, :]).then_inc(adj_landed[i], 16)
                if final:
                    b, nt = final
                    sp.wait_ge(out_added, b + 1)
                    sp.dma_start(out.rearrange("(t p) d -> p t d", p=P)[:, bass.ds(b * QT, nt), :],
                                 out_tile[:, 0:nt, :]).then_inc(out_stored, 16)

            run(sp, step)
            sp.wait_ge(out_stored, 16 * (NB + 1))

        @block.vector
        def _(dve):
            dve.wait_ge(pack_landed, 16)
            dve.tensor_copy(rep16[:], w["rep"]).then_inc(rep_ready, 1)

            def choose(b, nt):
                link = Links(dve, links, b * LINKS, spare[:])
                tiles = slice(0, nt)
                rows = bass.ds(b * QT, nt)
                stat = (st[:, 0, tiles], st[:, 1, tiles])
                shape = [P, nt, D]
                dve.wait_ge(near_turned, b + 1)
                link(dve.tensor_tensor(x3[:, tiles, :], ps_turn[:, 0:nt * D].rearrange("p (t d) -> p t d", d=D),
                                       nb[:, rows, :], ALU.add))
                link(dve.scalar_tensor_tensor(x3[:, tiles, :], x3[:, tiles, :], 0.0, xres[:, rows, :],
                                              ALU.max, ALU.add))
                layernorm_head(dve, link, x3[:, tiles, :], cen[:, tiles, :], sq[:, tiles, :], stat, D, LN_EPS, var_ready)
                dve.wait_ge(std_ready, b + 1)
                rstd = layernorm_tail(dve, link, cen, stat, shape)
                dve.tensor_tensor(h[:, tiles, :], cen[:, tiles, :], rstd, ALU.mult).then_inc(h_ready, 1)
                dve.wait_ge(logits_ready, b + 1)
                dve.tensor_copy(logits[:, tiles, :], ps_logits[:, 0:nt * ME].rearrange("p (t e) -> p t e", e=ME))\
                    .then_inc(logits_read, 1)
                dve.wait_ge(logits_read, b + 1)
                link.apart()
                for j in range(nt):
                    last = dve.max(top[:, j, :], logits[:, j, :])
                link(last, apart=True)
                for j in range(nt):
                    last = dve.max_index(where[:, j, :], top[:, j, :], logits[:, j, :])
                link(last)
                link(dve.tensor_copy(expert[:, tiles], where[:, tiles, 0]))
                for j in range(nt):
                    ins = dve.tensor_scalar(onehot[:, j, :], w["iota"], expert[:, j:j + 1], None, ALU.is_equal)
                link(ins)
                dve.nop().then_inc(onehot_ready, 1)
                for c in range(EC):
                    dve.wait_ge(hid_relu, b * EC + c + 1)
                    dve.wait_ge(sel_ready, b * EC + c + 1)
                    dve.tensor_tensor(hsel[:, c, 0:nt * P], ps_sel[c % 2][:, 0:nt * P], hid[:, c, 0:nt * P],
                                      ALU.mult).then_inc(hid_chosen, 1)
                assert link.n == LINKS, link.n

            def finish(b, nt):
                dve.wait_ge(out_ready, b + 1)
                wait(dve, out_stored, 16 * b)
                dve.scalar_tensor_tensor(out_tile[:, 0:nt, :], ps_out[:, 0:nt * D].rearrange("p (t d) -> p t d", d=D),
                                         0.0, x3[:, 0:nt, :], ALU.max, ALU.add).then_inc(out_added, 1)
                dve.wait_ge(out_added, b + 1)

            def step(products, choice, final):
                if final:
                    finish(*final)
                if choice:
                    choose(*choice)

            run(dve, step)

        @block.scalar
        def _(act):
            def step(products, choice, final):
                if choice:
                    b, nt = choice
                    width = nt * P
                    act.wait_ge(var_ready, b + 1)
                    act.activation(st[:, 0, 0:nt], st[:, 1, 0:nt], ACT.Sqrt).then_inc(std_ready, 1)
                    act.wait_ge(h_turned, b + 1)
                    act.copy(hT[:, 0:width], ps_turn[:, 0:width]).then_inc(hT_ready, 1)
                    for c in range(EC):
                        act.wait_ge(hid_ready, b * EC + c + 1)
                        act.activation(hid[:, c, 0:width], ps_hid[c % 2][:, 0:width], ACT.Relu,
                                       bias=w["b1"][:, c:c + 1]).then_inc(hid_relu, 1)
                    act.wait_ge(onehot_turned, b + 1)
                    act.copy(ohT16[:, 0:width], ps_turn[0:ME, 0:width]).then_inc(ohT_ready, 1)
                    act.copy(ohT[:, 0:width], ps_turn[0:ME, 0:width]).then_inc(ohT_ready, 1)
                if products:
                    b, nt = products
                    act.wait_ge(adj_used, len(PIECES) * (b + 1))
                    act.copy(near[:, 0:nt * P], ps_near[:, 0:nt * P]).then_inc(near_copied, 1)

            act.wait_ge(pack_landed, 16)
            run(act, step)

        @block.tensor
        def _(pe):
            pe.wait_ge(pack_landed, 16)
            pe.wait_ge(rep_ready, 1)

            def columns(nt):
                return [slice(j * P, (j + 1) * P) for j in range(nt)]

            def near_rows(b, nt):
                pe.wait_ge(near_copied, b + 1)
                wait(pe, ohT_ready, 2 * b)
                for cols in columns(nt):
                    last = pe.matmul(ps_turn[:, cols], near[:, cols], w["ident"], start=True, stop=True)
                last.then_inc(near_turned, 1)

            def turn_h(b, nt):
                pe.wait_ge(h_ready, b + 1)
                for j, cols in enumerate(columns(nt)):
                    last = pe.matmul(ps_turn[:, cols], h[:, j, :], w["ident"], start=True, stop=True)
                last.then_inc(h_turned, 1)

            def route(b, nt):
                pe.wait_ge(hT_ready, b + 1)
                for j, cols in enumerate(columns(nt)):
                    to = ps_logits[:, j * ME:(j + 1) * ME]
                    pe.matmul(to, hT[:, cols], w["routerT"], start=True, stop=False)
                    last = pe.matmul(to, w["ones_row"], w["router_b"], start=False, stop=True)
                last.then_inc(logits_ready, 1)

            def hidden(b, nt, c):
                wait(pe, hid_relu, b * EC + c - 1)
                pe.matmul(ps_hid[c % 2][:, 0:nt * P], w["w1"][:, c * P:(c + 1) * P], hT[:, 0:nt * P],
                          start=True, stop=True).then_inc(hid_ready, 1)

            def turn_choice(b, nt):
                pe.wait_ge(onehot_ready, b + 1)
                for j, cols in enumerate(columns(nt)):
                    last = pe.matmul(ps_turn[0:ME, cols], onehot[:, j, :], w["ident"], start=True, stop=True)
                last.then_inc(onehot_turned, 1)

            def select(b, nt, c):
                if c == 0:
                    pe.wait_ge(ohT_ready, 2 * b + 1)
                wait(pe, hid_chosen, b * EC + c - 1)
                pe.matmul(ps_sel[c % 2][:, 0:nt * P], rep16[:, c * P:(c + 1) * P], ohT16[:, 0:nt * P],
                          start=True, stop=True).then_inc(sel_ready, 1)

            def expert_out(b, nt):
                pe.wait_ge(hid_chosen, (b + 1) * EC)
                pe.wait_ge(ohT_ready, 2 * b + 2)
                wait(pe, out_added, b)
                for cols in columns(nt):
                    for c in range(EC):
                        pe.matmul(ps_out[:, cols], hsel[:, c, cols], w["w2"][:, c * D:(c + 1) * D], start=(c == 0), stop=False)
                    last = pe.matmul(ps_out[:, cols], ohT[:, cols], w["b2"], start=False, stop=True)
                last.then_inc(out_ready, 1)

            def adj_products(products, first, last):
                if not products:
                    return
                b, nt = products
                for i, (k0, k1) in enumerate(PIECES):
                    for k in range(max(k0, first), min(k1, last)):
                        if k == k0:
                            pe.wait_ge(adj_landed[i], 16 * (b + 1))
                        if k == 0:
                            wait(pe, near_copied, b)
                        ins = pe.matmul(ps_near[:, 0:nt * P], z[:, k, :], adj[:, k, 0:nt * P],
                                        start=(k == 0), stop=(k == NT - 1))
                        if k == k1 - 1:
                            ins.then_inc(adj_used, 1)

            def step(products, choice, final):
                if final:
                    expert_out(*final)
                if not choice:
                    adj_products(products, 0, NT)
                    return
                near_rows(*choice)
                adj_products(products, 0, 8)
                turn_h(*choice)
                adj_products(products, 8, 10)
                route(*choice)
                for c in range(EC):
                    hidden(*choice, c)
                    if c > 0:
                        adj_products(products, 9 + c, 10 + c)
                turn_choice(*choice)
                adj_products(products, 17, 19)
                for c in range(EC):
                    select(*choice, c)
                    if c > 0:
                        adj_products(products, 17 + c + 1, 17 + c + 2)
                adj_products(products, 26, NT)

            run(pe, step)


def model_program(nc, x_in, adj_main, adj_last, pack_gnn0, pack_att, pack_post, pack_moe, o_scratch, out):
    with ExitStack() as ctx:
        rows = lambda ctx, name, width=D: ctx.enter_context(nc.sbuf_tensor(name, [P, NT, width], F32))
        xres = rows(ctx, "xres")
        z = rows(ctx, "z")
        nb = rows(ctx, "nb")
        with ExitStack() as middle:
            sxT = middle.enter_context(nc.sbuf_tensor("sxT", [P, NP], F32))
            rsum = rows(middle, "rsum", NH * NE)
            with ExitStack() as inner:
                kst = inner.enter_context(nc.sbuf_tensor("kst", [P, NH, NP], F32R))
                gnn0_program(nc, x_in, adj_main, adj_last, pack_gnn0, xres, z, sxT, kst, nb)
                attention_program(nc, pack_att, sxT, kst, nb, rsum, o_scratch)
            post_program(nc, pack_post, o_scratch, xres, sxT, rsum, z, nb)
        moe_program(nc, adj_main, adj_last, pack_moe, out, xres, z, nb)


def pack_weights(np, pack, arrays):
    packed, at = np.zeros((P, pack_width(pack)), np.float32), 0
    for name, rows, cols in pack:
        packed[0:rows, at:at + cols] = arrays[name]
        at += cols
    return packed


def kernel(**inputs):
    import numpy as np
    import concourse.bacc as bacc
    from concourse.bass_utils import run_bass_kernel_spmd

    a = {name: np.asarray(value) for name, value in inputs.items()}
    f = lambda name: a["L0_ffn_" + name]

    x = np.zeros((NP, D), np.float32)
    x[:N] = a["x"]
    adjT = np.zeros((NP, NP), np.float32)
    adjT[:N, :N] = a["adj"].T
    adjT = adjT.reshape(NT, P, NP).transpose(1, 0, 2)
    adj_main = np.ascontiguousarray(
        adjT[:, :, :NB * BLK].reshape(P, NT, NB, BLK).transpose(2, 0, 1, 3))
    adj_last = np.ascontiguousarray(adjT[:, :, NB * BLK:])

    wk = np.zeros((P, NH, P), np.float32)
    wq = np.zeros((P, NH, NE, P), np.float32)
    wv = np.zeros((P, NH * HD), np.float32)
    rep = np.zeros((P, NH, NE, HD), np.float32)
    gate_w = np.zeros((P, NH, NE, NE), np.float32)
    fc1, fc2 = np.zeros((P, D), np.float32), np.zeros((P, D), np.float32)
    for n in range(NH):
        rows = slice(n * HD, (n + 1) * HD)
        for part in range(1, 4):
            cols = slice(part * HD, (part + 1) * HD)
            wk[rows, n, cols] = f("wk")[n].T
            for e in range(NE):
                wq[rows, n, e, cols] = f("wq")[n, e].T
        wv[rows, rows] = f("wv")[n].T
        fc1[rows, rows] = f("fc1_w").T
        fc2[rows, rows] = f("fc2_w").T
        for e in range(NE):
            gate_w[e * HD:(e + 1) * HD, n, :, e] = f("gate_w")[n][:, e * HD:(e + 1) * HD].T
            rep[rows, n, e, :] = np.eye(HD, dtype=np.float32)
    ident = np.eye(P, dtype=np.float32)
    after = np.triu(np.ones((P, P), np.float32), 1) * np.float32(MASKED)
    sel = np.repeat(np.eye(16, dtype=np.float32), 2, axis=0)
    ones_row = np.ones((1, P), np.float32)
    ones_rows = np.zeros((P, 1), np.float32)
    ones_rows[:32] = 1.0
    first_row = np.zeros((P, 1), np.float32)
    first_row[::HD] = 1.0
    spread = lambda v: np.broadcast_to(v.reshape(1, -1), (P, v.size))
    weight = a["L0_gnn_weight"]
    pack_gnn0 = pack_weights(np, PACK_GNN0, dict(
        ident=ident, w_self=weight[:D], w_near=weight[D:], bias=a["L0_gnn_bias"].reshape(1, D), ones_row=ones_row,
        ones_rows=ones_rows, hl_wT=f("hl_w").reshape(NH * HD, D).T, hl_b=f("hl_b").reshape(P, 1),
        wk=wk.reshape(P, -1), wv=wv))
    pack_att = pack_weights(np, PACK_ATT, dict(
        ident=ident, mask_rows=after, mask_cols=after.T, sel=sel, ones32=np.ones((P, 32), np.float32),
        wq=wq.reshape(P, -1), first_rows=np.repeat(np.eye(NE, dtype=np.float32), HD, axis=0) * first_row))
    pack_post = pack_weights(np, PACK_POST, dict(
        ident=ident, ones_row=ones_row, rep=rep.reshape(P, -1), gate_w=gate_w.reshape(P, -1), gate_b=spread(f("gate_b")),
        ln_g=spread(f("ln_g")), ln_b=spread(f("ln_b")), fnorm_g=spread(f("fnorm_g")), fnorm_b=spread(f("fnorm_b")),
        fc1=fc1, fc2=fc2, fc1_b=np.tile(f("fc1_b"), NH).reshape(1, D), fc2_b=np.tile(f("fc2_b"), NH).reshape(1, D),
        fgateT=f("fgate_w").T, node_w=a["L1_gnn_W1"], node_b=a["L1_gnn_b"],
        node_w2=a["L1_gnn_W2"].transpose(1, 0, 2).reshape(P, -1)))
    pack_moe = pack_weights(np, PACK_MOE, dict(
        ident=ident, ones_row=ones_row, routerT=a["L1_ffn_router_w"].T, router_b=a["L1_ffn_router_b"].reshape(1, ME),
        iota=spread(np.arange(ME, dtype=np.float32)), w1=a["L1_ffn_W1"].transpose(1, 0, 2).reshape(P, -1),
        b1=a["L1_ffn_b1"].reshape(EC, P).T, w2=a["L1_ffn_W2"].reshape(EC, P, D).transpose(1, 0, 2).reshape(P, -1),
        b2=a["L1_ffn_b2"], rep=np.repeat(np.eye(ME, dtype=np.float32), MH, axis=1)))

    arrays = dict(x_in=x, adj_main=adj_main, adj_last=adj_last, pack_gnn0=pack_gnn0, pack_att=pack_att,
                  pack_post=pack_post, pack_moe=pack_moe)
    nc = bacc.Bacc("TRN2", target_bir_lowering=False, num_devices=1)
    args = {name: nc.dram_tensor(name, v.shape, F32, kind="ExternalInput").ap() for name, v in arrays.items()}
    args["out"] = nc.dram_tensor("out", (NP, D), F32, kind="ExternalOutput").ap()
    o_scratch = nc.dram_tensor("o_scratch", (NB + 1, P, NH, BLK), F32, kind="Internal").ap()
    model_program(nc, o_scratch=o_scratch, **args)
    result = run_bass_kernel_spmd(nc, [arrays], core_ids=[0]).results[0]["out"]
    return result[:N]
```

```python
from contextlib import ExitStack

import concourse.bass as bass
from concourse import mybir

ALU = mybir.AluOpType
ACT = mybir.ActivationFunctionType
X = mybir.AxisListType.X
F32 = mybir.dt.float32
F32R = mybir.dt.float32r
BF16 = mybir.dt.bfloat16
U32 = mybir.dt.uint32

P = 128
N = 3327
NT = -(-N // P)
NP = NT * P
D = 128
QT = 4
BLK = QT * P
NB = NT // QT
LT = NT - NB * QT
NH, NE, HD = 4, 4, 32
NODE_K = 16
ME, MH = 32, 32
EC = ME * MH // P
PIECES = ((0, 7), (7, 13), (13, 20), (20, 26))
SCORE_SCALE = float(HD) ** 0.5
MASKED = -1e30
LN_EPS, HEAD_LN_EPS = 1e-5, 1e-8

PACK_GNN0 = (
    ("ident", P, P), ("w_self", P, D), ("w_near", P, D), ("bias", 1, D), ("ones_row", 1, P),
    ("hl_wT", P, D), ("hl_b", P, 1), ("wk", P, D), ("wv", P, D),
)
PACK_ATT = (
    ("ident", P, P), ("mask_rows", P, P), ("mask_cols", P, P), ("sel", P, 16), ("ones32", P, 32),
    ("wq", P, NH * P), ("first_rows", P, NE),
)
PACK_POST = (
    ("ident", P, P), ("ones_row", 1, P), ("rep", P, NH * P), ("gate_w", P, NH * NE * NE),
    ("gate_b", P, NH * NE), ("ln_g", P, HD), ("ln_b", P, HD), ("fnorm_g", P, HD), ("fnorm_b", P, HD),
    ("fc1", P, D), ("fc2", P, D), ("fc1_b", 1, D), ("fc2_b", 1, D), ("fgateT", P, NH),
    ("node_w", P, NODE_K), ("node_b", NODE_K, D), ("node_w2", P, NODE_K * D),
)
PACK_MOE = (
    ("ident", P, P), ("ones_row", 1, P), ("routerT", P, ME), ("router_b", 1, ME), ("iota", P, ME),
    ("w1", P, ME * MH), ("b1", P, EC), ("w2", P, EC * D), ("b2", ME, D), ("rep", ME, ME * MH),
)


def pack_width(pack):
    return sum(cols for _, _, cols in pack)


def pack_views(tile, pack):
    views, at = {}, 0
    for name, rows, cols in pack:
        views[name] = tile[0:rows, at:at + cols]
        at += cols
    return views


def wait(eng, sem, value):
    if not isinstance(value, int) or value > 0:
        eng.wait_ge(sem, value)


class Links:

    def __init__(self, eng, sem, start=0, spare=None):
        self.eng, self.sem, self.start, self.n, self.spare = eng, sem, start, 0, spare

    def __call__(self, ins, apart=False):
        self.n += 1
        ins.then_inc(self.sem, 1)
        self.eng.wait_ge(self.sem, self.start + self.n)
        if apart:
            self.apart()

    def apart(self):
        self.eng.memset(self.spare, 0.0)


def layernorm_head(dve, link, src, cen, sq, stat, width, eps, std_asked):
    shape = list(src.shape)
    s0, s1 = stat
    link(dve.tensor_reduce(s0, src, X, ALU.add))
    link(dve.scalar_tensor_tensor(cen, s0.unsqueeze(len(shape) - 1).to_broadcast(shape), -1.0 / width, src, ALU.mult, ALU.add))
    link(dve.tensor_tensor(sq, cen, cen, ALU.mult))
    link(dve.tensor_reduce(s1, sq, X, ALU.add))
    dve.tensor_scalar(s1, s1, 1.0 / width, eps, ALU.mult, ALU.add).then_inc(std_asked, 1)


def layernorm_tail(dve, link, cen, stat, shape):
    s0, s1 = stat
    link(dve.reciprocal(s1, s0))
    return s1.unsqueeze(len(shape) - 1).to_broadcast(shape)


def gnn0_program(nc, x_in, adj_main, adj_last, pack_in, xres, xn, sxT, kst, vals):
    with ExitStack() as ctx:
        sb = lambda name, shape, dt=F32: ctx.enter_context(nc.sbuf_tensor(f"g_{name}", shape, dt))
        ps = lambda name: ctx.enter_context(nc.psum_tensor(f"gp_{name}", [P, 512], F32))
        sem = lambda name: ctx.enter_context(nc.semaphore(f"g_{name}"))
        wp = sb("wp", [P, pack_width(PACK_GNN0)])
        w = pack_views(wp, PACK_GNN0)
        adj = sb("adj", [P, NT, BLK])
        FIRST = ((0, 7), (7, 13), (13, 20), (20, 26))
        cen, sq = sb("cen", [P, 7, D]), sb("sq", [P, 7, D])
        st, spare = sb("st", [P, 2, 7]), sb("spare", [1, 1])
        near, xnT, hT, sxb = sb("near", [P, BLK]), sb("xnT", [P, BLK]), sb("hT", [P, BLK]), sb("sxb", [P, BLK])
        xnb, h = sb("xnb", [P, QT, D]), sb("h", [P, QT, D])
        ps_near, ps_turn, ps_h, ps_v = ps("near"), ps("turn"), ps("h"), ps("v")
        ps_k = ps("k")
        x_landed, pack_landed = sem("x_landed"), sem("pack_landed")
        adj_landed = [sem(f"adj_landed{i}") for i in range(len(PIECES))]
        (adj_used, links, var_ready, std_ready, xn_ready, xn_staged, near_copied, xn_turned, xnT_copied, h_ready,
         x_updated, row_ready, row_turned, hT_ready, sx_summed, sx_ready, k_summed, k_high_ready, k_ready,
         v_summed, v_ready, ones_laid) = (sem(x) for x in (
            "adj_used", "links", "var_ready", "std_ready", "xn_ready", "xn_staged", "near_copied", "xn_turned",
            "xnT_copied", "h_ready", "x_updated", "row_ready", "row_turned", "hT_ready", "sx_summed", "sx_ready",
            "k_summed", "k_high_ready", "k_ready", "v_summed", "v_ready", "ones_laid"))
        LINKS = 5
        STARTS = 5 * len(FIRST)
        block = ctx.enter_context(nc.Block())

        def for_blocks(eng, body):
            body(0, QT)
            with eng.Fori(1, NB) as b:
                body(b, QT)
            body(NB, LT)

        @block.sync
        def _(sp):
            sp.dma_start(xres[:], x_in.rearrange("(t p) d -> p t d", p=P)).then_inc(x_landed, 16)
            sp.dma_start(wp[:], pack_in).then_inc(pack_landed, 16)

            def load(b, width, src):
                for i, (k0, k1) in enumerate(PIECES):
                    wait(sp, adj_used, len(PIECES) * (b - 1) + i + 1)
                    sp.dma_start(adj[:, k0:k1, 0:width], src[:, k0:k1, :]).then_inc(adj_landed[i], 16)

            load(0, BLK, adj_main[0])
            with sp.Fori(1, NB) as b:
                load(b, BLK, adj_main[bass.ds(b, 1)].rearrange("o p k m -> (o p) k m"))
            load(NB, LT * P, adj_last)

        @block.vector
        def _(dve):
            link = Links(dve, links)
            dve.wait_ge(x_landed, 16)
            for g, (t0, t1) in enumerate(FIRST):
                n = t1 - t0
                stat = (st[:, 0, 0:n], st[:, 1, 0:n])
                layernorm_head(dve, link, xres[:, t0:t1, :], cen[:, 0:n, :], sq[:, 0:n, :], stat, D, LN_EPS, var_ready)
                dve.wait_ge(std_ready, g + 1)
                rstd = layernorm_tail(dve, link, cen[:], stat, [P, n, D])
                dve.tensor_tensor(xn[:, t0:t1, :], cen[:, 0:n, :], rstd, ALU.mult).then_inc(xn_ready, 1)
                dve.wait_ge(xn_ready, g + 1)

            def body(b, nt):
                link = Links(dve, links, STARTS + b * LINKS)
                xb = xres[:, bass.ds(b * QT, nt), :]
                width = nt * P
                dve.wait_ge(h_ready, b + 1)
                dve.scalar_tensor_tensor(xb, ps_h[:, 0:width].rearrange("p (t d) -> p t d", d=D), 0.0, xb,
                                         ALU.max, ALU.add).then_inc(x_updated, 1)
                dve.wait_ge(x_updated, b + 1)
                dve.memset(spare[:], 0.0)
                stat = (st[:, 0, 0:nt], st[:, 1, 0:nt])
                layernorm_head(dve, link, xb, cen[:, 0:nt, :], sq[:, 0:nt, :], stat, D, LN_EPS, var_ready)
                dve.wait_ge(std_ready, len(FIRST) + b + 1)
                rstd = layernorm_tail(dve, link, cen[:], stat, [P, nt, D])
                dve.tensor_tensor(h[:, 0:nt, :], cen[:, 0:nt, :], rstd, ALU.mult).then_inc(row_ready, 1)
                for n in range(NH):
                    dve.wait_ge(k_high_ready, NH * b + n + 1)
                    block_cols = bass.ds(b * BLK, width)
                    dve.tensor_tensor(kst[HD:2 * HD, n, block_cols], ps_k[n * HD:(n + 1) * HD, 0:width],
                                      kst[0:HD, n, block_cols].bitcast(F32), ALU.subtract).then_inc(k_ready, 1)
                assert link.n == LINKS, link.n

            for_blocks(dve, body)

        @block.scalar
        def _(act):
            for g, (t0, t1) in enumerate(FIRST):
                act.wait_ge(var_ready, g + 1)
                act.activation(st[:, 0, 0:t1 - t0], st[:, 1, 0:t1 - t0], ACT.Sqrt).then_inc(std_ready, 1)

            def sums(b, nt):
                width = nt * P
                act.wait_ge(adj_used, len(PIECES) * (b + 1))
                wait(act, h_ready, b)
                act.copy(near[:, 0:width], ps_near[:, 0:width]).then_inc(near_copied, 1)
                act.wait_ge(xn_turned, b + 1)
                act.copy(xnT[:, 0:width], ps_v[:, 0:width]).then_inc(xnT_copied, 1)

            def keys(b, nt):
                width = nt * P
                act.wait_ge(var_ready, len(FIRST) + b + 1)
                act.activation(st[:, 0, 0:nt], st[:, 1, 0:nt], ACT.Sqrt).then_inc(std_ready, 1)
                act.wait_ge(row_turned, b + 1)
                act.copy(hT[:, 0:width], ps_turn[:, 0:width]).then_inc(hT_ready, 1)
                act.wait_ge(sx_summed, b + 1)
                act.activation(sxb[:, 0:width], ps_h[:, 0:width], ACT.Identity, bias=w["hl_b"]).then_inc(sx_ready, 1)
                act.wait_ge(sx_ready, 2 * b + 1)
                act.copy(sxT[:, bass.ds(b * BLK, width)], sxb[:, 0:width]).then_inc(sx_ready, 1)
                act.wait_ge(k_summed, b + 1)
                for n in range(NH):
                    for row in (0, 2 * HD):
                        last = act.copy(kst[row:row + HD, n, bass.ds(b * BLK, width)], ps_k[n * HD:(n + 1) * HD, 0:width])
                    last.then_inc(k_high_ready, 1)
                act.wait_ge(v_summed, b + 1)
                act.copy(vals[:, bass.ds(b * QT, nt), :], ps_v[:, 0:width].rearrange("p (t d) -> p t d", d=D))\
                    .then_inc(v_ready, 1)

            sums(0, QT)
            with act.Fori(1, NB) as b:
                keys(b - 1, QT)
                sums(b, QT)
            keys(NB - 1, QT)
            sums(NB, LT)
            keys(NB, LT)

        @block.gpsimd
        def _(pool):
            pool.memset(kst[3 * HD:, :, :].bitcast(mybir.dt.float32), 1.0).then_inc(ones_laid, 1)
            pool.wait_ge(ones_laid, 1)

            def stage(b, nt):
                pool.wait_ge(xn_ready, len(FIRST))
                wait(pool, xn_turned, b)
                pool.tensor_copy(xnb[:, 0:nt, :], xn[:, bass.ds(b * QT, nt), :]).then_inc(xn_staged, 1)

            for_blocks(pool, stage)

        @block.tensor
        def _(pe):
            pe.wait_ge(pack_landed, 16)

            def piece(b, nt, i):
                k0, k1 = PIECES[i]
                pe.wait_ge(adj_landed[i], 16 * (b + 1))
                pe.wait_ge(xn_ready, i + 1)
                if i == 0:
                    wait(pe, near_copied, b)
                for k in range(k0, k1):
                    last = pe.matmul(ps_near[:, 0:nt * P], xn[:, k, :], adj[:, k, 0:nt * P],
                                     start=(k == 0), stop=(k == NT - 1))
                last.then_inc(adj_used, 1)

            def turn_xn(b, nt):
                pe.wait_ge(xn_staged, b + 1)
                wait(pe, v_ready, b)
                for j in range(nt):
                    last = pe.matmul(ps_v[:, j * P:(j + 1) * P], xnb[:, j, :], w["ident"], start=True, stop=True)
                last.then_inc(xn_turned, 1)

            def layer(b, nt):
                pe.wait_ge(near_copied, b + 1)
                pe.wait_ge(xnT_copied, b + 1)
                wait(pe, sx_ready, 2 * b)
                for j in range(nt):
                    cols = slice(j * P, (j + 1) * P)
                    pe.matmul(ps_h[:, cols], xnT[:, cols], w["w_self"], start=True, stop=False)
                    pe.matmul(ps_h[:, cols], near[:, cols], w["w_near"], start=False, stop=False)
                    last = pe.matmul(ps_h[:, cols], w["ones_row"], w["bias"], start=False, stop=True)
                last.then_inc(h_ready, 1)

            def turn_row(b, nt):
                pe.wait_ge(row_ready, b + 1)
                for j in range(nt):
                    last = pe.matmul(ps_turn[:, j * P:(j + 1) * P], h[:, j, :], w["ident"], start=True, stop=True)
                last.then_inc(row_turned, 1)

            def project(b, nt):
                pe.wait_ge(hT_ready, b + 1)
                pe.wait_ge(x_updated, b + 1)
                pe.matmul(ps_h[:, 0:nt * P], w["hl_wT"], hT[:, 0:nt * P], start=True, stop=True).then_inc(sx_summed, 1)

            def keys(b, nt):
                pe.wait_ge(sx_ready, 2 * b + 1)
                wait(pe, k_ready, NH * b)
                pe.matmul(ps_k[:, 0:nt * P], w["wk"], sxb[:, 0:nt * P], start=True, stop=True).then_inc(k_summed, 1)
                for j in range(nt):
                    cols = slice(j * P, (j + 1) * P)
                    last = pe.matmul(ps_v[:, cols], sxb[:, cols], w["wv"], start=True, stop=True)
                last.then_inc(v_summed, 1)

            def sums_beside(b, nt, b0, nt0):
                piece(b, nt, 0)
                turn_row(b0, nt0)
                piece(b, nt, 1)
                project(b0, nt0)
                piece(b, nt, 2)
                keys(b0, nt0)
                piece(b, nt, 3)
                turn_xn(b, nt)
                layer(b, nt)

            for i in range(len(PIECES)):
                piece(0, QT, i)
            turn_xn(0, QT)
            layer(0, QT)
            with pe.Fori(1, NB) as b:
                sums_beside(b, QT, b - 1, QT)
            sums_beside(NB, LT, NB - 1, QT)
            turn_row(NB, LT)
            project(NB, LT)
            keys(NB, LT)


def attention_program(nc, pack_in, sxT, kst, vals, rsum, o_scratch, prefetch):
    with ExitStack() as ctx:
        sb = lambda name, shape, dt=F32: ctx.enter_context(nc.sbuf_tensor(f"a_{name}", shape, dt))
        sem = lambda name: ctx.enter_context(nc.semaphore(f"a_{name}"))
        wp = sb("wp", [P, pack_width(PACK_ATT)])
        w = pack_views(wp, PACK_ATT)
        ident16, mask_rows, mask_cols = (sb(n, [P, P], BF16) for n in ("ident16", "mask_rows16", "mask_cols16"))
        kstat, vstat = sb("kstat", [P, BLK], F32R), sb("vstat", [P, QT, HD])
        qst = [sb(f"qst{i}", [P, NE, BLK], F32R) for i in range(2)]
        probs = [sb(f"probs{i}", [P, NE, BLK]) for i in range(QT)]
        pair_sum = [sb(f"pair_sum{i}", [P, NE, BLK]) for i in range(2)]
        m, m_chunk, m2 = sb("m", [P, 16]), sb("m_chunk", [P, 16]), sb("m2", [P, 16, 2])
        spare, zeros = sb("spare", [1, 1]), sb("zeros", [P, BLK], BF16)
        nothing = sb("nothing", [P, 1])
        o_tile, l_tile = [sb(f"o_tile{i}", [P, BLK]) for i in range(2)], sb("l_tile", [P, BLK])

        ps_slot = [ctx.enter_context(nc.psum_tensor(f"ap_slot{i}", [P, 512], F32)) for i in range(2)]
        ps_score = [ctx.enter_context(nc.psum_tensor(f"ap_score{i}", [P, 2, 512], F32)) for i in range(2)]
        ps_o = ctx.enter_context(nc.psum_tensor("ap_o", [P, 512], F32))
        ps_l = ctx.enter_context(nc.psum_tensor("ap_l", [P, 512], F32))

        pack_landed, masks_ready, m_cleared = sem("pack_landed"), sem("masks_ready"), sem("m_cleared")
        slot_ready, slot_free, q_high_ready, chunk_merged, max_half, max_split = (
            sem(x) for x in ("slot_ready", "slot_free", "q_high_ready", "chunk_merged", "max_half", "max_split"))
        keys_staged, vals_staged, scores_ready, probs_ready, o_summed = (
            sem(x) for x in ("keys_staged", "vals_staged", "scores_ready", "probs_ready", "o_summed"))
        pair_added, l_summed = ([sem(f"{x}{i}") for i in range(2)] for x in ("pair_added", "l_summed"))
        shifted, q_repeated = sem("shifted"), sem("q_repeated")
        pair_cleared = sem("pair_cleared")
        o_copied, l_copied, o_stored = sem("o_copied"), sem("l_copied"), [sem(f"o_stored{i}") for i in range(2)]
        block = ctx.enter_context(nc.Block())

        def keys_before(b, nt, n):
            return 8 * b * (b + 1) + n * (QT * b + nt)

        def chunks_before(b, n):
            return 2 * b * (b + 1) + n * (b + 1)

        def diagonal_groups(nt):
            groups = []
            for j in range(nt):
                together = BLK // P // (j + 1)
                groups += [(j, e, together) for e in range(0, NE, together)]
            return groups

        def first_slot(b):
            diagonal = len(diagonal_groups(QT))
            if first(b):
                return Slot(diagonal + 3, (diagonal + 3) % 2)
            last = diagonal - len(diagonal_groups(LT)) + (QT - LT) * NE * NB if isinstance(b, int) and b == NB else 0
            return Slot(2 + diagonal + 32 * b * b + (4 * diagonal - 4) * b - last, diagonal % 2)

        class Slot:

            def __init__(self, at, odd):
                self.at, self.odd = at, odd

            def take(self):
                at, odd = self.at, self.odd
                self.at, self.odd = at + 1, 1 - odd
                return at, ps_slot[odd]

            def jump(self, at):
                self.at = at

        def first(b):
            return isinstance(b, int) and b == 0

        def following(b, nt, next_nt, n, far=1):
            if n + far < NH:
                return b, nt, n + far
            return (b + 1, next_nt, n + far - NH) if next_nt else None

        def preceding(b, nt, n):
            if n > 0:
                return b, nt, n - 1
            return None if first(b) else (b - 1, QT, NH - 1)

        def for_blocks(eng, body):
            body(0, QT, QT)
            with eng.Fori(1, NB - 1) as b:
                body(b, QT, QT)
            body(NB - 1, QT, LT)
            body(NB, LT, 0)

        @block.sync
        def _(sp):
            sp.dma_start(wp[:], pack_in).then_inc(pack_landed, 16)
            prefetch(sp)

            def body(b, nt, next_nt):
                for n in range(NH):
                    sp.wait_ge(o_copied, NH * b + n + 1)
                    sp.dma_start(o_scratch[bass.ds(b, 1), :, n, 0:nt * P].rearrange("o p s -> (o p) s"),
                                 o_tile[n % 2][:, 0:nt * P]).then_inc(o_stored[n % 2], 16)

            for_blocks(sp, body)
            for stored in o_stored:
                sp.wait_ge(stored, 16 * (NH // 2) * (NB + 1))

        @block.gpsimd
        def _(pool):
            def chunk(keys, chunk_at, tiles, diagonal, width):
                for g in range(2):
                    even, odd = 2 * g, 2 * g + 1
                    wait(pool, l_summed[g], chunk_at)
                    if even >= tiles:
                        pool.nop().then_inc(pair_added[g], 1)
                        continue
                    pool.wait_ge(probs_ready, 2 * (keys + odd) + 2)
                    first = odd * P if diagonal else 0
                    if diagonal:
                        alone = probs[even][:, :, even * P:odd * P]
                        pool.tensor_tensor(pair_sum[g][:, :, even * P:odd * P], alone, nothing[:].unsqueeze(2).to_broadcast([P, NE, P]), ALU.add)
                    pool.tensor_tensor(pair_sum[g][:, :, first:width], probs[even][:, :, first:width],
                                       probs[odd][:, :, first:width], ALU.add).then_inc(pair_added[g], 1)

            def body(b, nt, next_nt):
                for n in range(NH):
                    keys, chunks = keys_before(b, nt, n), chunks_before(b, n)
                    chunk(keys, chunks, nt, True, nt * P)
                    if not first(b):
                        with pool.Fori(0, b) as c:
                            chunk(keys + nt + QT * c, chunks + 1 + c, QT, False, nt * P)

            pool.wait_ge(masks_ready, 1)
            for_blocks(pool, body)

        @block.scalar
        def _(act):
            def stage_keys(n, first_tile, tiles, keys):
                wait(act, scores_ready, 2 * keys)
                act.copy(kstat[:, 0:tiles * P], kst[:, n, bass.ds(first_tile * P, tiles * P)]).then_inc(keys_staged, 1)

            def stage_values(n, first_tile, tiles, keys):
                wait(act, o_summed, keys)
                act.copy(vstat[:, 0:tiles, :], vals[:, bass.ds(first_tile, tiles), n * HD:(n + 1) * HD])\
                    .then_inc(vals_staged, 1)

            def queries(unit, slot):
                b, nt, n = unit
                s, to = slot.take()
                act.wait_ge(slot_ready, s + 1)
                for e in range(NE):
                    act.activation(qst[n % 2][0:HD, e, 0:nt * P], to[e * HD:(e + 1) * HD, 0:nt * P], ACT.Copy,
                                   scale=SCORE_SCALE).then_inc(q_high_ready, 1)
                act.wait_ge(q_high_ready, NE * (NH * b + n + 1))
                act.copy(qst[n % 2][HD:2 * HD, :, 0:nt * P], qst[n % 2][0:HD, :, 0:nt * P]).then_inc(q_repeated, 1)

            def copy_sums(unit):
                b, nt, n = unit
                act.wait_ge(l_summed[1], chunks_before(b, n + 1))
                act.copy(l_tile[:, 0:nt * P], ps_l[:, 0:nt * P]).then_inc(l_copied, 1)

            def chunk(n, first_tile, tiles, keys, chunk_at, diagonal, width, before):
                stage_values(n, first_tile, tiles, keys)
                for i in range(tiles):
                    wait(act, pair_added[i // 2], chunk_at)
                    for p in range(2):
                        act.wait_ge(scores_ready, 2 * (keys + i) + p + 1)
                        cols = slice(i * P if diagonal else 0, width)
                        act.activation(probs[i][:, 2 * p:2 * p + 2, cols], ps_score[p][:, :, cols], ACT.Exp)\
                            .then_inc(probs_ready, 1)
                    if i == min(2, tiles - 1) and before:
                        copy_sums(before)

            def body(b, nt, next_nt):
                slot = first_slot(b)
                width = nt * P
                for n in range(NH):
                    keys, chunks = keys_before(b, nt, n), chunks_before(b, n)
                    ahead, before = following(b, nt, next_nt, n), preceding(b, nt, n)
                    far = following(b, nt, next_nt, n, 2)
                    if ahead:
                        for _ in diagonal_groups(ahead[1]):
                            slot.take()
                        slot.jump(slot.at + NE * ahead[1] * ahead[0])
                    if before:
                        slot.take()
                    chunk(n, b * QT, nt, keys, chunks, True, width, before)
                    if not first(b):
                        with act.Fori(0, b) as c:
                            at = keys + nt + QT * c
                            stage_keys(n, c * QT, QT, at)
                            chunk(n, c * QT, QT, at, chunks + 1 + c, False, width, None)
                    if ahead:
                        stage_keys(ahead[2], ahead[0] * QT, ahead[1], keys_before(b, nt, n + 1))
                    act.wait_ge(o_summed, keys_before(b, nt, n + 1))
                    wait(act, o_stored[n % 2], 16 * (NH // 2 * b + n // 2))
                    act.copy(o_tile[n % 2][:, 0:width], ps_o[:, 0:width]).then_inc(o_copied, 1)
                    if far:
                        queries(far, slot)
                    if ahead:
                        slot.take()

            act.wait_ge(pack_landed, 16)
            queries((0, QT, 0), Slot(0, 0))
            after_maxima = 1 + len(diagonal_groups(QT))
            queries((0, QT, 1), Slot(after_maxima, after_maxima % 2))
            stage_keys(0, 0, QT, 0)
            for_blocks(act, body)
            copy_sums((NB, LT, NH - 1))

        @block.vector
        def _(dve):
            dve.memset(m[:], 0.0).then_inc(m_cleared, 1)
            dve.memset(nothing[:], 0.0).then_inc(masks_ready, 1)
            dve.memset(zeros[:], 0.0).then_inc(masks_ready, 1)
            dve.memset(m_chunk[:], 0.0).then_inc(chunk_merged, 1)
            dve.wait_ge(m_cleared, 1)
            dve.wait_ge(pack_landed, 16)
            for to, src in ((ident16, "ident"), (mask_rows, "mask_rows"), (mask_cols, "mask_cols")):
                dve.tensor_copy(to[:], w[src]).then_inc(masks_ready, 1)

            def queries(unit, at, frees):
                b, nt, n = unit
                for e in range(NE):
                    if e == 0:
                        dve.wait_ge(q_high_ready, NE * (NH * b + n + 1))
                    last = dve.scalar_tensor_tensor(qst[n % 2][2 * HD:3 * HD, e, 0:nt * P], at[e * HD:(e + 1) * HD, 0:nt * P],
                                                    SCORE_SCALE, qst[n % 2][0:HD, e, 0:nt * P].bitcast(F32),
                                                    ALU.mult, ALU.subtract)
                last.then_inc(slot_free, frees)

            def maxima(slot, to, groups, width=None):
                for j, e, together in groups:
                    s, at = slot.take()
                    keys = width or (j + 1) * P
                    dve.wait_ge(slot_ready, s + 1)
                    dve.tensor_reduce(to[:].rearrange("p (e j) -> p e j", j=QT)[:, e:e + together, j],
                                      at[:, 0:together * keys].rearrange("p (e s) -> p e s", s=keys), X, ALU.max)\
                        .then_inc(slot_free, 1)

            def diagonal_maxima(unit, slot):
                b, nt, n = unit
                wait(dve, max_split, NH * b + n)
                maxima(slot, m, diagonal_groups(nt))

            def chunk_maxima(unit, slot, c):
                b, nt, n = unit
                dve.wait_ge(chunk_merged, 2 * b * (b - 1) + n * b + 1 + c)
                maxima(slot, m_chunk, [(j, e, 1) for j in range(nt) for e in range(NE)], BLK)
                dve.wait_ge(slot_free, slot.at)
                dve.tensor_tensor(m[:], m[:], m_chunk[:], ALU.max).then_inc(chunk_merged, 1)

            def shift(unit, slot, far):
                b, nt, n = unit
                dve.wait_ge(slot_free, slot.at)
                wait(dve, chunk_merged, 2 * b * (b - 1) + (n + 1) * b + 1)
                dve.tensor_scalar(m2[:, :, 0].bitcast(F32R), m[:], -1.0, None, ALU.mult).then_inc(max_half, 1)
                dve.wait_ge(max_half, NH * b + n + 1)
                dve.scalar_tensor_tensor(m2[:, :, 1], m[:], -1.0, m2[:, :, 0], ALU.mult, ALU.subtract)\
                    .then_inc(max_split, 1)
                far_at = slot.take()[1] if far else None
                s, at = slot.take()
                dve.wait_ge(slot_ready, s + 1)
                shape = [HD, 2, nt, P]
                for pair in (slice(0, 2), slice(2, 4)):
                    rows = qst[n % 2][3 * HD:, pair, 0:nt * P].rearrange("r e (j s) -> r e j s", s=P)
                    mine = w["sel"][3 * HD:].rearrange("r (e j) -> r e j", j=QT)[:, pair, 0:nt].unsqueeze(3).to_broadcast(shape)
                    dve.tensor_tensor(rows, at[3 * HD:, 0:P].unsqueeze(1).unsqueeze(1).to_broadcast(shape), mine,
                                      ALU.mult).then_inc(shifted, 1)
                if far:
                    queries(far, far_at, 2)
                else:
                    dve.wait_ge(shifted, 2 * (NH * b + n + 1))
                    dve.nop().then_inc(slot_free, 1)

            def invert_sums(unit, slot):
                b, nt, n = unit
                s, at = slot.take()
                dve.wait_ge(slot_ready, s + 1)
                if not isinstance(b, int):
                    dve.memset(spare[:], 0.0)
                dve.reciprocal(rsum[:, bass.ds(b * QT, nt), n * NE:(n + 1) * NE],
                               at[:, 0:nt * NE].rearrange("p (t e) -> p t e", e=NE)).then_inc(slot_free, 1)

            def clear(b, nt, n):
                wait(dve, l_summed[1], chunks_before(b, n))
                dve.memset(pair_sum[1][:, :, 0:2 * P], 0.0).then_inc(pair_cleared, 1)

            def body(b, nt, next_nt):
                slot = first_slot(b)
                for n in range(NH):
                    ahead, before = following(b, nt, next_nt, n), preceding(b, nt, n)
                    if ahead:
                        diagonal_maxima(ahead, slot)
                        if ahead[2] == 0:
                            chunk_maxima(ahead, slot, 0)
                    clear(b, nt, n)
                    if before:
                        invert_sums(before, slot)
                    if ahead and not first(b):
                        start = slot.at
                        with dve.Fori(0, b) as c:
                            slot.jump(start + NE * ahead[1] * c)
                            at_chunk = c if ahead[2] else c + 1
                            chunk_maxima(ahead, slot, at_chunk)
                        slot.jump(start + NE * ahead[1] * b)
                    if ahead:
                        shift(ahead, slot, following(b, nt, next_nt, n, 2))
                return slot

            slot = Slot(0, 0)
            queries((0, QT, 0), slot.take()[1], 1)
            diagonal_maxima((0, QT, 0), slot)
            shift((0, QT, 0), slot, (0, QT, 1))
            ends = []
            for_blocks(dve, lambda *block: ends.append(body(*block)))
            invert_sums((NB, LT, NH - 1), ends[-1])

        @block.tensor
        def _(pe):
            pe.wait_ge(pack_landed, 16)
            pe.wait_ge(masks_ready, 5)

            def queries(unit, slot):
                b, nt, n = unit
                s, to = slot.take()
                wait(pe, slot_free, s - 1)
                pe.matmul(to[:, 0:nt * P], w["wq"][:, n * P:(n + 1) * P], sxT[:, bass.ds(b * BLK, nt * P)],
                          start=True, stop=True).then_inc(slot_ready, 1)

            def for_max(unit, slot, j, first_e, together, c):
                b, nt, n = unit
                s, to = slot.take()
                wait(pe, slot_free, s - 1)
                diagonal = c is None
                width = (j + 1) * P if diagonal else BLK
                for i in range(together):
                    at = i * width
                    last = pe.matmul(to[:, at:at + width], qst[n % 2][0:3 * HD, first_e + i, j * P:(j + 1) * P],
                                     kst[0:3 * HD, n, bass.ds((b if diagonal else c) * BLK, width)], start=True, stop=True)
                    if diagonal:
                        last = pe.matmul(to[:, at + width - P:at + width], ident16[:], mask_rows[:], start=False,
                                         stop=True, skip_group_check=True)
                last.then_inc(slot_ready, 1)

            def scores(n, keys, i, p, cols, diagonal):
                wait(pe, probs_ready, 2 * (keys + i - 1) + p + 1)
                for e in range(2):
                    last = pe.matmul(ps_score[p][:, e, cols], kstat[:, i * P:(i + 1) * P],
                                     qst[n % 2][:, 2 * p + e, cols], start=True, stop=True)
                    if diagonal:
                        last = pe.matmul(ps_score[p][:, e, cols.start:cols.start + P], ident16[:], mask_cols[:],
                                         start=False, stop=True, skip_group_check=True)
                last.then_inc(scores_ready, 1)

            def outputs(keys, i, cols, start):
                pe.wait_ge(probs_ready, 2 * (keys + i) + 2)
                for e in range(NE):
                    last = pe.matmul(ps_o[e * HD:(e + 1) * HD, cols], vstat[:, i, :], probs[i][:, e, cols],
                                     start=start, stop=True, skip_group_check=True)
                last.then_inc(o_summed, 1)

            def sums(g, chunks, unit):
                b, nt, n = unit
                pe.wait_ge(pair_added[g], chunks)
                if g == 1:
                    pe.wait_ge(pair_cleared, NH * b + n + 1)
                for e in range(NE):
                    last = pe.matmul(ps_l[e * HD:(e + 1) * HD, 0:nt * P], w["ones32"], pair_sum[g][:, e, 0:nt * P],
                                     start=False, stop=True, skip_group_check=True)
                last.then_inc(l_summed[g], 1)

            def zero_sums():
                pe.matmul(ps_l[:], zeros[:, 0:P], zeros[:], start=True, stop=True, skip_group_check=True)

            def turn_sums(unit, slot):
                b, nt, n = unit
                s, to = slot.take()
                wait(pe, slot_free, s - 1)
                pe.wait_ge(l_copied, NH * b + n + 1)
                for j in range(nt):
                    last = pe.matmul(to[:, j * NE:(j + 1) * NE], l_tile[:, j * P:(j + 1) * P], w["first_rows"],
                                     start=True, stop=True)
                last.then_inc(slot_ready, 1)

            def chunk(unit, slot, ahead, maxima, before, keys, chunk_at, tiles, diagonal, queries_at=None):
                b, nt, n = unit
                width = nt * P
                cols = [slice(i * P if diagonal else 0, width) for i in range(tiles)]
                asks = diagonal and ahead is not None
                per = -(-len(maxima) // (tiles - asks))
                left, places = list(maxima), 0

                def some_maxima(share=1, last=False):
                    nonlocal places
                    places += share
                    if diagonal:
                        done = at * per + (per if last else per // 4 * (places - tile_places))
                    else:
                        done = places * len(maxima) // 16
                    count = max(0, done - (len(maxima) - len(left)))
                    for one in left[:count]:
                        for_max(ahead, slot, *one)
                    del left[:count]

                pe.wait_ge(keys_staged, chunk_at + 1)
                for i in range(tiles):
                    at, tile_places = i - asks, places
                    if diagonal and i == 0:
                        pe.wait_ge(shifted, 2 * (NH * b + n) + 1)
                    scores(n, keys, i, 0, cols[i], diagonal)
                    if i == 1 and asks:
                        pe.wait_ge(slot_free, queries_at)
                        pe.wait_ge(q_repeated, NH * ahead[0] + ahead[2] + 1)
                    if at >= 0:
                        some_maxima()
                    if diagonal and i == 0:
                        pe.wait_ge(shifted, 2 * (NH * b + n) + 2)
                    scores(n, keys, i, 1, cols[i], diagonal)
                    if at >= 0:
                        some_maxima()
                    if i == 0 and (before or not diagonal):
                        sums(0, chunk_at, before or unit)
                    if i == min(2, tiles - 1) and (before or not diagonal):
                        sums(1, chunk_at, before or unit)
                    if at >= 0 and (diagonal or i == 2):
                        some_maxima(1 if diagonal else 2)
                    if i == 1:
                        pe.wait_ge(vals_staged, chunk_at + 1)
                        if diagonal:
                            wait(pe, o_copied, NH * b + n)
                    if i > 0:
                        outputs(keys, i - 1, cols[i - 1], diagonal and i == 1)
                    if at >= 0:
                        some_maxima(2 if i == tiles - 1 else 1, last=True)
                outputs(keys, tiles - 1, cols[tiles - 1], diagonal and tiles == 1)
                if not diagonal:
                    some_maxima()
                assert not left
                if diagonal:
                    if before:
                        turn_sums(before, slot)
                    zero_sums()

            def turn_max(unit, slot):
                b, nt, n = unit
                s, to = slot.take()
                pe.wait_ge(max_split, NH * b + n + 1)
                wait(pe, slot_free, s - 1)
                pe.matmul(to[3 * HD:, 0:P], m2[:].rearrange("p g h -> p (g h)"), w["ident"], start=True, stop=True)\
                    .then_inc(slot_ready, 1)

            def body(b, nt, next_nt):
                slot = first_slot(b)
                for n in range(NH):
                    unit = (b, nt, n)
                    keys, chunks = keys_before(b, nt, n), chunks_before(b, n)
                    ahead, before = following(b, nt, next_nt, n), preceding(b, nt, n)
                    each, diagonal, queries_at = [], [], slot.at
                    if ahead:
                        each = [(j, e, 1) for j in range(ahead[1]) for e in range(NE)]
                        diagonal = [(*group, None) for group in diagonal_groups(ahead[1])]
                        if ahead[2] == 0:
                            diagonal += [(*one, b) for one in each]
                    chunk(unit, slot, ahead, diagonal, before, keys, chunks, nt, True, queries_at)
                    if not first(b):
                        start = slot.at
                        with pe.Fori(0, b) as c:
                            slot.jump(start + len(each) * c)
                            chunk(unit, slot, ahead, [(*one, c) for one in each], None,
                                  keys + nt + QT * c, chunks + 1 + c, QT, False)
                        slot.jump(start + len(each) * b)
                    far = following(b, nt, next_nt, n, 2)
                    if far:
                        queries(far, slot)
                    if ahead:
                        turn_max(ahead, slot)
                return slot

            slot, unit = Slot(0, 0), (0, QT, 0)
            queries(unit, slot)
            pe.wait_ge(slot_free, slot.at)
            pe.wait_ge(q_repeated, 1)
            for group in diagonal_groups(QT):
                for_max(unit, slot, *group, None)
            queries((0, QT, 1), slot)
            turn_max(unit, slot)
            ends = []
            for_blocks(pe, lambda *block: ends.append(body(*block)))
            last = (NB, LT, NH - 1)
            for g in range(2):
                sums(g, chunks_before(NB, NH), last)
            turn_sums(last, ends[-1])


def post_program(nc, pack_landed, wp, o_scratch, xres, sxT, rsum, z, nb, prefetch):
    with ExitStack() as ctx:
        sb = lambda name, shape, dt=F32: ctx.enter_context(nc.sbuf_tensor(f"p_{name}", shape, dt))
        ps = lambda name: ctx.enter_context(nc.psum_tensor(f"pp_{name}", [P, 512], F32))
        sem = lambda name: ctx.enter_context(nc.semaphore(f"p_{name}"))
        w = pack_views(wp, PACK_POST)
        o_in, onT = sb("o_in", [P, NH, BLK]), sb("onT", [P, NH, BLK])
        sxb, turnT, hT, nodeT = sb("sxb", [P, BLK]), sb("turnT", [P, BLK]), sb("hT", [P, BLK]), sb("nodeT", [NODE_K, BLK])
        h, cen, sq = (sb(n, [P, QT, D]) for n in ("h", "cen", "sq"))
        fh, fcen, fsq, relu, nz, row = (sb(n, [P, QT, D]) for n in ("fh", "fcen", "fsq", "relu", "nz", "row"))
        st, fst = sb("st", [P, 2, QT * NH]), sb("fst", [P, 2, QT * NH])
        gate_terms = sb("gate_terms", [P, QT * NH, NE, NE])
        gate, gtop, gsum = sb("gate", [P, QT * NH, NE]), sb("gtop", [P, QT * NH]), sb("gsum", [P, QT * NH])
        fgate, fgtop, fgsum = sb("fgate", [P, QT, NH]), sb("fgtop", [P, QT]), sb("fgsum", [P, QT])
        prod, zprod = sb("prod", [P, QT, 512]), [sb(f"zprod{i}", [P, NODE_K * D]) for i in range(2)]
        node, spare = sb("node", [P, QT, NODE_K]), sb("spare", [1, 1])
        bank, ps_turn, ps_out, ps_z = [ps(f"bank{i}") for i in range(4)], ps("turn"), ps("out"), [ps(f"z{i}") for i in range(2)]

        links, flinks, z_links = sem("links"), sem("flinks"), sem("z_links")
        (o_landed, sx_staged, sx_spread, masked, gates_ready, gates_read, outs_ready, out0_mixed, sx_turned,
         exp_asked, exp_ready, fexp_asked, fexp_ready, var_ready, std_ready, fvar_ready, fstd_ready, mixed,
         row_ready, turned, turn_copied, fc_ready, fgate_ready, node_ready, nodeT_ready,
         node_copied, nb_ready, nb_copied, z_ready, z_scaled, z_summed) = (sem(x) for x in (
            "o_landed", "sx_staged", "sx_spread", "masked", "gates_ready", "gates_read", "outs_ready", "out0_mixed",
            "sx_turned", "exp_asked", "exp_ready", "fexp_asked", "fexp_ready", "var_ready", "std_ready",
            "fvar_ready", "fstd_ready", "mixed", "row_ready", "turned", "turn_copied", "fc_ready", "fgate_ready",
            "node_ready", "nodeT_ready", "node_copied", "nb_ready", "nb_copied", "z_ready", "z_scaled", "z_summed"))
        block = ctx.enter_context(nc.Block())

        LINKS, FLINKS = 17, 21

        def row_view(tile, nt):
            return tile[:, 0:nt * P].rearrange("p (t d) -> p t d", d=D)

        def heads_view(tile, nt):
            return tile[:, 0:nt, :].rearrange("p t (n d) -> p (t n) d", d=HD)

        def run(eng, step):
            step(None, None, None, (0, QT))
            step((0, QT), None, None, (1, QT))
            step((1, QT), (0, QT), None, (2, QT))
            step((2, QT), (1, QT), (0, QT), (3, QT))
            with eng.Fori(3, NB - 1) as b:
                step((b, QT), (b - 1, QT), (b - 2, QT), (b + 1, QT))
            step((NB - 1, QT), (NB - 2, QT), (NB - 3, QT), (NB, LT))
            step((NB, LT), (NB - 1, QT), (NB - 2, QT), None)
            step(None, (NB, LT), (NB - 1, QT), None)
            step(None, None, (NB, LT), None)

        @block.sync
        def _(sp):
            def step(mix, ffn, zsum, ahead):
                if ahead:
                    b, nt = ahead
                    wait(sp, masked, NH * b)
                    sp.dma_start(o_in[:, :, 0:nt * P], o_scratch[bass.ds(b, 1), :, :, 0:nt * P].rearrange("o p n s -> (o p) n s"))\
                        .then_inc(o_landed, 16)

            run(sp, step)
            prefetch(sp)

        @block.gpsimd
        def _(pool):
            def sum_z(b, nt):
                for j in range(nt):
                    link = Links(pool, z_links, 3 * (QT * b + j))
                    terms = zprod[j % 2]
                    pool.wait_ge(z_scaled, 4 * (QT * b + j) + 4)
                    width = NODE_K * D // 2
                    while width > D:
                        link(pool.tensor_tensor(terms[:, 0:width], terms[:, 0:width], terms[:, width:2 * width], ALU.add))
                        width //= 2
                    pool.tensor_tensor(z[:, bass.ds(b * QT + j, 1), :].rearrange("p o f -> p (o f)"),
                                       terms[:, 0:D], terms[:, D:2 * D], ALU.add).then_inc(z_summed, 1)

            with pool.Fori(0, NB) as b:
                sum_z(b, QT)
            sum_z(NB, LT)

        @block.scalar
        def _(act):
            def scale_z(zsum, first, last):
                if not zsum:
                    return
                b, nt = zsum
                for s in range(first, min(last, 4 * nt)):
                    j, q = s // 4, s % 4
                    act.wait_ge(z_ready, 16 * b + s + 1)
                    if q == 0:
                        wait(act, z_summed, QT * b + j - 1)
                    for i in range(4):
                        k = 4 * q + i
                        last_one = act.activation(zprod[j % 2][:, k * D:(k + 1) * D], ps_z[q % 2][:, i * D:(i + 1) * D],
                                                  ACT.Identity, scale=node[:, j, k:k + 1])
                    last_one.then_inc(z_scaled, 1)

            def root(stat, count, asked, ready, value):
                act.wait_ge(asked, value)
                act.activation(stat[:, 0, 0:count], stat[:, 1, 0:count], ACT.Sqrt).then_inc(ready, 1)

            def turn(ffn, i, to):
                b, nt = ffn
                act.wait_ge(turned, 4 * b + i)
                act.copy(to[:, 0:nt * P], ps_turn[:, 0:nt * P]).then_inc(turn_copied, 1)

            def exponent(g, asked, ready, b):
                act.wait_ge(asked, b + 1)
                act.activation(g, g, ACT.Exp).then_inc(ready, 1)

            def step(mix, ffn, zsum, ahead):
                if zsum:
                    zb, znt = zsum
                    turn(zsum, 4, hT)
                    act.wait_ge(node_ready, zb + 1)
                    act.copy(nodeT[:, 0:znt * P], ps_out[0:NODE_K, 0:znt * P]).then_inc(nodeT_ready, 1)
                if ffn:
                    turn(ffn, 1, turnT)
                if zsum:
                    act.wait_ge(nb_ready, zb + 1)
                    act.copy(nb[:, bass.ds(zb * QT, znt), :], row_view(ps_out, znt)).then_inc(nb_copied, 1)
                    act.wait_ge(node_copied, zb + 1)
                if mix:
                    b, nt = mix
                    exponent(gate[:, 0:nt * NH, :], exp_asked, exp_ready, b)
                scale_z(zsum, 0, 2)
                if ffn:
                    fb, fnt = ffn
                    turn(ffn, 2, turnT)
                    scale_z(zsum, 2, 4)
                if ahead:
                    ab, ant = ahead
                    wait(act, sx_turned, ab)
                    act.copy(sxb[:, 0:ant * P], sxT[:, bass.ds(ab * BLK, ant * P)]).then_inc(sx_staged, 1)
                if ffn:
                    root(fst, fnt * NH, fvar_ready, fstd_ready, 2 * fb + 1)
                    scale_z(zsum, 4, 5)
                if mix:
                    root(st, nt * NH, var_ready, std_ready, b + 1)
                if ffn:
                    scale_z(zsum, 5, 9)
                    turn(ffn, 3, turnT)
                    scale_z(zsum, 9, 10)
                    exponent(fgate[:, 0:fnt, :], fexp_asked, fexp_ready, fb)
                    scale_z(zsum, 10, 14)
                    root(fst, fnt, fvar_ready, fstd_ready, 2 * fb + 2)
                    scale_z(zsum, 14, 16)
                if zsum and not ffn:
                    scale_z(zsum, 2, 16)

            act.wait_ge(pack_landed, 16)
            run(act, step)

        @block.vector
        def _(dve):
            dve.wait_ge(pack_landed, 16)

            def softmax_top(link, g, top, total, read, asked):
                shape = list(g.shape)
                link(read(g))
                link(dve.tensor_reduce(top, g, X, ALU.max))
                dve.tensor_tensor(g, g, top.unsqueeze(2).to_broadcast(shape), ALU.subtract).then_inc(asked, 1)

            def softmax_rest(link, g, total):
                link(dve.tensor_reduce(total, g, X, ALU.add))
                link(dve.reciprocal(total, total))
                link(dve.tensor_tensor(g, g, total.unsqueeze(2).to_broadcast(list(g.shape)), ALU.mult))

            def layernorm_rest(link, to, cen, stat, affine=None):
                shape = list(cen.shape)
                rstd = layernorm_tail(dve, link, cen, stat, shape)
                last = dve.tensor_tensor(to, cen, rstd, ALU.mult)
                if affine:
                    link(last)
                    link(dve.tensor_tensor(to, to, w[affine[0]].unsqueeze(1).to_broadcast(shape), ALU.mult))
                    last = dve.tensor_tensor(to, to, w[affine[1]].unsqueeze(1).to_broadcast(shape), ALU.add)
                return last

            class Mix:

                def __init__(self, b, nt):
                    self.b, self.nt, self.groups = b, nt, nt * NH
                    self.link = Links(dve, links, b * LINKS, spare[:])
                    self.g, self.total = gate[:, 0:self.groups, :], gsum[:, 0:self.groups]
                    self.rs = rsum[:, bass.ds(b * QT, nt), :].rearrange("p t (n e) -> p (t n) e", e=NE)
                    self.stat = (st[:, 0, 0:self.groups], st[:, 1, 0:self.groups])

                def mask(self):
                    b, width = self.b, self.nt * P
                    dve.wait_ge(o_landed, 16 * (b + 1))
                    for n in range(NH):
                        dve.wait_ge(sx_spread, NH * b + n + 1)
                        dve.scalar_tensor_tensor(onT[:, n, 0:width], bank[n][:, 0:width], 0.0, o_in[:, n, 0:width],
                                                 ALU.not_equal, ALU.mult).then_inc(masked, 1)

                def gates(self):
                    b, nt, groups, link = self.b, self.nt, self.groups, self.link
                    terms = gate_terms[:, 0:groups, :, :]
                    dve.wait_ge(gates_ready, b + 1)
                    dve.tensor_tensor(terms, bank[3][:, 0:groups * NE * NE].rearrange("p (g o e) -> p g o e", o=NE, e=NE),
                                      self.rs.unsqueeze(2).to_broadcast([P, groups, NE, NE]), ALU.mult).then_inc(gates_read, 1)
                    dve.wait_ge(gates_read, b + 1)
                    link.apart()
                    link(dve.tensor_reduce(self.g, terms, X, ALU.add))
                    gb = w["gate_b"].rearrange("p (n e) -> p n e", e=NE).unsqueeze(1).to_broadcast([P, nt, NH, NE])
                    with_heads = lambda g: g.rearrange("p (t n) e -> p t n e", n=NH)
                    softmax_top(link, self.g, gtop[:, 0:groups], self.total,
                                lambda g: dve.tensor_tensor(with_heads(g), with_heads(g), gb, ALU.add), exp_asked)

                def weights(self):
                    dve.wait_ge(exp_ready, self.b + 1)
                    softmax_rest(self.link, self.g, self.total)
                    self.link(dve.tensor_tensor(self.g, self.g, self.rs, ALU.mult))

                def mix(self):
                    b, nt, link = self.b, self.nt, self.link
                    dve.wait_ge(outs_ready, b + 1)
                    for j in range(nt):
                        shape = [P, NH * NE, HD]
                        gs = gate[:, j * NH:(j + 1) * NH, :].rearrange("p n e -> p (n e)").unsqueeze(2).to_broadcast(shape)
                        last = dve.tensor_tensor(prod[:, j, :].rearrange("p (g d) -> p g d", d=HD),
                                                 bank[j][:].rearrange("p (g d) -> p g d", d=HD), gs, ALU.mult)
                        if j == 0:
                            last.then_inc(out0_mixed, 1)
                    link(last)
                    self.hv = heads_view(h, nt)
                    link(dve.tensor_reduce(self.hv, prod[:, 0:nt, :].rearrange("p t (n e d) -> p (t n) d e", e=NE, d=HD),
                                           X, ALU.add))

                def layernorm_asked(self):
                    b, nt, link = self.b, self.nt, self.link
                    dve.wait_ge(sx_turned, b + 1)
                    dve.tensor_tensor(h[:, 0:nt, :], row_view(bank[0], nt), h[:, 0:nt, :], ALU.add).then_inc(mixed, 1)
                    dve.wait_ge(mixed, b + 1)
                    layernorm_head(dve, link, self.hv, heads_view(cen, nt), heads_view(sq, nt), self.stat, HD,
                                   HEAD_LN_EPS, var_ready)

                def layernorm_rest(self):
                    b, nt, link = self.b, self.nt, self.link
                    dve.wait_ge(std_ready, b + 1)
                    layernorm_rest(link, heads_view(fh, nt), heads_view(cen, nt), self.stat, ("ln_g", "ln_b"))\
                        .then_inc(row_ready, 1)
                    dve.wait_ge(row_ready, 4 * b + 1)
                    link(dve.tensor_single_scalar(nz[:, 0:nt, :], fh[:, 0:nt, :], 0.0, ALU.not_equal))
                    assert link.n == LINKS, link.n

            class FeedForward:

                def __init__(self, b, nt):
                    self.b, self.nt, self.groups = b, nt, nt * NH
                    self.link = Links(dve, flinks, b * FLINKS, spare[:])
                    self.stat = (fst[:, 0, 0:self.groups], fst[:, 1, 0:self.groups])
                    self.row_stat = (fst[:, 0, 0:nt], fst[:, 1, 0:nt])
                    self.hv = heads_view(fh, nt)
                    self.g = fgate[:, 0:nt, :]
                    self.xb = xres[:, bass.ds(b * QT, nt), :]

                def relu(self):
                    b, nt = self.b, self.nt
                    dve.wait_ge(fc_ready, 2 * b + 1)
                    dve.scalar_tensor_tensor(relu[:, 0:nt, :], row_view(ps_out, nt), 0.0, nz[:, 0:nt, :], ALU.max, ALU.mult)\
                        .then_inc(row_ready, 1)

                def layernorm_asked(self):
                    b, nt, link = self.b, self.nt, self.link
                    dve.wait_ge(fc_ready, 2 * b + 2)
                    link(dve.tensor_tensor(nz[:, 0:nt, :], row_view(ps_out, nt), nz[:, 0:nt, :], ALU.mult))
                    link(dve.tensor_tensor(fh[:, 0:nt, :], fh[:, 0:nt, :], nz[:, 0:nt, :], ALU.add))
                    layernorm_head(dve, link, self.hv, heads_view(fcen, nt), heads_view(fsq, nt), self.stat, HD,
                                   HEAD_LN_EPS, fvar_ready)

                def layernorm_rest(self):
                    dve.wait_ge(fstd_ready, 2 * self.b + 1)
                    layernorm_rest(self.link, self.hv, heads_view(fcen, self.nt), self.stat, ("fnorm_g", "fnorm_b"))\
                        .then_inc(row_ready, 1)

                def gates(self):
                    dve.wait_ge(fgate_ready, self.b + 1)
                    softmax_top(self.link, self.g, fgtop[:, 0:self.nt], fgsum[:, 0:self.nt], lambda g: dve.tensor_copy(
                        g, ps_out[:, 0:self.groups].rearrange("p (t n) -> p t n", n=NH)), fexp_asked)

                def update(self):
                    b, nt, link = self.b, self.nt, self.link
                    dve.wait_ge(fexp_ready, b + 1)
                    softmax_rest(link, self.g, fgsum[:, 0:nt])
                    fg = self.g.rearrange("p t n -> p (t n)").unsqueeze(2).to_broadcast([P, self.groups, HD])
                    link(dve.tensor_tensor(heads_view(fcen, nt), self.hv, fg, ALU.mult))
                    link(dve.tensor_tensor(self.xb, self.xb, fcen[:, 0:nt, :], ALU.add), apart=True)
                    layernorm_head(dve, link, self.xb, fcen[:, 0:nt, :], fsq[:, 0:nt, :], self.row_stat, D, LN_EPS, fvar_ready)

                def row(self):
                    dve.wait_ge(fstd_ready, 2 * self.b + 2)
                    layernorm_rest(self.link, row[:, 0:self.nt, :], fcen[:, 0:self.nt, :], self.row_stat).then_inc(row_ready, 1)
                    assert self.link.n == FLINKS, self.link.n

            def factors(b, nt):
                dve.wait_ge(node_ready, b + 1)
                dve.tensor_copy(node[:, 0:nt, :], ps_turn[:, 0:nt * NODE_K].rearrange("p (t k) -> p t k", k=NODE_K))\
                    .then_inc(node_copied, 1)

            def step(mix, ffn, zsum, ahead):
                m = Mix(*mix) if mix else None
                f = FeedForward(*ffn) if ffn else None
                if m:
                    m.gates()
                if zsum:
                    factors(*zsum)
                if f:
                    f.relu()
                if m:
                    m.weights()
                if m:
                    m.mix()
                if f:
                    f.layernorm_asked()
                if m:
                    m.layernorm_asked()
                if f:
                    f.layernorm_rest()
                if ahead:
                    Mix(*ahead).mask()
                if f:
                    f.gates()
                    f.update()
                    f.row()
                if m:
                    m.layernorm_rest()

            run(dve, step)

        @block.tensor
        def _(pe):
            pe.wait_ge(pack_landed, 16)

            def turn(b, nt, i, src):
                pe.wait_ge(row_ready, 4 * b + i)
                if i == 1:
                    wait(pe, node_copied, b)
                for j in range(nt):
                    last = pe.matmul(ps_turn[:, j * P:(j + 1) * P], src[:, j, :], w["ident"], start=True, stop=True)
                last.then_inc(turned, 1)

            def z_products(zsum, first, last):
                if not zsum:
                    return
                b, nt = zsum
                for s in range(first, min(last, 4 * nt)):
                    j, q = s // 4, s % 4
                    wait(pe, z_scaled, 16 * b + s - 1)
                    pe.matmul(ps_z[q % 2][:], hT[:, j * P:(j + 1) * P], w["node_w2"][:, q * 512:(q + 1) * 512],
                              start=True, stop=True).then_inc(z_ready, 1)

            def spread_sx(b, nt):
                pe.wait_ge(sx_staged, b + 1)
                wait(pe, mixed, b)
                for n in range(NH):
                    pe.matmul(bank[n][:, 0:nt * P], w["rep"][:, n * P:(n + 1) * P], sxb[:, 0:nt * P],
                              start=True, stop=True).then_inc(sx_spread, 1)

            def gate_products(b, nt):
                pe.wait_ge(masked, NH * (b + 1))
                for j in range(nt):
                    for n in range(NH):
                        at = (j * NH + n) * NE * NE
                        last = pe.matmul(bank[3][:, at:at + NE * NE], onT[:, n, j * P:(j + 1) * P],
                                         w["gate_w"][:, n * NE * NE:(n + 1) * NE * NE], start=True, stop=True)
                last.then_inc(gates_ready, 1)

            def turn_outs(b, nt, tiles):
                for j in tiles:
                    for n in range(NH):
                        last = pe.matmul(bank[j][:, n * P:(n + 1) * P], onT[:, n, j * P:(j + 1) * P], w["ident"],
                                         start=True, stop=True)
                if nt - 1 in tiles:
                    last.then_inc(outs_ready, 1)

            def turn_sx(b, nt):
                pe.wait_ge(out0_mixed, b + 1)
                for j in range(nt):
                    last = pe.matmul(bank[0][:, j * P:(j + 1) * P], sxb[:, j * P:(j + 1) * P], w["ident"],
                                     start=True, stop=True)
                last.then_inc(sx_turned, 1)

            def fc(b, nt, layer):
                pe.wait_ge(turn_copied, 4 * b + layer)
                if layer == 1:
                    wait(pe, nb_copied, b)
                for j in range(nt):
                    cols = slice(j * P, (j + 1) * P)
                    pe.matmul(ps_out[:, cols], turnT[:, cols], w[f"fc{layer}"], start=True, stop=False)
                    last = pe.matmul(ps_out[:, cols], w["ones_row"], w[f"fc{layer}_b"], start=False, stop=True)
                last.then_inc(fc_ready, 1)

            def head_gates(b, nt):
                pe.wait_ge(turn_copied, 4 * b + 3)
                for j in range(nt):
                    last = pe.matmul(ps_out[:, j * NH:(j + 1) * NH], turnT[:, j * P:(j + 1) * P], w["fgateT"],
                                     start=True, stop=True)
                last.then_inc(fgate_ready, 1)

            def graph_inputs(b, nt):
                pe.wait_ge(turn_copied, 4 * b + 4)
                pe.matmul(ps_out[0:NODE_K, 0:nt * P], w["node_w"], hT[:, 0:nt * P], start=True, stop=True)
                for j in range(nt):
                    last = pe.matmul(ps_turn[:, j * NODE_K:(j + 1) * NODE_K], hT[:, j * P:(j + 1) * P], w["node_w"],
                                     start=True, stop=True)
                last.then_inc(node_ready, 1)

            def node_bias(b, nt):
                pe.wait_ge(nodeT_ready, b + 1)
                for j in range(nt):
                    cols = slice(j * P, (j + 1) * P)
                    last = pe.matmul(ps_out[:, cols], nodeT[:, cols], w["node_b"], start=True, stop=True)
                last.then_inc(nb_ready, 1)

            def step(mix, ffn, zsum, ahead):
                if zsum:
                    turn(*zsum, 4, row)
                    graph_inputs(*zsum)
                if ffn:
                    turn(*ffn, 1, fh)
                if zsum:
                    node_bias(*zsum)
                if ffn:
                    fc(*ffn, 1)
                if mix and mix[1] == QT:
                    pe.wait_ge(gates_read, mix[0] + 1)
                    turn_outs(*mix, (3,))
                z_products(zsum, 0, 2)
                if ffn:
                    turn(*ffn, 2, relu)
                    z_products(zsum, 2, 3)
                    fc(*ffn, 2)
                    z_products(zsum, 3, 4)
                if mix:
                    turn_sx(*mix)
                if ffn:
                    z_products(zsum, 4, 6)
                if ahead:
                    spread_sx(*ahead)
                if ffn:
                    z_products(zsum, 6, 9)
                    turn(*ffn, 3, fh)
                    z_products(zsum, 9, 10)
                    head_gates(*ffn)
                    z_products(zsum, 10, 14)
                if ahead:
                    b, nt = ahead
                    gate_products(b, nt)
                    turn_outs(b, nt, range(min(nt, 3)))
                z_products(zsum, 14 if ffn else 2, 16)

            run(pe, step)


def moe_program(nc, adj_main, adj_last, pack_landed, adj_landed, wp, adj, out, xres, z, nb):
    with ExitStack() as ctx:
        sb = lambda name, shape, dt=F32: ctx.enter_context(nc.sbuf_tensor(f"m_{name}", shape, dt))
        ps = lambda name: ctx.enter_context(nc.psum_tensor(f"mp_{name}", [P, 512], F32))
        sem = lambda name: ctx.enter_context(nc.semaphore(f"m_{name}"))
        w = pack_views(wp, PACK_MOE)
        near, hT, ohT = sb("near", [P, BLK]), sb("hT", [P, BLK]), sb("ohT", [ME, BLK])
        ohT16, rep16 = sb("ohT16", [ME, BLK], BF16), sb("rep16", [ME, ME * MH], BF16)
        x3, h, cen, sq, out_tile = (sb(n, [P, QT, D]) for n in ("x3", "h", "cen", "sq", "out"))
        st, spare = sb("st", [P, 2, QT]), sb("spare", [1, 1])
        logits, onehot = sb("logits", [P, QT, ME]), sb("onehot", [P, QT, ME])
        top, where, expert = sb("top", [P, QT, 8]), sb("where", [P, QT, 8], U32), sb("expert", [P, QT])
        hid, hsel = sb("hid", [P, EC, BLK]), sb("hsel", [P, EC, BLK])
        ps_near, ps_turn, ps_logits, ps_out = ps("near"), ps("turn"), ps("logits"), ps("out")
        ps_hid, ps_sel = [ps(f"hid{i}") for i in range(2)], [ps(f"sel{i}") for i in range(2)]
        (adj_used, near_copied, near_turned, links, var_ready, std_ready, h_ready, h_turned, hT_ready,
         logits_ready, logits_read, onehot_ready, onehot_turned, ohT_ready, rep_ready, hid_ready, hid_relu,
         sel_ready, hid_chosen, out_ready, out_added, out_stored) = (sem(n) for n in (
            "adj_used", "near_copied", "near_turned", "links", "var_ready", "std_ready", "h_ready", "h_turned",
            "hT_ready", "logits_ready", "logits_read", "onehot_ready", "onehot_turned", "ohT_ready", "rep_ready",
            "hid_ready", "hid_relu", "sel_ready", "hid_chosen", "out_ready", "out_added", "out_stored"))
        LINKS = 11
        block = ctx.enter_context(nc.Block())

        def run(eng, step):
            step((0, QT), None, None)
            step((1, QT), (0, QT), None)
            step((2, QT), (1, QT), (0, QT))
            with eng.Fori(3, NB) as b:
                step((b, QT), (b - 1, QT), (b - 2, QT))
            step((NB, LT), (NB - 1, QT), (NB - 2, QT))
            step(None, (NB, LT), (NB - 1, QT))
            step(None, None, (NB, LT))

        @block.sync
        def _(sp):
            def step(products, choice, final):
                if products and not (isinstance(products[0], int) and products[0] == 0):
                    b, nt = products
                    src = adj_last if isinstance(b, int) and b == NB else (
                        adj_main[bass.ds(b, 1)].rearrange("o p k m -> (o p) k m"))
                    for i, (k0, k1) in enumerate(PIECES):
                        wait(sp, adj_used, len(PIECES) * (b - 1) + i + 1)
                        sp.dma_start(adj[:, k0:k1, 0:nt * P], src[:, k0:k1, :]).then_inc(adj_landed[i], 16)
                if final:
                    b, nt = final
                    sp.wait_ge(out_added, b + 1)
                    sp.dma_start(out.rearrange("(t p) d -> p t d", p=P)[:, bass.ds(b * QT, nt), :],
                                 out_tile[:, 0:nt, :]).then_inc(out_stored, 16)

            run(sp, step)
            sp.wait_ge(out_stored, 16 * (NB + 1))

        @block.vector
        def _(dve):
            dve.wait_ge(pack_landed, 16)
            dve.tensor_copy(rep16[:], w["rep"]).then_inc(rep_ready, 1)

            def choose(b, nt):
                link = Links(dve, links, b * LINKS, spare[:])
                tiles = slice(0, nt)
                rows = bass.ds(b * QT, nt)
                stat = (st[:, 0, tiles], st[:, 1, tiles])
                shape = [P, nt, D]
                dve.wait_ge(near_turned, b + 1)
                link(dve.tensor_tensor(x3[:, tiles, :], ps_turn[:, 0:nt * D].rearrange("p (t d) -> p t d", d=D),
                                       nb[:, rows, :], ALU.add))
                link(dve.scalar_tensor_tensor(x3[:, tiles, :], x3[:, tiles, :], 0.0, xres[:, rows, :],
                                              ALU.max, ALU.add))
                layernorm_head(dve, link, x3[:, tiles, :], cen[:, tiles, :], sq[:, tiles, :], stat, D, LN_EPS, var_ready)
                dve.wait_ge(std_ready, b + 1)
                rstd = layernorm_tail(dve, link, cen, stat, shape)
                dve.tensor_tensor(h[:, tiles, :], cen[:, tiles, :], rstd, ALU.mult).then_inc(h_ready, 1)
                dve.wait_ge(logits_ready, b + 1)
                dve.tensor_copy(logits[:, tiles, :], ps_logits[:, 0:nt * ME].rearrange("p (t e) -> p t e", e=ME))\
                    .then_inc(logits_read, 1)
                dve.wait_ge(logits_read, b + 1)
                link.apart()
                for j in range(nt):
                    last = dve.max(top[:, j, :], logits[:, j, :])
                link(last, apart=True)
                for j in range(nt):
                    last = dve.max_index(where[:, j, :], top[:, j, :], logits[:, j, :])
                link(last)
                link(dve.tensor_copy(expert[:, tiles], where[:, tiles, 0]))
                for j in range(nt):
                    ins = dve.tensor_scalar(onehot[:, j, :], w["iota"], expert[:, j:j + 1], None, ALU.is_equal)
                link(ins)
                dve.nop().then_inc(onehot_ready, 1)
                for c in range(EC):
                    dve.wait_ge(hid_relu, b * EC + c + 1)
                    dve.wait_ge(sel_ready, b * EC + c + 1)
                    dve.tensor_tensor(hsel[:, c, 0:nt * P], ps_sel[c % 2][:, 0:nt * P], hid[:, c, 0:nt * P],
                                      ALU.mult).then_inc(hid_chosen, 1)
                assert link.n == LINKS, link.n

            def finish(b, nt):
                dve.wait_ge(out_ready, b + 1)
                wait(dve, out_stored, 16 * b)
                dve.scalar_tensor_tensor(out_tile[:, 0:nt, :], ps_out[:, 0:nt * D].rearrange("p (t d) -> p t d", d=D),
                                         0.0, x3[:, 0:nt, :], ALU.max, ALU.add).then_inc(out_added, 1)
                dve.wait_ge(out_added, b + 1)

            def step(products, choice, final):
                if final:
                    finish(*final)
                if choice:
                    choose(*choice)

            run(dve, step)

        @block.scalar
        def _(act):
            def step(products, choice, final):
                if choice:
                    b, nt = choice
                    width = nt * P
                    act.wait_ge(var_ready, b + 1)
                    act.activation(st[:, 0, 0:nt], st[:, 1, 0:nt], ACT.Sqrt).then_inc(std_ready, 1)
                    act.wait_ge(h_turned, b + 1)
                    act.copy(hT[:, 0:width], ps_turn[:, 0:width]).then_inc(hT_ready, 1)
                    for c in range(EC):
                        act.wait_ge(hid_ready, b * EC + c + 1)
                        act.activation(hid[:, c, 0:width], ps_hid[c % 2][:, 0:width], ACT.Relu,
                                       bias=w["b1"][:, c:c + 1]).then_inc(hid_relu, 1)
                    act.wait_ge(onehot_turned, b + 1)
                    act.copy(ohT16[:, 0:width], ps_turn[0:ME, 0:width]).then_inc(ohT_ready, 1)
                    act.copy(ohT[:, 0:width], ps_turn[0:ME, 0:width]).then_inc(ohT_ready, 1)
                if products:
                    b, nt = products
                    act.wait_ge(adj_used, len(PIECES) * (b + 1))
                    act.copy(near[:, 0:nt * P], ps_near[:, 0:nt * P]).then_inc(near_copied, 1)

            act.wait_ge(pack_landed, 16)
            run(act, step)

        @block.tensor
        def _(pe):
            pe.wait_ge(pack_landed, 16)
            pe.wait_ge(rep_ready, 1)

            def columns(nt):
                return [slice(j * P, (j + 1) * P) for j in range(nt)]

            def near_rows(b, nt):
                pe.wait_ge(near_copied, b + 1)
                wait(pe, ohT_ready, 2 * b)
                for cols in columns(nt):
                    last = pe.matmul(ps_turn[:, cols], near[:, cols], w["ident"], start=True, stop=True)
                last.then_inc(near_turned, 1)

            def turn_h(b, nt):
                pe.wait_ge(h_ready, b + 1)
                for j, cols in enumerate(columns(nt)):
                    last = pe.matmul(ps_turn[:, cols], h[:, j, :], w["ident"], start=True, stop=True)
                last.then_inc(h_turned, 1)

            def route(b, nt):
                pe.wait_ge(hT_ready, b + 1)
                for j, cols in enumerate(columns(nt)):
                    to = ps_logits[:, j * ME:(j + 1) * ME]
                    pe.matmul(to, hT[:, cols], w["routerT"], start=True, stop=False)
                    last = pe.matmul(to, w["ones_row"], w["router_b"], start=False, stop=True)
                last.then_inc(logits_ready, 1)

            def hidden(b, nt, c):
                wait(pe, hid_relu, b * EC + c - 1)
                pe.matmul(ps_hid[c % 2][:, 0:nt * P], w["w1"][:, c * P:(c + 1) * P], hT[:, 0:nt * P],
                          start=True, stop=True).then_inc(hid_ready, 1)

            def turn_choice(b, nt):
                pe.wait_ge(onehot_ready, b + 1)
                for j, cols in enumerate(columns(nt)):
                    last = pe.matmul(ps_turn[0:ME, cols], onehot[:, j, :], w["ident"], start=True, stop=True)
                last.then_inc(onehot_turned, 1)

            def select(b, nt, c):
                if c == 0:
                    pe.wait_ge(ohT_ready, 2 * b + 1)
                wait(pe, hid_chosen, b * EC + c - 1)
                pe.matmul(ps_sel[c % 2][:, 0:nt * P], rep16[:, c * P:(c + 1) * P], ohT16[:, 0:nt * P],
                          start=True, stop=True).then_inc(sel_ready, 1)

            def expert_out(b, nt):
                pe.wait_ge(hid_chosen, (b + 1) * EC)
                pe.wait_ge(ohT_ready, 2 * b + 2)
                wait(pe, out_added, b)
                for cols in columns(nt):
                    for c in range(EC):
                        pe.matmul(ps_out[:, cols], hsel[:, c, cols], w["w2"][:, c * D:(c + 1) * D], start=(c == 0), stop=False)
                    last = pe.matmul(ps_out[:, cols], ohT[:, cols], w["b2"], start=False, stop=True)
                last.then_inc(out_ready, 1)

            def adj_products(products, first, last):
                if not products:
                    return
                b, nt = products
                for i, (k0, k1) in enumerate(PIECES):
                    for k in range(max(k0, first), min(k1, last)):
                        if k == k0:
                            pe.wait_ge(adj_landed[i], 16 * (b + 1))
                        if k == 0:
                            wait(pe, near_copied, b)
                        ins = pe.matmul(ps_near[:, 0:nt * P], z[:, k, :], adj[:, k, 0:nt * P],
                                        start=(k == 0), stop=(k == NT - 1))
                        if k == k1 - 1:
                            ins.then_inc(adj_used, 1)

            def step(products, choice, final):
                if final:
                    expert_out(*final)
                if not choice:
                    adj_products(products, 0, NT)
                    return
                near_rows(*choice)
                adj_products(products, 0, 8)
                turn_h(*choice)
                adj_products(products, 8, 10)
                route(*choice)
                for c in range(EC):
                    hidden(*choice, c)
                    if c > 0:
                        adj_products(products, 9 + c, 10 + c)
                turn_choice(*choice)
                adj_products(products, 17, 19)
                for c in range(EC):
                    select(*choice, c)
                    if c > 0:
                        adj_products(products, 17 + c + 1, 17 + c + 2)
                adj_products(products, 26, NT)

            run(pe, step)


def model_program(nc, x_in, adj_main, adj_last, pack_gnn0, pack_att, pack_post, pack_moe, o_scratch, out):
    with ExitStack() as ctx:
        rows = lambda ctx, name, width=D: ctx.enter_context(nc.sbuf_tensor(name, [P, NT, width], F32))
        pack = lambda ctx, name, columns: ctx.enter_context(nc.sbuf_tensor(name, [P, pack_width(columns)], F32))
        sem = lambda name: ctx.enter_context(nc.semaphore(name))
        post_landed, moe_landed = sem("pack_post_landed"), sem("pack_moe_landed")
        adj_landed = [sem(f"moe_adj_landed{i}") for i in range(len(PIECES))]
        xres = rows(ctx, "xres")
        z = rows(ctx, "z")
        nb = rows(ctx, "nb")
        sxT = ctx.enter_context(nc.sbuf_tensor("sxT", [P, NP], F32))
        rsum = rows(ctx, "rsum", NH * NE)
        wp_post = pack(ctx, "wp_post", PACK_POST)
        with ExitStack() as inner:
            kst = inner.enter_context(nc.sbuf_tensor("kst", [P, NH, NP], F32R))
            gnn0_program(nc, x_in, adj_main, adj_last, pack_gnn0, xres, z, sxT, kst, nb)
            attention_program(nc, pack_att, sxT, kst, nb, rsum, o_scratch,
                              lambda eng: eng.dma_start(wp_post[:], pack_post).then_inc(post_landed, 16))
        wp_moe = pack(ctx, "wp_moe", PACK_MOE)
        adj = ctx.enter_context(nc.sbuf_tensor("moe_adj", [P, NT, BLK], F32))

        def load_first(eng):
            eng.dma_start(wp_moe[:], pack_moe).then_inc(moe_landed, 16)
            for (k0, k1), landed in zip(PIECES, adj_landed):
                eng.dma_start(adj[:, k0:k1, :], adj_main[0][:, k0:k1, :]).then_inc(landed, 16)

        post_program(nc, post_landed, wp_post, o_scratch, xres, sxT, rsum, z, nb, load_first)
        moe_program(nc, adj_main, adj_last, moe_landed, adj_landed, wp_moe, adj, out, xres, z, nb)


def pack_weights(np, pack, arrays):
    packed, at = np.zeros((P, pack_width(pack)), np.float32), 0
    for name, rows, cols in pack:
        packed[0:rows, at:at + cols] = arrays[name]
        at += cols
    return packed


def kernel(**inputs):
    import numpy as np
    import concourse.bacc as bacc
    from concourse.bass_utils import run_bass_kernel_spmd

    a = {name: np.asarray(value) for name, value in inputs.items()}
    f = lambda name: a["L0_ffn_" + name]

    x = np.zeros((NP, D), np.float32)
    x[:N] = a["x"]
    adjT = np.zeros((NP, NP), np.float32)
    adjT[:N, :N] = a["adj"].T
    adjT = adjT.reshape(NT, P, NP).transpose(1, 0, 2)
    adj_main = np.ascontiguousarray(
        adjT[:, :, :NB * BLK].reshape(P, NT, NB, BLK).transpose(2, 0, 1, 3))
    adj_last = np.ascontiguousarray(adjT[:, :, NB * BLK:])

    wk = np.zeros((P, NH * HD), np.float32)
    wq = np.zeros((P, NH, NE, HD), np.float32)
    wv = np.zeros((P, NH * HD), np.float32)
    rep = np.zeros((P, NH, NE, HD), np.float32)
    gate_w = np.zeros((P, NH, NE, NE), np.float32)
    fc1, fc2 = np.zeros((P, D), np.float32), np.zeros((P, D), np.float32)
    for n in range(NH):
        rows = slice(n * HD, (n + 1) * HD)
        wk[rows, rows] = f("wk")[n].T
        wv[rows, rows] = f("wv")[n].T
        fc1[rows, rows] = f("fc1_w").T
        fc2[rows, rows] = f("fc2_w").T
        for e in range(NE):
            wq[rows, n, e] = f("wq")[n, e].T
            gate_w[e * HD:(e + 1) * HD, n, :, e] = f("gate_w")[n][:, e * HD:(e + 1) * HD].T
            rep[rows, n, e, :] = np.eye(HD, dtype=np.float32)
    ident = np.eye(P, dtype=np.float32)
    after = np.triu(np.ones((P, P), np.float32), 1) * np.float32(MASKED)
    sel = np.zeros((P, 16), np.float32)
    sel[96:] = np.repeat(np.eye(16, dtype=np.float32), 2, axis=0)
    ones_row = np.ones((1, P), np.float32)
    first_row = np.zeros((P, 1), np.float32)
    first_row[::HD] = 1.0
    spread = lambda v: np.broadcast_to(v.reshape(1, -1), (P, v.size))
    weight = a["L0_gnn_weight"]
    pack_gnn0 = pack_weights(np, PACK_GNN0, dict(
        ident=ident, w_self=weight[:D], w_near=weight[D:], bias=a["L0_gnn_bias"].reshape(1, D), ones_row=ones_row,
        hl_wT=f("hl_w").reshape(NH * HD, D).T, hl_b=f("hl_b").reshape(P, 1),
        wk=wk, wv=wv))
    pack_att = pack_weights(np, PACK_ATT, dict(
        ident=ident, mask_rows=after, mask_cols=after.T, sel=sel, ones32=np.ones((P, 32), np.float32),
        wq=wq.reshape(P, -1), first_rows=np.repeat(np.eye(NE, dtype=np.float32), HD, axis=0) * first_row))
    pack_post = pack_weights(np, PACK_POST, dict(
        ident=ident, ones_row=ones_row, rep=rep.reshape(P, -1), gate_w=gate_w.reshape(P, -1), gate_b=spread(f("gate_b")),
        ln_g=spread(f("ln_g")), ln_b=spread(f("ln_b")), fnorm_g=spread(f("fnorm_g")), fnorm_b=spread(f("fnorm_b")),
        fc1=fc1, fc2=fc2, fc1_b=np.tile(f("fc1_b"), NH).reshape(1, D), fc2_b=np.tile(f("fc2_b"), NH).reshape(1, D),
        fgateT=f("fgate_w").T, node_w=a["L1_gnn_W1"], node_b=a["L1_gnn_b"],
        node_w2=a["L1_gnn_W2"].transpose(1, 0, 2).reshape(P, -1)))
    pack_moe = pack_weights(np, PACK_MOE, dict(
        ident=ident, ones_row=ones_row, routerT=a["L1_ffn_router_w"].T, router_b=a["L1_ffn_router_b"].reshape(1, ME),
        iota=spread(np.arange(ME, dtype=np.float32)), w1=a["L1_ffn_W1"].transpose(1, 0, 2).reshape(P, -1),
        b1=a["L1_ffn_b1"].reshape(EC, P).T, w2=a["L1_ffn_W2"].reshape(EC, P, D).transpose(1, 0, 2).reshape(P, -1),
        b2=a["L1_ffn_b2"], rep=np.repeat(np.eye(ME, dtype=np.float32), MH, axis=1)))

    arrays = dict(x_in=x, adj_main=adj_main, adj_last=adj_last, pack_gnn0=pack_gnn0, pack_att=pack_att,
                  pack_post=pack_post, pack_moe=pack_moe)
    nc = bacc.Bacc("TRN2", target_bir_lowering=False, num_devices=1)
    args = {name: nc.dram_tensor(name, v.shape, F32, kind="ExternalInput").ap() for name, v in arrays.items()}
    args["out"] = nc.dram_tensor("out", (NP, D), F32, kind="ExternalOutput").ap()
    o_scratch = nc.dram_tensor("o_scratch", (NB + 1, P, NH, BLK), F32, kind="Internal").ap()
    model_program(nc, o_scratch=o_scratch, **args)
    result = run_bass_kernel_spmd(nc, [arrays], core_ids=[0]).results[0]["out"]
    return result[:N]
```
